# Optimizing a Trainium2 kernel written in Bass

```python
import numpy as np
import jax
import jax.numpy as jnp

def _softmax(x, axis=-1):
    return jax.nn.softmax(x, axis=axis)

def _gelu(x):
    return jax.nn.gelu(x, approximate=True)

def _silu(x):
    return jax.nn.silu(x)

def _sigmoid(x):
    return jax.nn.sigmoid(x)

def _layernorm(x, axis=-1, eps=1e-05):
    m = jnp.mean(x, axis=axis, keepdims=True)
    v = jnp.var(x, axis=axis, keepdims=True)
    return (x - m) / jnp.sqrt(v + eps)

def _scatter_add(tgt, idx, src, axis=0):
    return tgt.at[idx].add(src)

def _segment_sum(src, seg, n):
    return jax.ops.segment_sum(src, seg, n)
kernel_name = 'mk_xattn_ffn_d4_seqx_r4_7d67ff'

def setup_inputs(seed: int=0):
    np.random.seed(seed)
    _w = jnp.asarray

    def _rec_inputs():
        import jax
        import jax.numpy as jnp
        _rk = jax.random.key(seed)
        x = -0.0002928 + 1 * jax.random.normal(jax.random.fold_in(_rk, 1), (8, 256, 256), jnp.float32)
        _lenS = 256 - jax.random.randint(jax.random.fold_in(_rk, 7), (8,), 0, max(1, 256 // 4) + 1, jnp.int32)
        _lenS2 = 256 - jax.random.randint(jax.random.fold_in(_rk, 8), (8,), 0, max(1, 256 // 4) + 1, jnp.int32)
        _ctx_1024P = jax.random.normal(jax.random.fold_in(_rk, 11), (8, 16, 256), jnp.float32)
        _ctx_1024c = jax.random.dirichlet(jax.random.fold_in(_rk, 511), 0.3 * jnp.ones((16,), jnp.float32), (8, 256))
        _ctx_1024t = jnp.einsum('bsk,bkd->bsd', _ctx_1024c, _ctx_1024P)
        _ctx_1024t = _ctx_1024t * jax.lax.rsqrt(jnp.mean(jnp.square(_ctx_1024t)) + 1e-12) * 0.953939
        ctx_1024 = 2.81802e-05 + 1.00001 * (_ctx_1024t + 0.3 * jax.random.normal(jax.random.fold_in(_rk, 611), (8, 256, 256), jnp.float32))
        _validS = jnp.arange(256)[None, :] < _lenS[:, None]
        _validS2 = jnp.arange(256)[None, :] < _lenS2[:, None]
        _causal = jnp.tril(jnp.ones((256, 256), dtype=bool))
        mask_BxS2_bk0 = jnp.logical_not(jnp.broadcast_to(_validS2[:, :], (8, 256)))
        return (x, ctx_1024, mask_BxS2_bk0)
    x, ctx_1024, mask_BxS2_bk0 = _rec_inputs()

    def _L0_xattn_setup():
        import jax, jax.numpy as jnp
        import numpy as np
        NUM_HEADS, NUM_KV, HEAD_DIM, WIDTH = (4, 1, 64, 256)
        MASK_FILL = -2.3819763e+38

        def _apply_rope(x, positions, max_wavelength=10000.0):
            d = x.shape[-1]
            freq_exp = 2.0 / d * jnp.arange(d // 2, dtype=jnp.float32)
            timescale = max_wavelength ** freq_exp
            radians = positions[..., None].astype(jnp.float32) / timescale
            radians = radians[..., None, :]
            sin, cos = (jnp.sin(radians), jnp.cos(radians))
            x1, x2 = jnp.split(x, 2, axis=-1)
            out = jnp.concatenate([x1 * cos - x2 * sin, x2 * cos + x1 * sin], axis=-1)
            return out.astype(x.dtype)

        def _rmsnorm(x, scale):
            var = jnp.mean(jnp.square(x.astype(jnp.float32)), axis=-1, keepdims=True)
            normed = x * jax.lax.rsqrt(var + 1e-06)
            return (normed * (1 + scale)).astype(x.dtype)
        key = jax.random.key(seed)
        ks = jax.random.split(key, 7)
        B, T, S = (8, 128, 512)
        return {'x': jax.random.normal(ks[0], (B, T, WIDTH), jnp.float32), 'mem_seq': jax.random.normal(ks[1], (B, S, WIDTH), jnp.float32), 'mem_mask': jax.random.randint(ks[2], (B, S), 0, 2).astype(bool), 'rms_scale': jax.random.normal(ks[3], (WIDTH,), jnp.float32) * 0.02, 'q_w': jax.random.normal(ks[4], (NUM_HEADS, WIDTH, HEAD_DIM), jnp.float32) / np.sqrt(WIDTH), 'kv_w': jax.random.normal(ks[5], (2, NUM_KV, WIDTH, HEAD_DIM), jnp.float32) / np.sqrt(WIDTH), 'out_w': jax.random.normal(ks[6], (NUM_HEADS, HEAD_DIM, WIDTH), jnp.float32) / np.sqrt(NUM_HEADS * HEAD_DIM)}
    _L0_xattn_all = _L0_xattn_setup()
    _L0_xattn_in = {k: v for k, v in _L0_xattn_all.items() if k in ('rms_scale', 'q_w', 'kv_w', 'out_w')}
    del _L0_xattn_all

    def _L0_ffn_setup():
        import jax, jax.numpy as jnp
        import numpy as np
        NUM_EXPERTS = 8
        TOP_K = 2
        key = jax.random.key(seed)
        ks = jax.random.split(key, 6)
        B, S, D, H, E = (4, 256, 256, 512, NUM_EXPERTS)
        x = jax.random.normal(ks[0], (B, S, D), dtype=jnp.float32)
        Wg = jax.random.normal(ks[1], (D, E), dtype=jnp.float32) * 0.02
        W1 = jax.random.normal(ks[2], (E, D, H), dtype=jnp.float32) * 0.02
        b1 = jax.random.normal(ks[3], (E, H), dtype=jnp.float32) * 0.02
        W2 = jax.random.normal(ks[4], (E, H, D), dtype=jnp.float32) * 0.02
        b2 = jax.random.normal(ks[5], (E, D), dtype=jnp.float32) * 0.02
        return {'x': x, 'Wg': Wg, 'W1': W1, 'b1': b1, 'W2': W2, 'b2': b2}
    _L0_ffn_all = _L0_ffn_setup()
    _L0_ffn_in = {k: v for k, v in _L0_ffn_all.items() if k in ('Wg', 'W1', 'b1', 'W2', 'b2')}
    del _L0_ffn_all

    def _L1_xattn_setup():
        import jax, jax.numpy as jnp
        import numpy as np
        B, L, D, H = (4, 512, 256, 16)
        DH = D // H
        SCALE = 1.0 / float(np.sqrt(DH))

        def _split_heads(x):
            b, l, _ = x.shape
            return x.reshape(b, l, H, DH).transpose(0, 2, 1, 3)
        key = jax.random.key(seed)
        ks = jax.random.split(key, 11)
        s = 0.02
        return {'q': jax.random.normal(ks[0], (B, L, D), jnp.float32), 'k': jax.random.normal(ks[1], (B, L, D), jnp.float32), 'v': jax.random.normal(ks[2], (B, L, D), jnp.float32), 'Wq': jax.random.normal(ks[3], (D, D), jnp.float32) * s, 'bq': jnp.zeros((D,), jnp.float32), 'Wk': jax.random.normal(ks[4], (D, D), jnp.float32) * s, 'bk': jnp.zeros((D,), jnp.float32), 'Wv': jax.random.normal(ks[5], (D, D), jnp.float32) * s, 'bv': jnp.zeros((D,), jnp.float32), 'Wo': jax.random.normal(ks[6], (D, D), jnp.float32) * s, 'bo': jnp.zeros((D,), jnp.float32)}
    _L1_xattn_all = _L1_xattn_setup()
    _L1_xattn_in = {k: v for k, v in _L1_xattn_all.items() if k in ('Wq', 'bq', 'Wk', 'bk', 'Wv', 'bv', 'Wo', 'bo')}
    del _L1_xattn_all

    def _L1_ffn_setup():
        import jax, jax.numpy as jnp
        import numpy as np
        D = 256
        E = 8
        H = 512
        TOP_K = 2
        ALPHA = 0.5
        LN_EPS = 1e-05

        def _experts_all(x, W1, b1, W2, b2):
            h = jax.nn.relu(jnp.einsum('bld,edh->eblh', x, W1) + b1[:, None, None, :])
            return jnp.einsum('eblh,ehd->ebld', h, W2) + b2[:, None, None, :]

        def _selected_expert(x, expert_idx, W1, b1, W2, b2):
            oh = jax.nn.one_hot(expert_idx, E, dtype=x.dtype)
            return jnp.einsum('ebld,ble->bld', _experts_all(x, W1, b1, W2, b2), oh)

        def _layer_norm(x, gamma, beta):
            mu = jnp.mean(x, axis=-1, keepdims=True)
            var = jnp.mean(jnp.square(x - mu), axis=-1, keepdims=True)
            return (x - mu) * jax.lax.rsqrt(var + LN_EPS) * gamma + beta
        key = jax.random.key(seed)
        ks = jax.random.split(key, 8)
        x = jax.random.normal(ks[0], (2, 512, D), dtype=jnp.float32)
        gate_W = jax.random.normal(ks[1], (D, E), dtype=jnp.float32) * 0.02
        gate_b = jnp.zeros((E,), dtype=jnp.float32)
        W1 = jax.random.normal(ks[2], (E, D, H), dtype=jnp.float32) * 0.02
        b1 = jnp.zeros((E, H), dtype=jnp.float32)
        W2 = jax.random.normal(ks[3], (E, H, D), dtype=jnp.float32) * 0.02
        b2 = jnp.zeros((E, D), dtype=jnp.float32)
        ln_gamma = jnp.ones((D,), dtype=jnp.float32)
        ln_beta = jnp.zeros((D,), dtype=jnp.float32)
        return {'x': x, 'gate_W': gate_W, 'gate_b': gate_b, 'W1': W1, 'b1': b1, 'W2': W2, 'b2': b2, 'ln_gamma': ln_gamma, 'ln_beta': ln_beta}
    _L1_ffn_all = _L1_ffn_setup()
    _L1_ffn_in = {k: v for k, v in _L1_ffn_all.items() if k in ('gate_W', 'gate_b', 'W1', 'b1', 'W2', 'b2', 'ln_gamma', 'ln_beta')}
    del _L1_ffn_all

    def _L2_xattn_setup():
        import jax, jax.numpy as jnp
        import numpy as np
        EPS_BACKEND = 1e-06
        NORM_EPS = 1e-06
        NUM_HEADS = 4

        def _mlstm_forward(q, k, v, ig_kernel, ig_bias, fg_kernel, fg_bias, outnorm_weight):
            B, S, E = q.shape
            NH = ig_bias.shape[0]
            DH = E // NH
            gate_input = jnp.concatenate([q, k, v], axis=-1)
            igate = gate_input @ ig_kernel + ig_bias
            fgate = gate_input @ fg_kernel + fg_bias
            qh = q.reshape(B, S, NH, DH).transpose(0, 2, 1, 3)
            kh = k.reshape(B, S, NH, DH).transpose(0, 2, 1, 3)
            vh = v.reshape(B, S, NH, DH).transpose(0, 2, 1, 3)
            ig = igate.transpose(0, 2, 1)
            fg = fgate.transpose(0, 2, 1)
            log_fg = jax.nn.log_sigmoid(fg)
            cums = jnp.concatenate([jnp.zeros((B, NH, 1), log_fg.dtype), jnp.cumsum(log_fg, axis=-1)], axis=-1)
            fg_mat = cums[..., :, None] - cums[..., None, :]
            mask = jnp.tril(jnp.ones((S + 1, S + 1), bool))
            fg_mat = jnp.where(mask, fg_mat, -jnp.inf)[..., 1:, 1:]
            log_D = fg_mat + ig[..., None, :]
            max_log_D = jnp.max(log_D, axis=-1, keepdims=True)
            D = jnp.exp(log_D - max_log_D)
            qk = jnp.einsum('bnsd,bntd->bnst', qh, kh) / jnp.sqrt(jnp.float32(DH))
            C = qk * D
            normalizer = jnp.maximum(jnp.abs(C.sum(-1, keepdims=True)), jnp.exp(-max_log_D))
            h = jnp.einsum('bnst,bntd->bnsd', C / (normalizer + EPS_BACKEND), vh)
            h = h.transpose(0, 2, 1, 3)
            mean = h.mean(-1, keepdims=True)
            var = h.var(-1, keepdims=True)
            hn = (h - mean) * jax.lax.rsqrt(var + NORM_EPS) * outnorm_weight
            return hn.reshape(B, S, E)
        key = jax.random.key(seed)
        ks = jax.random.split(key, 8)
        B, S, E, NH = (2, 512, 256, NUM_HEADS)
        DH = E // NH
        q = jax.random.normal(ks[0], (B, S, E), jnp.float32)
        k = jax.random.normal(ks[1], (B, S, E), jnp.float32)
        v = jax.random.normal(ks[2], (B, S, E), jnp.float32)
        ig_kernel = jax.random.normal(ks[3], (3 * E, NH), jnp.float32) * 0.02
        fg_kernel = jax.random.normal(ks[4], (3 * E, NH), jnp.float32) * 0.02
        ig_bias = jax.random.normal(ks[5], (NH,), jnp.float32) * 0.1
        fg_bias = jnp.linspace(3.0, 6.0, NH, dtype=jnp.float32)
        outnorm_weight = jnp.ones((NH, DH), jnp.float32)
        return {'q': q, 'k': k, 'v': v, 'ig_kernel': ig_kernel, 'ig_bias': ig_bias, 'fg_kernel': fg_kernel, 'fg_bias': fg_bias, 'outnorm_weight': outnorm_weight}
    _L2_xattn_all = _L2_xattn_setup()
    _L2_xattn_in = {k: v for k, v in _L2_xattn_all.items() if k in ('ig_kernel', 'ig_bias', 'fg_kernel', 'fg_bias', 'outnorm_weight')}
    del _L2_xattn_all

    def _L2_ffn_setup():
        import jax, jax.numpy as jnp
        import numpy as np
        DIM = 256

        def _reference_tuple_inner(x, W_r, W_k, W_v, mu_r, mu_k):
            B, T, C = x.shape
            x_prev = jnp.concatenate([jnp.zeros((B, 1, C), x.dtype), x[:, :-1, :]], axis=1)
            xr = mu_r * x + (1.0 - mu_r) * x_prev
            xk = mu_k * x + (1.0 - mu_k) * x_prev
            r = jax.nn.sigmoid(jnp.einsum('btc,dc->btd', xr, W_r))
            k = jnp.einsum('btc,dc->btd', xk, W_k)
            k_act = jnp.square(jax.nn.relu(k))
            out = r * jnp.einsum('btc,dc->btd', k_act, W_v)
            new_state = x[:, -1, :]
            return (out, new_state)
        key = jax.random.key(seed)
        ks = jax.random.split(key, 6)
        B, T, C = (8, 512, DIM)
        x = jax.random.normal(ks[0], (B, T, C), dtype=jnp.float32)
        s = 1.0 / np.sqrt(C)
        W_r = jax.random.uniform(ks[1], (C, C), jnp.float32, -s, s)
        W_k = jax.random.uniform(ks[2], (C, C), jnp.float32, -s, s)
        W_v = jax.random.uniform(ks[3], (C, C), jnp.float32, -s, s)
        mu_r = jax.random.uniform(ks[4], (C,), jnp.float32)
        mu_k = jax.random.uniform(ks[5], (C,), jnp.float32)
        return {'x': x, 'W_r': W_r, 'W_k': W_k, 'W_v': W_v, 'mu_r': mu_r, 'mu_k': mu_k}
    _L2_ffn_all = _L2_ffn_setup()
    _L2_ffn_in = {k: v for k, v in _L2_ffn_all.items() if k in ('W_r', 'W_k', 'W_v', 'mu_r', 'mu_k')}
    del _L2_ffn_all

    def _L3_xattn_setup():
        import jax, jax.numpy as jnp
        import numpy as np
        D_MODEL = 256
        HEADS = 16
        D_K = D_MODEL // HEADS
        key = jax.random.key(seed)
        ks = jax.random.split(key, 11)
        B, S = (4, 512)
        s = 1.0 / np.sqrt(D_MODEL)
        return {'q': jax.random.normal(ks[0], (B, S, D_MODEL), dtype=jnp.float32), 'k': jax.random.normal(ks[1], (B, S, D_MODEL), dtype=jnp.float32), 'v': jax.random.normal(ks[2], (B, S, D_MODEL), dtype=jnp.float32), 'Wq': jax.random.normal(ks[3], (D_MODEL, D_MODEL), dtype=jnp.float32) * s, 'bq': jnp.zeros((D_MODEL,), dtype=jnp.float32), 'Wk': jax.random.normal(ks[4], (D_MODEL, D_MODEL), dtype=jnp.float32) * s, 'bk': jnp.zeros((D_MODEL,), dtype=jnp.float32), 'Wv': jax.random.normal(ks[5], (D_MODEL, D_MODEL), dtype=jnp.float32) * s, 'bv': jnp.zeros((D_MODEL,), dtype=jnp.float32), 'Wo': jax.random.normal(ks[6], (D_MODEL, D_MODEL), dtype=jnp.float32) * s, 'bo': jnp.zeros((D_MODEL,), dtype=jnp.float32)}
    _L3_xattn_all = _L3_xattn_setup()
    _L3_xattn_in = {k: v for k, v in _L3_xattn_all.items() if k in ('Wq', 'bq', 'Wk', 'bk', 'Wv', 'bv', 'Wo', 'bo')}
    del _L3_xattn_all

    def _L3_ffn_setup():
        import jax, jax.numpy as jnp
        import numpy as np
        B, T = (2, 512)
        D_MODEL, D_HIDDEN = (256, 512)
        N_EXPERTS, TOP_K = (8, 2)
        N_TOKENS = B * T
        CAPACITY = 2 * N_TOKENS * TOP_K // N_EXPERTS
        key = jax.random.key(seed)
        k_x, k_rw, k_w, k_v, k_o = jax.random.split(key, 5)
        x = jax.random.normal(k_x, (B, T, D_MODEL), jnp.float32)
        router_w = jax.random.normal(k_rw, (N_EXPERTS, D_MODEL), jnp.float32) * D_MODEL ** (-0.5)
        router_b = jnp.zeros((N_EXPERTS,), jnp.float32)
        W = jax.random.normal(k_w, (N_EXPERTS, D_MODEL, D_HIDDEN), jnp.float32) * D_MODEL ** (-0.5)
        V = jax.random.normal(k_v, (N_EXPERTS, D_MODEL, D_HIDDEN), jnp.float32) * D_MODEL ** (-0.5)
        W_out = jax.random.normal(k_o, (N_EXPERTS, D_HIDDEN, D_MODEL), jnp.float32) * D_HIDDEN ** (-0.5)
        return {'x': x, 'router_w': router_w, 'router_b': router_b, 'W': W, 'V': V, 'W_out': W_out}
    _L3_ffn_all = _L3_ffn_setup()
    _L3_ffn_in = {k: v for k, v in _L3_ffn_all.items() if k in ('router_w', 'router_b', 'W', 'V', 'W_out')}
    del _L3_ffn_all
    return {'x': x, 'ctx_1024': ctx_1024, 'mask_BxS2_bk0': mask_BxS2_bk0, 'L0_xattn_rms_scale': _L0_xattn_in['rms_scale'], 'L0_xattn_q_w': _L0_xattn_in['q_w'], 'L0_xattn_kv_w': _L0_xattn_in['kv_w'], 'L0_xattn_out_w': _L0_xattn_in['out_w'], 'L0_ffn_Wg': _L0_ffn_in['Wg'], 'L0_ffn_W1': _L0_ffn_in['W1'], 'L0_ffn_b1': _L0_ffn_in['b1'], 'L0_ffn_W2': _L0_ffn_in['W2'], 'L0_ffn_b2': _L0_ffn_in['b2'], 'L1_xattn_Wq': _L1_xattn_in['Wq'], 'L1_xattn_bq': _L1_xattn_in['bq'], 'L1_xattn_Wk': _L1_xattn_in['Wk'], 'L1_xattn_bk': _L1_xattn_in['bk'], 'L1_xattn_Wv': _L1_xattn_in['Wv'], 'L1_xattn_bv': _L1_xattn_in['bv'], 'L1_xattn_Wo': _L1_xattn_in['Wo'], 'L1_xattn_bo': _L1_xattn_in['bo'], 'L1_ffn_gate_W': _L1_ffn_in['gate_W'], 'L1_ffn_gate_b': _L1_ffn_in['gate_b'], 'L1_ffn_W1': _L1_ffn_in['W1'], 'L1_ffn_b1': _L1_ffn_in['b1'], 'L1_ffn_W2': _L1_ffn_in['W2'], 'L1_ffn_b2': _L1_ffn_in['b2'], 'L1_ffn_ln_gamma': _L1_ffn_in['ln_gamma'], 'L1_ffn_ln_beta': _L1_ffn_in['ln_beta'], 'L2_xattn_ig_kernel': _L2_xattn_in['ig_kernel'], 'L2_xattn_ig_bias': _L2_xattn_in['ig_bias'], 'L2_xattn_fg_kernel': _L2_xattn_in['fg_kernel'], 'L2_xattn_fg_bias': _L2_xattn_in['fg_bias'], 'L2_xattn_outnorm_weight': _L2_xattn_in['outnorm_weight'], 'L2_ffn_W_r': _L2_ffn_in['W_r'], 'L2_ffn_W_k': _L2_ffn_in['W_k'], 'L2_ffn_W_v': _L2_ffn_in['W_v'], 'L2_ffn_mu_r': _L2_ffn_in['mu_r'], 'L2_ffn_mu_k': _L2_ffn_in['mu_k'], 'L3_xattn_Wq': _L3_xattn_in['Wq'], 'L3_xattn_bq': _L3_xattn_in['bq'], 'L3_xattn_Wk': _L3_xattn_in['Wk'], 'L3_xattn_bk': _L3_xattn_in['bk'], 'L3_xattn_Wv': _L3_xattn_in['Wv'], 'L3_xattn_bv': _L3_xattn_in['bv'], 'L3_xattn_Wo': _L3_xattn_in['Wo'], 'L3_xattn_bo': _L3_xattn_in['bo'], 'L3_ffn_router_w': _L3_ffn_in['router_w'], 'L3_ffn_router_b': _L3_ffn_in['router_b'], 'L3_ffn_W': _L3_ffn_in['W'], 'L3_ffn_V': _L3_ffn_in['V'], 'L3_ffn_W_out': _L3_ffn_in['W_out']}

def reference(x, ctx_1024, mask_BxS2_bk0, L0_xattn_rms_scale, L0_xattn_q_w, L0_xattn_kv_w, L0_xattn_out_w, L0_ffn_Wg, L0_ffn_W1, L0_ffn_b1, L0_ffn_W2, L0_ffn_b2, L1_xattn_Wq, L1_xattn_bq, L1_xattn_Wk, L1_xattn_bk, L1_xattn_Wv, L1_xattn_bv, L1_xattn_Wo, L1_xattn_bo, L1_ffn_gate_W, L1_ffn_gate_b, L1_ffn_W1, L1_ffn_b1, L1_ffn_W2, L1_ffn_b2, L1_ffn_ln_gamma, L1_ffn_ln_beta, L2_xattn_ig_kernel, L2_xattn_ig_bias, L2_xattn_fg_kernel, L2_xattn_fg_bias, L2_xattn_outnorm_weight, L2_ffn_W_r, L2_ffn_W_k, L2_ffn_W_v, L2_ffn_mu_r, L2_ffn_mu_k, L3_xattn_Wq, L3_xattn_bq, L3_xattn_Wk, L3_xattn_bk, L3_xattn_Wv, L3_xattn_bv, L3_xattn_Wo, L3_xattn_bo, L3_ffn_router_w, L3_ffn_router_b, L3_ffn_W, L3_ffn_V, L3_ffn_W_out):
    import jax
    import jax.numpy as jnp

    def _L0_xattn_ref(x, mem_seq, mem_mask, rms_scale, q_w, kv_w, out_w):
        import jax, jax.numpy as jnp
        import numpy as np
        NUM_HEADS, NUM_KV, HEAD_DIM, WIDTH = (4, 1, 64, 256)
        MASK_FILL = -2.3819763e+38

        def _apply_rope(x, positions, max_wavelength=10000.0):
            d = x.shape[-1]
            freq_exp = 2.0 / d * jnp.arange(d // 2, dtype=jnp.float32)
            timescale = max_wavelength ** freq_exp
            radians = positions[..., None].astype(jnp.float32) / timescale
            radians = radians[..., None, :]
            sin, cos = (jnp.sin(radians), jnp.cos(radians))
            x1, x2 = jnp.split(x, 2, axis=-1)
            out = jnp.concatenate([x1 * cos - x2 * sin, x2 * cos + x1 * sin], axis=-1)
            return out.astype(x.dtype)

        def _rmsnorm(x, scale):
            var = jnp.mean(jnp.square(x.astype(jnp.float32)), axis=-1, keepdims=True)
            normed = x * jax.lax.rsqrt(var + 1e-06)
            return (normed * (1 + scale)).astype(x.dtype)
        B, S, _ = mem_seq.shape
        T = x.shape[1]
        G = NUM_HEADS // NUM_KV
        xn = _rmsnorm(x, rms_scale)
        mn = _rmsnorm(mem_seq, rms_scale)
        q = jnp.einsum('BTD,NDH->BTNH', xn, q_w)
        kv = jnp.einsum('BSD,cKDH->cBSKH', mn, kv_w)
        k, v = (kv[0], kv[1])
        q_pos = jnp.broadcast_to(jnp.arange(S, T + S), (B, T))
        k_pos = jnp.broadcast_to(jnp.arange(S), (B, S))
        q = _apply_rope(q, q_pos) * HEAD_DIM ** (-0.5)
        k = _apply_rope(k, k_pos)
        q = q.reshape(B, T, NUM_KV, G, HEAD_DIM)
        logits = jnp.einsum('BTKGH,BSKH->BKGTS', q, k, preferred_element_type=jnp.float32)
        masked = jnp.where(mem_mask[:, None, None, None, :], logits, MASK_FILL)
        probs = jax.nn.softmax(masked, axis=-1).astype(x.dtype)
        enc = jnp.einsum('BKGTS,BSKH->BTKGH', probs, v).reshape(B, T, NUM_HEADS, HEAD_DIM)
        return jnp.einsum('BTNH,NHD->BTD', enc, out_w)

    def _L0_ffn_ref(x, Wg, W1, b1, W2, b2):
        import jax, jax.numpy as jnp
        import numpy as np
        NUM_EXPERTS = 8
        TOP_K = 2
        B, S, D = x.shape
        E, _, H = W1.shape
        OUT = W2.shape[2]
        xm = x.reshape(-1, D)
        logits = xm @ Wg
        probs = jax.nn.softmax(logits, axis=-1)
        topk_p, topk_i = jax.lax.top_k(probs, TOP_K)
        flat_e = topk_i.reshape(-1)
        flat_p = topk_p.reshape(-1)
        order = jnp.argsort(flat_e)
        tok_idx = order // TOP_K
        e_sorted = flat_e[order]
        p_sorted = flat_p[order]
        xs = xm[tok_idx]
        y = jnp.zeros((xs.shape[0], OUT), dtype=xs.dtype)
        for e in range(E):
            h = jax.nn.relu(xs @ W1[e] + b1[e])
            ye = h @ W2[e] + b2[e]
            m = (e_sorted == e)[:, None].astype(xs.dtype)
            y = y + m * ye
        y = y * p_sorted[:, None]
        out = jnp.zeros((B * S, OUT), dtype=y.dtype).at[tok_idx].add(y)
        return out.reshape(B, S, OUT)

    def _L1_xattn_ref(q, k, v, Wq, bq, Wk, bk, Wv, bv, Wo, bo):
        import jax, jax.numpy as jnp
        import numpy as np
        B, L, D, H = (4, 512, 256, 16)
        DH = D // H
        SCALE = 1.0 / float(np.sqrt(DH))

        def _split_heads(x):
            b, l, _ = x.shape
            return x.reshape(b, l, H, DH).transpose(0, 2, 1, 3)
        qh = _split_heads(q @ Wq.T + bq)
        kh = _split_heads(k @ Wk.T + bk)
        vh = _split_heads(v @ Wv.T + bv)
        scores = jnp.einsum('bhqd,bhkd->bhqk', qh, kh) * SCALE
        attn = jax.nn.softmax(scores, axis=-1)
        out = jnp.einsum('bhqk,bhkd->bhqd', attn, vh)
        out = out.transpose(0, 2, 1, 3).reshape(q.shape[0], q.shape[1], D)
        return out @ Wo.T + bo

    def _L1_ffn_ref(x, gate_W, gate_b, W1, b1, W2, b2, ln_gamma, ln_beta):
        import jax, jax.numpy as jnp
        import numpy as np
        D = 256
        E = 8
        H = 512
        TOP_K = 2
        ALPHA = 0.5
        LN_EPS = 1e-05

        def _experts_all(x, W1, b1, W2, b2):
            h = jax.nn.relu(jnp.einsum('bld,edh->eblh', x, W1) + b1[:, None, None, :])
            return jnp.einsum('eblh,ehd->ebld', h, W2) + b2[:, None, None, :]

        def _selected_expert(x, expert_idx, W1, b1, W2, b2):
            oh = jax.nn.one_hot(expert_idx, E, dtype=x.dtype)
            return jnp.einsum('ebld,ble->bld', _experts_all(x, W1, b1, W2, b2), oh)

        def _layer_norm(x, gamma, beta):
            mu = jnp.mean(x, axis=-1, keepdims=True)
            var = jnp.mean(jnp.square(x - mu), axis=-1, keepdims=True)
            return (x - mu) * jax.lax.rsqrt(var + LN_EPS) * gamma + beta
        residual = x
        gate_logits = jnp.einsum('bld,de->ble', x, gate_W) + gate_b
        gate_weights = jax.nn.softmax(gate_logits, axis=-1)
        topk_vals, topk_idx = jax.lax.top_k(gate_weights, TOP_K)
        boost = jax.lax.stop_gradient(x)
        outs = []
        for i in range(TOP_K):
            eo = _selected_expert(boost, topk_idx[:, :, i], W1, b1, W2, b2)
            outs.append(eo)
            if i < TOP_K - 1:
                boost = boost + ALPHA * jax.lax.stop_gradient(eo)
        fused = sum((topk_vals[:, :, i:i + 1] * outs[i] for i in range(TOP_K)))
        return _layer_norm(residual + fused, ln_gamma, ln_beta)

    def _L2_xattn_ref(q, k, v, ig_kernel, ig_bias, fg_kernel, fg_bias, outnorm_weight):
        import jax, jax.numpy as jnp
        import numpy as np
        EPS_BACKEND = 1e-06
        NORM_EPS = 1e-06
        NUM_HEADS = 4

        def _mlstm_forward(q, k, v, ig_kernel, ig_bias, fg_kernel, fg_bias, outnorm_weight):
            B, S, E = q.shape
            NH = ig_bias.shape[0]
            DH = E // NH
            gate_input = jnp.concatenate([q, k, v], axis=-1)
            igate = gate_input @ ig_kernel + ig_bias
            fgate = gate_input @ fg_kernel + fg_bias
            qh = q.reshape(B, S, NH, DH).transpose(0, 2, 1, 3)
            kh = k.reshape(B, S, NH, DH).transpose(0, 2, 1, 3)
            vh = v.reshape(B, S, NH, DH).transpose(0, 2, 1, 3)
            ig = igate.transpose(0, 2, 1)
            fg = fgate.transpose(0, 2, 1)
            log_fg = jax.nn.log_sigmoid(fg)
            cums = jnp.concatenate([jnp.zeros((B, NH, 1), log_fg.dtype), jnp.cumsum(log_fg, axis=-1)], axis=-1)
            fg_mat = cums[..., :, None] - cums[..., None, :]
            mask = jnp.tril(jnp.ones((S + 1, S + 1), bool))
            fg_mat = jnp.where(mask, fg_mat, -jnp.inf)[..., 1:, 1:]
            log_D = fg_mat + ig[..., None, :]
            max_log_D = jnp.max(log_D, axis=-1, keepdims=True)
            D = jnp.exp(log_D - max_log_D)
            qk = jnp.einsum('bnsd,bntd->bnst', qh, kh) / jnp.sqrt(jnp.float32(DH))
            C = qk * D
            normalizer = jnp.maximum(jnp.abs(C.sum(-1, keepdims=True)), jnp.exp(-max_log_D))
            h = jnp.einsum('bnst,bntd->bnsd', C / (normalizer + EPS_BACKEND), vh)
            h = h.transpose(0, 2, 1, 3)
            mean = h.mean(-1, keepdims=True)
            var = h.var(-1, keepdims=True)
            hn = (h - mean) * jax.lax.rsqrt(var + NORM_EPS) * outnorm_weight
            return hn.reshape(B, S, E)
        return _mlstm_forward(q, k, v, ig_kernel, ig_bias, fg_kernel, fg_bias, outnorm_weight)

    def _L2_ffn_ref(x, W_r, W_k, W_v, mu_r, mu_k):
        import jax, jax.numpy as jnp
        import numpy as np
        DIM = 256

        def _reference_tuple_inner(x, W_r, W_k, W_v, mu_r, mu_k):
            B, T, C = x.shape
            x_prev = jnp.concatenate([jnp.zeros((B, 1, C), x.dtype), x[:, :-1, :]], axis=1)
            xr = mu_r * x + (1.0 - mu_r) * x_prev
            xk = mu_k * x + (1.0 - mu_k) * x_prev
            r = jax.nn.sigmoid(jnp.einsum('btc,dc->btd', xr, W_r))
            k = jnp.einsum('btc,dc->btd', xk, W_k)
            k_act = jnp.square(jax.nn.relu(k))
            out = r * jnp.einsum('btc,dc->btd', k_act, W_v)
            new_state = x[:, -1, :]
            return (out, new_state)
        return _reference_tuple_inner(x, W_r, W_k, W_v, mu_r, mu_k)[0]

    def _L3_xattn_ref(q, k, v, Wq, bq, Wk, bk, Wv, bv, Wo, bo):
        import jax, jax.numpy as jnp
        import numpy as np
        D_MODEL = 256
        HEADS = 16
        D_K = D_MODEL // HEADS
        B, S, _ = q.shape

        def proj(x, W, b):
            return (x @ W.T + b).reshape(B, -1, HEADS, D_K).transpose(0, 2, 1, 3)
        qh = proj(q, Wq, bq)
        kh = proj(k, Wk, bk)
        vh = proj(v, Wv, bv)
        scores = jnp.einsum('bhqd,bhkd->bhqk', qh, kh) / jnp.sqrt(jnp.float32(D_K))
        attn = jax.nn.softmax(scores, axis=-1)
        out = jnp.einsum('bhqk,bhkd->bhqd', attn, vh)
        concat = out.transpose(0, 2, 1, 3).reshape(B, S, D_MODEL)
        return concat @ Wo.T + bo

    def _L3_ffn_ref(x, router_w, router_b, W, V, W_out):
        import jax, jax.numpy as jnp
        import numpy as np
        B, T = (2, 512)
        D_MODEL, D_HIDDEN = (256, 512)
        N_EXPERTS, TOP_K = (8, 2)
        N_TOKENS = B * T
        CAPACITY = 2 * N_TOKENS * TOP_K // N_EXPERTS
        Bq, Tq, D = x.shape
        N = Bq * Tq
        x_flat = x.reshape(N, D)
        router_logits = x_flat @ router_w.T + router_b
        top_vals, top_ids = jax.lax.top_k(router_logits, TOP_K)
        top_probs = jax.nn.softmax(top_vals, axis=-1)
        x_pad = jnp.concatenate([x_flat, jnp.zeros((1, D), x_flat.dtype)], axis=0)
        probs_pad = jnp.concatenate([top_probs, jnp.zeros((1, TOP_K), top_probs.dtype)], axis=0)
        out = jnp.zeros((N + 1, D), x_flat.dtype)
        for e in range(N_EXPERTS):
            tok, slot = jnp.nonzero(top_ids == e, size=CAPACITY, fill_value=(N, 0))
            w = probs_pad[tok, slot][:, None]
            xin = x_pad[tok]
            a = xin @ W[e]
            b = xin @ V[e]
            y = a * (b * jax.nn.sigmoid(b)) @ W_out[e]
            out = out.at[tok].add(y * w)
        return out[:N].reshape(Bq, Tq, D)
    x = x + _L0_xattn_ref(_layernorm(x, axis=-1), ctx_1024, mask_BxS2_bk0, L0_xattn_rms_scale, L0_xattn_q_w, L0_xattn_kv_w, L0_xattn_out_w)
    x = x + _L0_ffn_ref(_layernorm(x, axis=-1), L0_ffn_Wg, L0_ffn_W1, L0_ffn_b1, L0_ffn_W2, L0_ffn_b2)
    x = x + _L1_xattn_ref(_layernorm(x, axis=-1), ctx_1024, ctx_1024, L1_xattn_Wq, L1_xattn_bq, L1_xattn_Wk, L1_xattn_bk, L1_xattn_Wv, L1_xattn_bv, L1_xattn_Wo, L1_xattn_bo)
    x = x + _L1_ffn_ref(_layernorm(x, axis=-1), L1_ffn_gate_W, L1_ffn_gate_b, L1_ffn_W1, L1_ffn_b1, L1_ffn_W2, L1_ffn_b2, L1_ffn_ln_gamma, L1_ffn_ln_beta)
    x = x + _L2_xattn_ref(_layernorm(x, axis=-1), ctx_1024, ctx_1024, L2_xattn_ig_kernel, L2_xattn_ig_bias, L2_xattn_fg_kernel, L2_xattn_fg_bias, L2_xattn_outnorm_weight)
    x = x + _L2_ffn_ref(_layernorm(x, axis=-1), L2_ffn_W_r, L2_ffn_W_k, L2_ffn_W_v, L2_ffn_mu_r, L2_ffn_mu_k)
    x = x + _L3_xattn_ref(_layernorm(x, axis=-1), ctx_1024, ctx_1024, L3_xattn_Wq, L3_xattn_bq, L3_xattn_Wk, L3_xattn_bk, L3_xattn_Wv, L3_xattn_bv, L3_xattn_Wo, L3_xattn_bo)
    x = x + _L3_ffn_ref(_layernorm(x, axis=-1), L3_ffn_router_w, L3_ffn_router_b, L3_ffn_W, L3_ffn_V, L3_ffn_W_out)
    return x

_drawn_inputs = setup_inputs


def setup_inputs(seed=0):
    import zlib

    import numpy as np

    out = dict(_drawn_inputs(seed))
    spreads = {'L1_xattn_bq': (0.0, 0.8),
     'L1_xattn_bk': (0.0, 0.8),
     'L1_xattn_bv': (0.0, 0.1),
     'L1_xattn_bo': (0.0, 0.1),
     'L1_ffn_gate_b': (0.0, 0.736),
     'L1_ffn_b1': (0.0, 0.638),
     'L1_ffn_b2': (0.0, 0.391),
     'L1_ffn_ln_gamma': (1.0, 0.2),
     'L1_ffn_ln_beta': (0.0, 0.1),
     'L2_xattn_outnorm_weight': (1.0, 0.2),
     'L3_xattn_bq': (0.0, 0.574),
     'L3_xattn_bk': (0.0, 0.8),
     'L3_xattn_bv': (0.0, 0.1),
     'L3_xattn_bo': (0.0, 0.1),
     'L3_ffn_router_b': (0.0, 0.1)}
    factors = {'L0_xattn_rms_scale': 3.501,
     'L0_ffn_b1': 8.0,
     'L0_ffn_b2': 4.835,
     'L1_xattn_Wq': 8.0,
     'L1_xattn_Wk': 8.0,
     'L1_ffn_gate_W': 2.814,
     'L1_ffn_W1': 3.648,
     'L1_ffn_W2': 3.316,
     'L2_xattn_ig_bias': 8.0,
     'L2_ffn_W_r': 4.79,
     'L2_ffn_mu_r': 7.367,
     'L2_ffn_mu_k': 2.748}
    for name, (base, spread) in spreads.items():
        noise = np.random.default_rng([zlib.crc32(name.encode()), seed]).standard_normal(out[name].shape)
        drawn = base * np.exp(spread * noise) if base else spread * noise
        out[name] = jnp.asarray(drawn.astype(out[name].dtype))
    for name, factor in factors.items():
        out[name] = (out[name] * factor).astype(out[name].dtype)
    return out
```

```python
from contextlib import ExitStack

import numpy as np

import concourse.bass as bass
from concourse import mybir

F32 = mybir.dt.float32
I32 = mybir.dt.int32
U32 = mybir.dt.uint32
U8 = mybir.dt.uint8
ALU = mybir.AluOpType
ACT = mybir.ActivationFunctionType
AX = mybir.AxisListType

P = 128
B, S, D = 8, 256, 256
TPB = S // P
NT = B * TPB
DC = D // P
LN_EPS = 1e-5
E, H = 8, 512
HC = H // P
R = 128
TILES = 2 * B * S // R + E
CAPACITY = 512

CONST = {}
_at = 0
for _name, _width in (("ident", P), ("before", P), ("ones", P), ("upto", P), ("restart", P), ("head", 8),
                      ("iota", 8), ("even", 1), ("odd", 1), ("pick", 4 * P), ("half", 16), ("cosq", S), ("sinq", S), ("cosk", S), ("sink", S)):
    CONST[_name] = (_at, _at + _width)
    _at += _width
CONSTS = _at


PRIMED = 1


def prime(eng, *sems):
    for sem in sems:
        eng.sem_inc(sem, PRIMED)


def semaphores(nc, ctx, name):
    made = []

    def clear():
        nc.clear_and_free_semaphores(made)
        nc.all_engine_barrier(sem_only=True)

    ctx.callback(clear)

    def sem(n):
        made.append(nc.alloc_semaphore(name + n))
        return made[-1]

    return sem


class Chain:

    def __init__(self, eng, sem, base=0):
        self.eng, self.sem, self.base, self.n = eng, sem, base, 0

    def __call__(self, ins):
        self.n += 1
        ins.then_inc(self.sem, 1)
        self.eng.wait_ge(self.sem, self.base + self.n)


def bcast(ap, n):
    return ap.unsqueeze(2).to_broadcast([ap.shape[0], ap.shape[1], n])


def layer_norm_stats(vector, X, stats, moments, var_eps, stats_done, ready, eps=LN_EPS):
    for t in range(NT):
        vector.bn_stats(stats[:, t, :], X[:, t, :]).then_inc(stats_done, 1)
    for t in range(NT):
        vector.wait_ge(stats_done, t + 1)
        vector.bn_aggr(moments[:, t, :], stats[:, t, :]).then_inc(stats_done, 1)
    vector.wait_ge(stats_done, 2 * NT)
    vector.tensor_scalar(var_eps[:, :], moments[:, :, 1], eps, None, ALU.add).then_inc(ready, 1)


def layer_norm_root(pool, G, rstd, var_eps, var_ready, rstd_ready):
    pool.wait_ge(var_ready, 1)
    pool.tensor_tensor(rstd[:, :], var_eps[:, :], G.mhalf(NT), ALU.pow).then_inc(rstd_ready, 1)


def over_batches(eng, front, pair, pairs, finish):
    def body(b, q, before, after):
        for g in range(pairs):
            pair(b, q, g, before)
            if before is not None and g in finish:
                finish[g](before)
            if after is not None and g in front:
                front[g](after, 1 - q)

    for piece in front.values():
        piece(0, 0)
    body(0, 0, None, 1)
    with eng.Fori(0, B // 2 - 1) as two:
        for q in (1, 0):
            b = 2 * two + 2 - q
            body(b, q, b - 1, b + 1)
    body(B - 1, 1, B - 2, None)
    pair(B, 0, 0, B - 1)
    for piece in finish.values():
        piece(B - 1)


def mha_block(nc, G, name, weights, vectors, ctx_t):
    HEADS, DH = 16, D // 16
    PAIRS = HEADS // 2
    GB = TPB * PAIRS
    VW = DH + 1
    PVN = 6 * VW
    VCOLS = (HEADS - 1) * VW + PVN
    X, PS = G.X, G.PS
    with ExitStack() as ctx:
        sb = lambda n, shape, dt=F32: ctx.enter_context(nc.sbuf_tensor(name + n, shape, dt))
        sem = semaphores(nc, ctx, name)
        w = sb("w", [P, 4, DC, D])
        vec = sb("vec", [P, 2 * DC + 2 * D])
        nbq = sb("nbq", [P, DC])
        ctxT = sb("ctxT", [P, DC, S])
        stats, moments = sb("stats", [P, NT, 6]), sb("moments", [P, NT, 2])
        var_eps, rstd = sb("var_eps", [P, NT]), sb("rstd", [P, NT])
        xn = sb("xn", [P, TPB, D])
        xnT = sb("xnT", [P, DC, S])
        qT, kT = sb("qT", [P, 2, DC, S]), sb("kT", [P, DC, S])
        kTm = sb("kTm", [P, 2, HEADS, S])
        vaug = sb("vaug", [P, 2, TPB, VCOLS])
        nmax = sb("nmax", [P, 2, 2])
        prob = sb("prob", [P, 2, 2, S])
        probT = sb("probT", [P, 2, 4, P])
        rsum = sb("rsum", [P, TPB, HEADS])
        enc, encT = sb("enc", [P, TPB, D]), sb("encT", [P, DC, S])
        w_landed, ctx_landed = sem("w_landed"), sem("ctx_landed")
        stats_done, chain_s, kmask_s = sem("stats_done"), sem("chain"), sem("kmask_done")
        var_ready, rstd_ready, xn_ready = sem("var_ready"), sem("rstd_ready"), sem("xn_ready")
        xT_done, xnT_ready = sem("xT_done"), sem("xnT_ready")
        q_done, q_ready = sem("q_done"), sem("q_ready")
        k_done, k_ready = sem("k_done"), sem("k_ready")
        v_done, v_ready = sem("v_done"), sem("v_ready")
        score_done, max_ready, prob_ready = sem("score_done"), sem("max_ready"), sem("prob_ready")
        probT_done, probT_ready, pv_done = sem("probT_done"), sem("probT_ready"), sem("pv_done")
        enc_ready, encT_done, encT_ready = sem("enc_ready"), sem("encT_done"), sem("encT_ready")
        out_done, added, nbq_ready, ones_ready = sem("out_done"), sem("added"), sem("nbq_ready"), sem("ones_ready")
        bq, bk = vec[:, 0:DC], vec[:, DC:2 * DC]
        bv, bo = vec[:, 2 * DC:2 * DC + D], vec[:, 2 * DC + D:2 * DC + 2 * D]
        ps_x, ps_q = PS[0], PS[1]
        ps_s, ps_t, ps_o = [PS[2], PS[3]], [PS[4], PS[5]], [PS[6], PS[7]]
        LAST = GB - 1
        CH = TPB + 1
        block = ctx.enter_context(nc.Block())

        @block.sync
        def _(sync):
            sync.dma_start(vec[:, :], vectors).then_inc(w_landed, 16)
            for i in range(4):
                sync.dma_start(w[:, i, :, :], weights[i].rearrange("(c p) n -> p c n", p=P)).then_inc(w_landed, 16)
            with sync.Fori(0, B) as b:
                sync.wait_ge(v_done, PRIMED + b)
                sync.dma_start(ctxT[:, :, :], ctx_t[b].rearrange("(c p) n -> p c n", p=P)).then_inc(ctx_landed, 16)

        @block.gpsimd
        def _(pool):
            prime(pool, kmask_s)
            layer_norm_root(pool, G, rstd, var_eps, var_ready, rstd_ready)

            def mask_keys(b, q):
                pool.wait_ge(k_ready, PRIMED + b + 1)
                if not isinstance(b, int) or b >= 2:
                    pool.wait_ge(score_done, PRIMED + GB * (b - 1))
                for h in range(HEADS):
                    rows_of_head = G.const("head")[:, h % 8:h % 8 + 1].to_broadcast([P, S])
                    ins = pool.tensor_tensor(kTm[:, q, h, :], kT[:, h // 8, :], rows_of_head, ALU.mult)
                    if h % 2:
                        ins.then_inc(kmask_s, 1)

            mask_keys(0, 0)
            mask_keys(1, 1)
            with pool.Fori(1, B // 2) as two:
                for q in range(2):
                    mask_keys(2 * two + q, q)

        @block.scalar
        def _(act):
            prime(act, q_ready, prob_ready)
            act.wait_ge(w_landed, 16 * 5)
            act.mul(nbq[:, :], bq, -0.25).then_inc(nbq_ready, 1)
            act.wait_ge(nbq_ready, 1)

            def queries(b, q):
                act.wait_ge(q_done, PRIMED + b + 1)
                if not isinstance(b, int) or b >= 2:
                    act.wait_ge(score_done, PRIMED + GB * (b - 1))
                for c in range(DC):
                    ins = act.activation(qT[:, q, c, :], ps_q[:, c * S:(c + 1) * S], ACT.Identity,
                                         bias=nbq[:, c:c + 1], scale=-0.25)
                ins.then_inc(q_ready, 1)

            def exponents(b, q, g, before):
                if isinstance(b, int) and b == B:
                    return
                act.wait_ge(max_ready, PRIMED + GB * b + g + 1)
                if before is not None or g >= 2:
                    act.wait_ge(probT_done, PRIMED + GB * b + g - 1)
                for i in range(2):
                    ins = act.activation(prob[:, g % 2, i, :], ps_s[g % 2][:, i * S:(i + 1) * S], ACT.Exp,
                                         bias=nmax[:, g % 2, i:i + 1], scale=-1.0)
                ins.then_inc(prob_ready, 1)

            over_batches(act, {10: queries}, exponents, GB, {})

        @block.vector
        def _(vector):
            prime(vector, chain_s, xn_ready, xnT_ready, k_ready, v_ready, max_ready, probT_ready, enc_ready, encT_ready, added)
            vector.memset(vaug[:, :, :, :], 1.0).then_inc(ones_ready, 1)
            layer_norm_stats(vector, X, stats, moments, var_eps, stats_done, var_ready)
            vector.wait_ge(w_landed, 16 * 5)
            vector.wait_ge(ones_ready, 1)
            vector.wait_ge(rstd_ready, 1)

            def normalize(b, q):
                vector.wait_ge(xT_done, PRIMED + b)
                for k in range(TPB):
                    t = TPB * b + k
                    ins = vector.tensor_scalar(xn[:, k, :], X[:, bass.ds(t, 1), :].rearrange("p o d -> p (o d)"),
                                               moments[:, bass.ds(t, 1), 0], rstd[:, bass.ds(t, 1)],
                                               ALU.subtract, ALU.mult)
                ins.then_inc(xn_ready, 1)

            def x_turned(b, q):
                vector.wait_ge(xT_done, PRIMED + b + 1)
                vector.wait_ge(q_done, PRIMED + b)
                vector.tensor_copy(xnT[:, :, :].rearrange("p c s -> p (c s)"), ps_x[:, :]).then_inc(xnT_ready, 1)

            def keys(b, q):
                vector.wait_ge(k_done, PRIMED + b + 1)
                vector.wait_ge(kmask_s, PRIMED + PAIRS * b)
                for c in range(DC):
                    ins = vector.tensor_scalar(kT[:, c, :], ps_x[:, c * S:(c + 1) * S], bk[:, c:c + 1], None, ALU.add)
                ins.then_inc(k_ready, 1)

            def values(b, q):
                vector.wait_ge(v_done, PRIMED + b + 1)
                if not isinstance(b, int) or b >= 2:
                    vector.wait_ge(pv_done, PRIMED + GB * (b - 1))
                for k in range(TPB):
                    ins = vector.tensor_tensor(
                        vaug[:, q, k, 0:HEADS * VW].rearrange("p (h v) -> p h v", v=VW)[:, :, 0:DH],
                        ps_q[:, k * D:(k + 1) * D].rearrange("p (h v) -> p h v", v=DH),
                        bv.rearrange("p (h v) -> p h v", v=DH), ALU.add)
                ins.then_inc(v_ready, 1)

            def turn_probabilities(b, g):
                vector.wait_ge(probT_done, PRIMED + GB * b + g + 1)
                if not isinstance(b, int) or b > 0 or g >= 2:
                    vector.wait_ge(pv_done, PRIMED + GB * b + g - 1)
                vector.tensor_copy(probT[:, g % 2, :, :].rearrange("p a t -> p (a t)"),
                                   ps_t[g % 2][:, :]).then_inc(probT_ready, 1)

            def encode(b, k):
                chain = Chain(vector, chain_s, PRIMED + b * CH + k)
                vector.wait_ge(pv_done, PRIMED + GB * b + PAIRS * (k + 1))
                o = ps_o[k][:, 0:HEADS * VW].rearrange("p (h v) -> p h v", v=VW)
                chain(vector.reciprocal(rsum[:, k, :], o[:, :, DH]))
                vector.wait_ge(encT_done, PRIMED + b)
                vector.tensor_tensor(enc[:, k, :].rearrange("p (h v) -> p h v", v=DH), o[:, :, 0:DH],
                                     bcast(rsum[:, k, :], DH), ALU.mult).then_inc(enc_ready, 1)

            def pair(b, q, g, before):
                if not isinstance(b, int) or b < B:
                    vector.wait_ge(score_done, PRIMED + GB * b + g + 1)
                    if before is not None or g >= 2:
                        vector.wait_ge(prob_ready, PRIMED + GB * b + g - 1)
                    vector.tensor_reduce(nmax[:, g % 2, :], ps_s[g % 2][:, :].rearrange("p (h s) -> p h s", s=S),
                                         AX.X, ALU.min).then_inc(max_ready, 1)
                if g:
                    turn_probabilities(b, g - 1)
                elif before is not None:
                    turn_probabilities(before, LAST)
                if g == PAIRS + 1:
                    encode(b, 0)

            def enc_turned(b):
                vector.wait_ge(encT_done, PRIMED + b + 1)
                vector.wait_ge(out_done, PRIMED + b)
                vector.tensor_copy(encT[:, :, :].rearrange("p c s -> p (c s)"), ps_x[:, :]).then_inc(encT_ready, 1)

            def add(b):
                chain = Chain(vector, chain_s, PRIMED + b * CH + TPB)
                vector.wait_ge(out_done, PRIMED + b + 1)
                x = X[:, bass.ds(TPB * b, TPB), :]
                chain(vector.tensor_tensor(x, ps_q[:, :].rearrange("p (k d) -> p k d", d=D), x, ALU.add))
                vector.tensor_tensor(x, x, bo.unsqueeze(1).to_broadcast([P, TPB, D]), ALU.add).then_inc(added, 1)

            over_batches(vector, {6: normalize, 8: x_turned, 10: keys, 12: values}, pair, GB,
                         {1: lambda b: encode(b, 1), 4: enc_turned, 6: add})

        @block.tensor
        def _(pe):
            prime(pe, xT_done, q_done, k_done, v_done, score_done, probT_done, pv_done, encT_done, out_done)
            ident = G.const("ident")
            pe.wait_ge(w_landed, 16 * 5)

            def turn(source, to):
                for c in range(DC):
                    for k in range(TPB):
                        ins = pe.transpose(to[:, c * S + k * P:c * S + (k + 1) * P],
                                           source[:, k, c * P:(c + 1) * P], ident)
                return ins

            def turn_x(b, q):
                pe.wait_ge(xn_ready, PRIMED + b + 1)
                if not isinstance(b, int) or b >= 2:
                    pe.wait_ge(encT_ready, PRIMED + b - 1)
                turn(xn, ps_x).then_inc(xT_done, 1)

            def project_qk(b, q):
                pe.wait_ge(xnT_ready, PRIMED + b + 1)
                if not isinstance(b, int) or b >= 2:
                    pe.wait_ge(added, PRIMED + b - 1)
                pe.wait_ge(ctx_landed, 16 * (b + 1))
                for i, source, to, done in ((0, xnT, ps_q, q_done), (1, ctxT, ps_x, k_done)):
                    for m in range(DC):
                        for c in range(DC):
                            ins = pe.matmul(to[:, m * S:(m + 1) * S], w[:, i, c, m * P:(m + 1) * P], source[:, c, :],
                                            start=c == 0, stop=c == DC - 1)
                    ins.then_inc(done, 1)

            def project_v(b, q):
                pe.wait_ge(q_ready, PRIMED + b + 1)
                for k in range(TPB):
                    for c in range(DC):
                        ins = pe.matmul(ps_q[:, k * D:(k + 1) * D], ctxT[:, c, k * P:(k + 1) * P], w[:, 2, c, :],
                                        start=c == 0, stop=c == DC - 1)
                ins.then_inc(v_done, 1)

            def scores(b, q, g):
                k, j = divmod(g, PAIRS)
                if k == 0:
                    pe.wait_ge(kmask_s, PRIMED + PAIRS * b + j + 1)
                if g == 0:
                    pe.wait_ge(q_ready, PRIMED + b + 1)
                if not isinstance(b, int) or b > 0 or g >= 2:
                    pe.wait_ge(prob_ready, PRIMED + GB * b + g - 1)
                pe.matmul(ps_s[g % 2][:, :], qT[:, q, j // 4, k * P:(k + 1) * P], kTm[:, q, 2 * j:2 * j + 2, :],
                          start=True, stop=True).then_inc(score_done, 1)

            def transposes(b, g):
                pe.wait_ge(prob_ready, PRIMED + GB * b + g + 1)
                if not isinstance(b, int) or b > 0 or g >= 2:
                    pe.wait_ge(probT_ready, PRIMED + GB * b + g - 1)
                for i in range(2):
                    for c in range(TPB):
                        ins = pe.transpose(ps_t[g % 2][:, (2 * i + c) * P:(2 * i + c + 1) * P],
                                           prob[:, g % 2, i, c * P:(c + 1) * P], ident)
                ins.then_inc(probT_done, 1)

            def values(b, q, g):
                k, j = divmod(g, PAIRS)
                pe.wait_ge(probT_ready, PRIMED + GB * b + g + 1)
                if j == 0 and (not isinstance(b, int) or b > 0):
                    pe.wait_ge(enc_ready, PRIMED + TPB * (b - 1) + k + 1)
                if g == 0:
                    pe.wait_ge(v_ready, PRIMED + b + 1)
                for i in range(2):
                    at = (2 * j + i) * VW
                    for c in range(TPB):
                        ins = pe.matmul(ps_o[k][:, at:at + PVN], probT[:, g % 2, 2 * i + c, :],
                                        vaug[:, q, c, at:at + PVN], start=c == 0, stop=c == TPB - 1)
                ins.then_inc(pv_done, 1)

            def pair(b, q, g, before):
                if not isinstance(b, int) or b < B:
                    if before is None and g == 0:
                        scores(b, q, 0)
                    if g < LAST:
                        scores(b, q, g + 1)
                    elif not (isinstance(b, int) and b == B - 1):
                        scores(b + 1, 1 - q, 0)
                    transposes(b, g)
                if g:
                    values(b, q, g - 1)
                elif before is not None:
                    values(before, 1 - q, LAST)

            def turn_enc(b):
                pe.wait_ge(enc_ready, PRIMED + TPB * (b + 1))
                pe.wait_ge(k_ready, PRIMED + b + 1 + (0 if isinstance(b, int) and b == B - 1 else 1))
                turn(enc, ps_x).then_inc(encT_done, 1)

            def project_out(b):
                pe.wait_ge(encT_ready, PRIMED + b + 1)
                pe.wait_ge(v_ready, PRIMED + b + 1 + (0 if isinstance(b, int) and b == B - 1 else 1))
                for k in range(TPB):
                    for c in range(DC):
                        ins = pe.matmul(ps_q[:, k * D:(k + 1) * D], encT[:, c, k * P:(k + 1) * P], w[:, 3, c, :],
                                        start=c == 0, stop=c == DC - 1)
                ins.then_inc(out_done, 1)

            over_batches(pe, {7: turn_x, 9: project_qk, 11: project_v}, pair, GB, {3: turn_enc, 5: project_out})


class Routing:

    def __init__(self, nc, ctx, name):
        sb = lambda n, shape, dt=F32: ctx.enter_context(nc.sbuf_tensor(name + n, shape, dt))
        self.xn = sb("xn", [P, NT, D])
        self.slots = sb("slots", [P, 2, NT], U32)
        self.share = sb("share", [P, 2, NT])
        self.bounds = sb("bounds", [P, 2, 2, E], I32)
        self.took = [sb("took0", [P, NT, D]), sb("took1", [P, NT, D])]


def scatter_rows(pool, G, source, slots, ready, scattered):
    pool.wait_ge(ready, 1)
    for t in range(NT):
        pool.indirect_dma_start(G.rows[:, :], bass.IndirectOffsetOnAxis(slots[:, t:t + 1], 0),
                                source[:, t, :], None).then_inc(scattered, 16)


def router_block(nc, G, name, rt, w_router, bias, joint, over_all, capacity):
    X, PS = G.X, G.PS
    with ExitStack() as ctx:
        sb = lambda n, shape, dt=F32: ctx.enter_context(nc.sbuf_tensor(name + n, shape, dt))
        sem = semaphores(nc, ctx, name)
        w, bias_sb = sb("w", [P, DC, E]), sb("bias", [P, E])
        stats, moments = sb("stats", [P, NT, 6]), sb("moments", [P, NT, 2])
        var_eps, rstd = sb("var_eps", [P, NT]), sb("rstd", [P, NT])
        xT = sb("xT", [P, 2, DC, P])
        logits, best = sb("logits", [P, NT, E]), sb("best", [P, NT, 8])
        best_at = sb("best_at", [P, NT, 8], U32)
        weight, total = sb("weight", [P, NT, 8]), sb("total", [P, NT])
        chosen_at = sb("chosen_at", [P, 2, NT])
        chosen = sb("chosen", [P, 3, NT, E])
        tile_sum, running = sb("tile_sum", [P, E, NT]), sb("running", [P, E, NT])
        rank = sb("rank", [P, NT, E])
        picked = sb("picked", [P, NT, E])
        tiles, tiles_i, end = sb("tiles", [P, E]), sb("tiles_i", [P, E], I32), sb("end", [P, E])
        first = sb("first", [P, E])
        slot_f, keep = sb("slot_f", [P, NT]), sb("keep", [P, NT])
        landed, stats_done, chain_s = sem("landed"), sem("stats_done"), sem("chain")
        var_ready, rstd_ready, xn_ready = sem("var_ready"), sem("rstd_ready"), sem("xn_ready")
        xT_done, xT_ready, logits_done = sem("xT_done"), sem("xT_ready"), sem("logits_done")
        shifted, weight_ready = sem("shifted"), sem("weight_ready")
        chosen_ready, counted = sem("chosen_ready"), sem("counted")
        slots_ready, scattered = sem("slots_ready"), sem("scattered")
        ps_logits, ps_within, ps_tile = PS[2], PS[3], PS[4]
        dispatches = [(2, (0, 1))] if joint else [(0, (0,)), (1, (1,))]
        block = ctx.enter_context(nc.Block())

        @block.sync
        def _(sync):
            sync.dma_start(w[:, :, :], w_router.rearrange("(c p) e -> p c e", p=P)).then_inc(landed, 16)
            sync.dma_start(bias_sb[:, :], bias).then_inc(landed, 16)

        @block.gpsimd
        def _(pool):
            layer_norm_root(pool, G, rstd, var_eps, var_ready, rstd_ready)
            pool.wait_ge(xn_ready, NT)
            for k in range(2 if joint else 1):
                scatter_rows(pool, G, rt.xn, rt.slots[:, k, :], slots_ready, scattered)
            pool.wait_ge(scattered, 16 * NT * (2 if joint else 1))

        @block.scalar
        def _(act):
            for t in range(NT):
                act.wait_ge(xT_done, t + 1)
                if t >= 2:
                    act.wait_ge(logits_done, t - 1)
                act.copy(xT[:, t % 2, :, :].rearrange("p c s -> p (c s)"), PS[t % 2][:, 0:D]).then_inc(xT_ready, 1)
            act.wait_ge(shifted, 1)
            act.activation(weight[:, :, :], weight[:, :, :], ACT.Exp).then_inc(weight_ready, 1)

        @block.tensor
        def _(pe):
            pe.wait_ge(landed, 32)

            def logits_of(t):
                pe.wait_ge(xT_ready, t + 1)
                for c in range(DC):
                    ins = pe.matmul(ps_logits[:, t * E:(t + 1) * E], xT[:, t % 2, c, :], w[:, c, :],
                                    start=c == 0, stop=c == DC - 1)
                ins.then_inc(logits_done, 1)

            for t in range(NT):
                pe.wait_ge(xn_ready, t + 1)
                if t >= 2:
                    pe.wait_ge(xT_ready, t - 1)
                for c in range(DC):
                    ins = pe.transpose(PS[t % 2][:, c * P:(c + 1) * P], rt.xn[:, t, c * P:(c + 1) * P],
                                       G.const("ident"))
                ins.then_inc(xT_done, 1)
                if t:
                    logits_of(t - 1)
            logits_of(NT - 1)
            for n, (which, _) in enumerate(dispatches):
                pe.wait_ge(chosen_ready, 1)
                rhs = chosen[:, which, :, :].rearrange("p t e -> p (t e)")
                pe.matmul(ps_within[:, n * P:(n + 1) * P], G.const("before"), rhs, start=True, stop=True)
                pe.matmul(ps_tile[:, n * P:(n + 1) * P], G.const("ones"), rhs, start=True, stop=True).then_inc(counted, 1)

        @block.vector
        def _(vector):
            chain = Chain(vector, chain_s)
            layer_norm_stats(vector, X, stats, moments, var_eps, stats_done, var_ready)
            vector.wait_ge(rstd_ready, 1)
            for t in range(NT):
                vector.tensor_scalar(rt.xn[:, t, :], X[:, t, :], moments[:, t, 0:1], rstd[:, t:t + 1],
                                     ALU.subtract, ALU.mult).then_inc(xn_ready, 1)
            vector.wait_ge(landed, 32)
            vector.wait_ge(logits_done, NT)
            chain(vector.tensor_tensor(logits[:, :, :], ps_logits[:, 0:NT * E].rearrange("p (t e) -> p t e", e=E),
                                       bias_sb[:, :].unsqueeze(1).to_broadcast([P, NT, E]), ALU.add))
            for t in range(NT):
                ins = vector.max(best[:, t, :], logits[:, t, :])
                if t == NT - 1:
                    chain(ins)
            for t in range(NT):
                ins = vector.max_index(best_at[:, t, :], best[:, t, :], logits[:, t, :])
            vector.tensor_tensor(weight[:, :, :], best[:, :, :], best[:, :, 0:1].to_broadcast([P, NT, 8]),
                                 ALU.subtract).then_inc(shifted, 1)
            vector.wait_ge(shifted, 1)
            chain(vector.tensor_copy(chosen_at[:, :, :], best_at[:, :, 0:2].rearrange("p t k -> p k t")))
            iota = G.const("iota").unsqueeze(1).to_broadcast([P, NT, E])
            for k in range(2):
                chain(vector.tensor_tensor(chosen[:, k, :, :], iota, bcast(chosen_at[:, k, :], E), ALU.is_equal))
            vector.tensor_tensor(chosen[:, 2, :, :], chosen[:, 0, :, :], chosen[:, 1, :, :],
                                 ALU.add).then_inc(chosen_ready, 1)
            vector.wait_ge(weight_ready, 1)
            chain(vector.tensor_reduce(total[:, :], weight[:, :, :] if over_all else weight[:, :, 0:2], AX.X, ALU.add))
            chain(vector.reciprocal(total[:, :], total[:, :]))
            for k in range(2):
                chain(vector.tensor_tensor(rt.share[:, k, :], weight[:, :, k], total[:, :], ALU.mult))
            for n, (which, ks) in enumerate(dispatches):
                vector.wait_ge(counted, len(dispatches))
                within = ps_within[:, n * P:(n + 1) * P].rearrange("p (t e) -> p t e", e=E)
                chain(vector.tensor_copy(tile_sum[:, :, :],
                                         ps_tile[:, n * P:(n + 1) * P].rearrange("p (t e) -> p e t", e=E)))
                flat = lambda a: a.rearrange("p e t -> p (e t)")
                chain(vector.tensor_tensor_scan(flat(running[:, :, :]), G.const("restart"), flat(tile_sum[:, :, :]),
                                                0.0, ALU.mult, ALU.add))
                chain(vector.tensor_scalar(tiles[:, :], running[:, :, NT - 1], float(R - 1), 1.0 / R, ALU.add, ALU.mult))
                chain(vector.tensor_scalar(tiles_i[:, :], tiles[:, :], -0.498, None, ALU.add))
                chain(vector.tensor_scalar(tiles[:, :], tiles_i[:, :], 1.0, None, ALU.max))
                chain(vector.tensor_tensor_scan(end[:, :], G.const("ones")[:, 0:E], tiles[:, :], 0.0, ALU.mult, ALU.add))
                chain(vector.tensor_tensor(first[:, :], end[:, :], tiles[:, :], ALU.subtract))
                chain(vector.tensor_copy(rt.bounds[:, n, 0, :], first[:, :]))
                chain(vector.tensor_copy(rt.bounds[:, n, 1, :], end[:, :]))
                chain(vector.tensor_tensor(running[:, :, :], running[:, :, :], tile_sum[:, :, :], ALU.subtract))
                chain(vector.tensor_tensor(rank[:, :, :], within, running[:, :, :].rearrange("p e t -> p t e"), ALU.add))
                if capacity:
                    for k in ks:
                        chain(vector.tensor_tensor(picked[:, :, :], rank[:, :, :], chosen[:, k, :, :], ALU.mult))
                        chain(vector.tensor_reduce(keep[:, :], picked[:, :, :], AX.X, ALU.add))
                        chain(vector.tensor_scalar(keep[:, :], keep[:, :], float(capacity), None, ALU.is_lt))
                        chain(vector.tensor_tensor(rt.share[:, k, :], rt.share[:, k, :], keep[:, :], ALU.mult))
                chain(vector.tensor_scalar(first[:, :], first[:, :], float(R), None, ALU.mult))
                chain(vector.tensor_tensor(rank[:, :, :], rank[:, :, :],
                                           first[:, :].unsqueeze(1).to_broadcast([P, NT, E]), ALU.add))
                for k in ks:
                    chain(vector.tensor_tensor(picked[:, :, :], rank[:, :, :], chosen[:, k, :, :], ALU.mult))
                    chain(vector.tensor_reduce(slot_f[:, :], picked[:, :, :], AX.X, ALU.add))
                    chain(vector.tensor_copy(rt.slots[:, k, :], slot_f[:, :]))
                if n == 0:
                    vector.tensor_scalar(total[:, :], total[:, :], 1.0, None, ALU.mult).then_inc(slots_ready, 1)


def experts_block(nc, G, name, rt, n, weights, biases):
    GLU = len(weights) == 3
    UP = len(weights) - 1
    WB = 3
    HALVES = ((0, 1), (2, 3))
    PS = G.PS
    with ExitStack() as ctx:
        sb = lambda m, shape, dt=F32: ctx.enter_context(nc.sbuf_tensor(name + m, shape, dt))
        sem = semaphores(nc, ctx, name)
        up = [[sb(f"up{q}{i}", [P, DC, H]) for i in range(UP)] for q in range(WB)]
        down = [sb(f"down{q}", [P, HC, D]) for q in range(WB)]
        b1, b2 = sb("b1", [P, E, HC]), sb("b2", [P, E, D])
        xt, xT = sb("xt", [P, D]), sb("xT", [P, DC, R])
        hT, gate = sb("hT", [P, HC, R]), sb("gate", [P, HC, R])
        y = sb("y", [P, D])
        biases_landed, x_landed = sem("biases_landed"), sem("x_landed")
        weights_landed = [sem(f"weights{q}_landed") for q in range(WB)]
        stored = sem("stored")
        xT_done, xT_ready = sem("xT_done"), sem("xT_ready")
        h_done = sem("h_done")
        hT_ready = [sem("hT0_ready"), sem("hT1_ready")]
        y_done, y_ready = sem("y_done"), sem("y_ready")
        gate_ready, gated = sem("gate_ready"), sem("gated")
        ps_t, ps_y, ps_h = PS[0], PS[1], [PS[2], PS[3]]
        block = ctx.enter_context(nc.Block())

        def each_expert(eng, body):
            ends = [eng.value_load(rt.bounds[0:1, n, 1, e:e + 1], min_val=0, max_val=TILES) for e in range(E)]
            for e in range(E):
                body(e, ends[e - 1] if e else 0, ends[e])
            return ends[-1]

        @block.sync
        def _(sync):
            prime(sync, x_landed)

            def load(j):
                sync.dma_start(xt[:, :], G.rows[bass.ds(j * R, R), :]).then_inc(x_landed, 16)

            load(0)
            if biases is not None:
                sync.dma_start(b1[:, :, :].rearrange("p e c -> p (e c)"), biases[0]).then_inc(biases_landed, 16)
                sync.dma_start(b2[:, :, :].rearrange("p e d -> p (e d)"), biases[1]).then_inc(biases_landed, 16)
            count = sync.value_load(rt.bounds[0:1, n, 1, E - 1:E], min_val=0, max_val=TILES)
            with sync.Fori(0, count) as j:
                sync.wait_ge(xT_done, PRIMED + j + 1)
                load(j + 1)

        @block.scalar
        def _(act):
            prime(act, gate_ready, stored)
            if not GLU:
                prime(act, hT_ready[0])

            def load(e):
                q = e % WB
                for i in reversed(range(UP)):
                    act.dma_start(up[q][i][:, :, :], weights[i][e].rearrange("(c p) n -> p c n", p=P)).then_inc(weights_landed[q], 16)
                act.dma_start(down[q][:, :, :], weights[UP][e].rearrange("(c p) n -> p c n", p=P)).then_inc(weights_landed[q], 16)

            for e in range(WB - 1):
                load(e)
            if not GLU:
                act.wait_ge(biases_landed, 32)

            def expert(e, lo, hi):
                if e + WB - 1 < E:
                    if e:
                        act.wait_ge(y_done, PRIMED + lo)
                    load(e + WB - 1)
                with act.Fori(lo, hi) as j:
                    act.wait_ge(h_done, PRIMED + 2 * j + 1)
                    if GLU:
                        act.wait_ge(gated, PRIMED + j)
                        act.activation(gate[:, :, :].rearrange("p c r -> p (c r)"), ps_h[1][:, :],
                                       ACT.Sigmoid).then_inc(gate_ready, 1)
                    else:
                        for m in HALVES[0]:
                            ins = act.activation(hT[:, m, :], ps_h[0][:, m * R:(m + 1) * R], ACT.Relu,
                                                 bias=b1[:, e, m:m + 1])
                        ins.then_inc(hT_ready[0], 1)
                    act.wait_ge(y_ready, PRIMED + j + 1)
                    act.dma_start(G.rows[bass.ds(j * R, R), :], y[:, :]).then_inc(stored, 16)

            each_expert(act, expert)

        @block.vector
        def _(vector):
            prime(vector, xT_ready, hT_ready[1], y_ready, gated)
            if GLU:
                prime(vector, hT_ready[0])
            else:
                vector.wait_ge(biases_landed, 32)

            def xT_of(j):
                vector.wait_ge(xT_done, PRIMED + j + 1)
                vector.wait_ge(h_done, PRIMED + 2 * j)
                vector.tensor_copy(xT[:, :, :].rearrange("p c r -> p (c r)"), ps_t[:, 0:D]).then_inc(xT_ready, 1)

            xT_of(0)

            def expert(e, lo, hi):
                with vector.Fori(lo, hi) as j:
                    if GLU:
                        flat = lambda a: a[:, :, :].rearrange("p c r -> p (c r)")
                        vector.wait_ge(gate_ready, PRIMED + j + 1)
                        vector.wait_ge(y_done, PRIMED + j)
                        vector.tensor_tensor(flat(hT), ps_h[1][:, :], flat(gate), ALU.mult).then_inc(gated, 1)
                        vector.wait_ge(gated, PRIMED + j + 1)
                        vector.wait_ge(h_done, PRIMED + 2 * j + 2)
                        for i, (m, _) in enumerate(HALVES):
                            part = flat(hT)[:, m * R:(m + 2) * R]
                            vector.tensor_tensor(part, ps_h[0][:, m * R:(m + 2) * R], part, ALU.mult).then_inc(hT_ready[i], 1)
                    else:
                        vector.wait_ge(h_done, PRIMED + 2 * j + 2)
                        for m in HALVES[1]:
                            ins = vector.tensor_scalar(hT[:, m, :], ps_h[1][:, (m - 2) * R:(m - 1) * R],
                                                       b1[:, e, m:m + 1], 0.0, ALU.add, ALU.max)
                        ins.then_inc(hT_ready[1], 1)
                    xT_of(j + 1)
                    vector.wait_ge(y_done, PRIMED + j + 1)
                    vector.wait_ge(stored, PRIMED + 16 * j)
                    if biases is None:
                        vector.tensor_copy(y[:, :], ps_y[:, 0:D]).then_inc(y_ready, 1)
                    else:
                        vector.tensor_tensor(y[:, :], ps_y[:, 0:D], b2[:, e, :], ALU.add).then_inc(y_ready, 1)

            count = each_expert(vector, expert)
            vector.wait_ge(stored, PRIMED + 16 * count)
            vector.memset(y[:, 0:1], 0.0)

        @block.tensor
        def _(pe):
            prime(pe, xT_done, h_done, y_done)

            def transposes(j):
                pe.wait_ge(x_landed, PRIMED + 16 * j + 16)
                pe.wait_ge(xT_ready, PRIMED + j)
                for c in range(DC):
                    ins = pe.transpose(ps_t[:, c * R:(c + 1) * R], xt[:, c * P:(c + 1) * P], G.const("ident"))
                ins.then_inc(xT_done, 1)

            transposes(0)

            def expert(e, lo, hi):
                q = e % WB
                pe.wait_ge(weights_landed[q], 16 * (UP + 1) * (e // WB + 1))
                with pe.Fori(lo, hi) as j:
                    pe.wait_ge(xT_ready, PRIMED + j + 1)
                    for half in hT_ready:
                        pe.wait_ge(half, PRIMED + j)
                    for i in reversed(range(UP)):
                        for m in range(HC):
                            to = ps_h[i][:, m * R:(m + 1) * R] if GLU else ps_h[m // 2][:, m % 2 * R:(m % 2 + 1) * R]
                            for c in range(DC):
                                ins = pe.matmul(to, up[q][i][:, c, m * P:(m + 1) * P],
                                                xT[:, c, :], start=c == 0, stop=c == DC - 1)
                            if GLU and m == HC - 1 or not GLU and m % 2:
                                ins.then_inc(h_done, 1)
                    transposes(j + 1)
                    pe.wait_ge(y_ready, PRIMED + j)
                    for i, half in enumerate(HALVES):
                        pe.wait_ge(hT_ready[i], PRIMED + j + 1)
                        for m in half:
                            ins = pe.matmul(ps_y[:, 0:D], hT[:, m, :], down[q][:, m, :], start=m == 0, stop=m == HC - 1)
                    ins.then_inc(y_done, 1)

            each_expert(pe, expert)


def combine_block(nc, G, name, rt):
    with ExitStack() as ctx:
        sem = semaphores(nc, ctx, name)
        gathered = [sem(f"gathered{t}") for t in range(4)]
        added = sem("added")
        block = ctx.enter_context(nc.Block())

        @block.gpsimd
        def _(pool):
            for t in range(NT):
                for k in range(2):
                    pool.indirect_dma_start(rt.took[k][:, t, :], None, G.rows[:, :],
                                            bass.IndirectOffsetOnAxis(rt.slots[:, k, t:t + 1], 0)
                                            ).then_inc(gathered[t % 4], 16)
                if t >= 3:
                    pool.wait_ge(gathered[(t - 3) % 4], 32 * ((t - 3) // 4 + 1))

        @block.vector
        def _(vector):
            for k in range(2):
                for t in range(NT):
                    if k == 0:
                        vector.wait_ge(gathered[t % 4], 32 * (t // 4 + 1))
                    else:
                        vector.wait_ge(added, t + 1)
                    ins = vector.scalar_tensor_tensor(out=G.X[:, t, :], in0=rt.took[k][:, t, :],
                                                      scalar=rt.share[:, k, t:t + 1], in1=G.X[:, t, :],
                                                      op0=ALU.mult, op1=ALU.add)
                    if k == 0:
                        ins.then_inc(added, 1)


def l0_ffn(nc, G, a):
    with ExitStack() as ctx:
        rt = Routing(nc, ctx, "f0_")
        router_block(nc, G, "f0r_", rt, a["w_route0"], a["b_route0"], joint=True, over_all=True, capacity=None)
        experts_block(nc, G, "f0e_", rt, 0, (a["W1_0"], a["W2_0"]), (a["b1_0"], a["b2_0"]))
        combine_block(nc, G, "f0c_", rt)


def l3_ffn(nc, G, a):
    with ExitStack() as ctx:
        rt = Routing(nc, ctx, "f3_")
        router_block(nc, G, "f3r_", rt, a["w_route3"], a["b_route3"], joint=True, over_all=False, capacity=CAPACITY)
        experts_block(nc, G, "f3e_", rt, 0, (a["W_3"], a["V_3"], a["Wout_3"]), None)
        combine_block(nc, G, "f3c_", rt)


def boost_block(nc, G, name, rt):
    with ExitStack() as ctx:
        sem = semaphores(nc, ctx, name)
        gathered = [sem(f"gathered{t}") for t in range(4)]
        boosted, scattered = sem("boosted"), sem("scattered")
        block = ctx.enter_context(nc.Block())

        @block.gpsimd
        def _(pool):
            def scatter(t):
                pool.wait_ge(boosted, t + 1)
                pool.indirect_dma_start(G.rows[:, :], bass.IndirectOffsetOnAxis(rt.slots[:, 1, t:t + 1], 0),
                                        rt.took[1][:, t, :], None).then_inc(scattered, 16)

            for t in range(NT):
                pool.indirect_dma_start(rt.took[0][:, t, :], None, G.rows[:, :],
                                        bass.IndirectOffsetOnAxis(rt.slots[:, 0, t:t + 1], 0)
                                        ).then_inc(gathered[t % 4], 16)
                if t >= 3:
                    pool.wait_ge(gathered[(t - 3) % 4], 16 * ((t - 3) // 4 + 1))
            for i in range(4):
                pool.wait_ge(gathered[i], 16 * (NT // 4))
            for t in range(NT):
                scatter(t)
            pool.wait_ge(scattered, 16 * NT)

        @block.vector
        def _(vector):
            for t in range(NT):
                vector.wait_ge(gathered[t % 4], 16 * (t // 4 + 1))
                vector.scalar_tensor_tensor(out=rt.took[1][:, t, :], in0=rt.took[0][:, t, :], scalar=0.5,
                                            in1=rt.xn[:, t, :], op0=ALU.mult, op1=ALU.add).then_inc(boosted, 1)


def fuse_block(nc, G, name, rt, affine):
    X = G.X
    with ExitStack() as ctx:
        sb = lambda m, shape, dt=F32: ctx.enter_context(nc.sbuf_tensor(name + m, shape, dt))
        sem = semaphores(nc, ctx, name)
        gamma_beta = sb("gamma_beta", [P, 2, D])
        stats, moments = sb("stats", [P, NT, 6]), sb("moments", [P, NT, 2])
        var_eps, rstd = sb("var_eps", [P, NT]), sb("rstd", [P, NT])
        gathered = [sem(f"gathered{t}") for t in range(4)]
        landed, first_added, both_added = sem("landed"), sem("first_added"), sem("both_added")
        stats_done, var_ready, rstd_ready = sem("stats_done"), sem("var_ready"), sem("rstd_ready")
        normed, scaled, moved = sem("normed"), sem("scaled"), sem("moved")
        block = ctx.enter_context(nc.Block())

        @block.sync
        def _(sync):
            sync.dma_start(gamma_beta[:, :, :].rearrange("p i d -> p (i d)"), affine).then_inc(landed, 16)

        @block.gpsimd
        def _(pool):
            for t in range(NT):
                pool.indirect_dma_start(rt.took[1][:, t, :], None, G.rows[:, :],
                                        bass.IndirectOffsetOnAxis(rt.slots[:, 1, t:t + 1], 0)
                                        ).then_inc(gathered[t % 4], 16)
                if t >= 3:
                    pool.wait_ge(gathered[(t - 3) % 4], 16 * ((t - 3) // 4 + 1))
            layer_norm_root(pool, G, rstd, var_eps, var_ready, rstd_ready)
            pool.wait_ge(landed, 16)
            for t in range(NT):
                pool.wait_ge(normed, t + 1)
                pool.tensor_tensor(rt.took[0][:, t, :], rt.took[0][:, t, :], gamma_beta[:, 0, :], ALU.mult).then_inc(scaled, 1)
                pool.wait_ge(scaled, t + 1)
                pool.tensor_tensor(rt.took[0][:, t, :], rt.took[0][:, t, :], gamma_beta[:, 1, :], ALU.add).then_inc(moved, 1)

        @block.vector
        def _(vector):
            for t in range(NT):
                vector.scalar_tensor_tensor(out=rt.xn[:, t, :], in0=rt.took[0][:, t, :], scalar=rt.share[:, 0, t:t + 1],
                                            in1=rt.xn[:, t, :], op0=ALU.mult, op1=ALU.add).then_inc(first_added, 1)
            for t in range(NT):
                vector.wait_ge(first_added, t + 1)
                vector.wait_ge(gathered[t % 4], 16 * (t // 4 + 1))
                vector.scalar_tensor_tensor(out=rt.xn[:, t, :], in0=rt.took[1][:, t, :], scalar=rt.share[:, 1, t:t + 1],
                                            in1=rt.xn[:, t, :], op0=ALU.mult, op1=ALU.add).then_inc(both_added, 1)
            vector.wait_ge(both_added, NT)
            layer_norm_stats(vector, rt.xn, stats, moments, var_eps, stats_done, var_ready)
            vector.wait_ge(rstd_ready, 1)
            for t in range(NT):
                vector.tensor_scalar(rt.took[0][:, t, :], rt.xn[:, t, :], moments[:, t, 0:1], rstd[:, t:t + 1],
                                     ALU.subtract, ALU.mult).then_inc(normed, 1)
            for t in range(NT):
                vector.wait_ge(moved, t + 1)
                vector.tensor_tensor(X[:, t, :], X[:, t, :], rt.took[0][:, t, :], ALU.add)


def l1_ffn(nc, G, a):
    with ExitStack() as ctx:
        rt = Routing(nc, ctx, "f1_")
        w, b = (a["W1_1"], a["W2_1"]), (a["b1_1"], a["b2_1"])
        router_block(nc, G, "f1r_", rt, a["w_route1"], a["b_route1"], joint=False, over_all=True, capacity=None)
        experts_block(nc, G, "f1e0_", rt, 0, w, b)
        boost_block(nc, G, "f1b_", rt)
        experts_block(nc, G, "f1e1_", rt, 1, w, b)
        fuse_block(nc, G, "f1c_", rt, a["affine1"])


MASK_FILL = 2.3819763e38


def l0_attention(nc, G, a):
    HEADS, DH = 4, 64
    PAIRS = HEADS // 2
    GB = TPB * PAIRS
    PVN = 96
    RMS_EPS = 1e-6
    X, PS, name = G.X, G.PS, "a0_"
    with ExitStack() as ctx:
        sb = lambda n, shape, dt=F32: ctx.enter_context(nc.sbuf_tensor(name + n, shape, dt))
        sem = semaphores(nc, ctx, name)
        w, wk, wv = sb("w", [P, 3, DC, D]), sb("wk", [P, 2, DC, P]), sb("wv", [P, DC, DH])
        gain = sb("gain", [P, DC])
        context = sb("context", [P, NT, D])
        kept_u8 = sb("kept_u8", [P, B, S], U8)
        kept, fill = sb("kept", [P, B, S]), sb("fill", [P, B, S])
        stats, moments = sb("stats", [P, NT, 6]), sb("moments", [P, NT, 2])
        c_stats, c_moments = sb("c_stats", [P, NT, 6]), sb("c_moments", [P, NT, 2])
        var_eps, c_sq = sb("var_eps", [P, NT]), sb("c_sq", [P, NT])
        rstd, xf, cf = sb("rstd", [P, NT]), sb("xf", [P, NT]), sb("cf", [P, NT])
        xn, cn = sb("xn", [P, TPB, D]), sb("cn", [P, TPB, D])
        xnT, cnT = sb("xnT", [P, DC, S]), sb("cnT", [P, DC, S])
        turn = sb("turn", [P, 2, DC, S])
        qT, kT, kTm = sb("qT", [P, DC, S]), sb("kT", [P, S]), sb("kTm", [P, 2, S])
        vaug = sb("vaug", [P, TPB, PVN])
        masked = sb("masked", [P, 2, 2, S])
        nmax = sb("nmax", [P, 2, 2])
        prob, probT = sb("prob", [P, 2, 2, S]), sb("probT", [P, 2, 4, P])
        rsum = sb("rsum", [P, TPB, HEADS])
        enc, encT = sb("enc", [P, TPB, D]), sb("encT", [P, DC, S])
        landed, gain_ready, scaled, ones_ready = sem("landed"), sem("gain_ready"), sem("scaled"), sem("ones_ready")
        stats_done, c_stats_done, var_ready, c_var_ready = sem("stats_done"), sem("c_stats_done"), sem("var_ready"), sem("c_var_ready")
        c_sq_ready, root_s, root_ready = sem("c_sq_ready"), sem("root_steps"), sem("root_ready")
        kept_ready, fill_ready = sem("kept_ready"), sem("fill_ready")
        chain_s, xn_ready, xT_done, xnT_ready = sem("chain"), sem("xn_ready"), sem("xT_done"), sem("xnT_ready")
        q_done, q_ready, k_done, k_ready = sem("q_done"), sem("q_ready"), sem("k_done"), sem("k_ready")
        v_done, v_ready = sem("v_done"), sem("v_ready")
        score_done, max_ready, prob_ready = sem("score_done"), sem("max_ready"), sem("prob_ready")
        probT_done, probT_ready, pv_done = sem("probT_done"), sem("probT_ready"), sem("pv_done")
        enc_ready, encT_done, encT_ready = sem("enc_ready"), sem("encT_done"), sem("encT_ready")
        out_done, added = sem("out_done"), sem("added")
        ps_x, ps_q, ps_s, ps_t, ps_o = PS[0], PS[1], [PS[2], PS[3]], [PS[4], PS[5]], [PS[6], PS[7]]
        LOADS = 9
        block = ctx.enter_context(nc.Block())

        @block.sync
        def _(sync):
            sync.dma_start(context[:, :, :], a["ctx"].rearrange("b (k p) d -> p (b k) d", p=P)).then_inc(landed, 16)
            sync.dma_start(gain[:, :], a["gain_att0"]).then_inc(landed, 16)
            for i in range(3):
                sync.dma_start(w[:, i, :, :], a["w_att0"][i].rearrange("(c p) n -> p c n", p=P)).then_inc(landed, 16)
            for i in range(2):
                sync.dma_start(wk[:, i, :, :], a["wk_att0"][i].rearrange("(c p) n -> p c n", p=P)).then_inc(landed, 16)
            sync.dma_start(wv[:, :, :], a["wv_att0"].rearrange("(c p) n -> p c n", p=P)).then_inc(landed, 16)
            sync.dma_start(kept_u8[:, :, :].rearrange("p b s -> p (b s)"), a["kept"].to_broadcast([P, B * S])).then_inc(landed, 16)

        @block.gpsimd
        def _(pool):
            step = Chain(pool, root_s)
            half = G.mhalf(NT)
            pool.wait_ge(c_sq_ready, 1)
            step(pool.tensor_tensor(cf[:, :], c_sq[:, :], half, ALU.pow))
            pool.wait_ge(var_ready, 1)
            step(pool.tensor_tensor(rstd[:, :], var_eps[:, :], half, ALU.pow))
            step(pool.tensor_tensor(xf[:, :], rstd[:, :], rstd[:, :], ALU.mult))
            step(pool.tensor_tensor(xf[:, :], xf[:, :], moments[:, :, 1], ALU.mult))
            step(pool.tensor_scalar(xf[:, :], xf[:, :], RMS_EPS, None, ALU.add))
            step(pool.tensor_tensor(xf[:, :], xf[:, :], half, ALU.pow))
            pool.tensor_tensor(xf[:, :], xf[:, :], rstd[:, :], ALU.mult).then_inc(root_ready, 1)
            pool.wait_ge(landed, 16 * LOADS)
            pool.tensor_copy(kept[:, :, :], kept_u8[:, :, :]).then_inc(kept_ready, 1)
            pool.wait_ge(kept_ready, 1)
            pool.tensor_scalar(fill[:, :, :], kept[:, :, :], -MASK_FILL, MASK_FILL, ALU.mult, ALU.add).then_inc(fill_ready, 1)

        @block.scalar
        def _(act):
            prime(act, xnT_ready, v_ready, prob_ready)
            with act.Fori(0, B) as b:
                act.wait_ge(xT_done, PRIMED + b + 1)
                act.wait_ge(v_done, PRIMED + b)
                act.copy(xnT[:, :, :].rearrange("p c s -> p (c s)"), ps_x[:, :])
                act.copy(cnT[:, :, :].rearrange("p c s -> p (c s)"), ps_q[:, :]).then_inc(xnT_ready, 1)
                act.wait_ge(v_done, PRIMED + b + 1)
                act.wait_ge(pv_done, PRIMED + GB * b)
                act.wait_ge(ones_ready, 1)
                act.copy(vaug[:, :, 0:DH], ps_x[:, 0:TPB * DH].rearrange("p (k v) -> p k v", v=DH)).then_inc(v_ready, 1)
                for g in range(GB):
                    act.wait_ge(max_ready, PRIMED + GB * b + g + 1)
                    act.wait_ge(probT_done, PRIMED + GB * b + max(g - 1, 0))
                    for i in range(2):
                        ins = act.activation(prob[:, g % 2, i, :], masked[:, g % 2, i, :], ACT.Exp,
                                             bias=nmax[:, g % 2, i:i + 1], scale=-1.0)
                    ins.then_inc(prob_ready, 1)

        @block.vector
        def _(vector):
            prime(vector, chain_s, xn_ready, q_ready, k_ready, max_ready, probT_ready, enc_ready, encT_ready, added)
            vector.memset(vaug[:, :, :], 1.0).then_inc(ones_ready, 1)
            vector.wait_ge(landed, 16 * LOADS)
            vector.tensor_scalar(gain[:, :], gain[:, :], 1.0, None, ALU.add).then_inc(gain_ready, 1)
            layer_norm_stats(vector, context, c_stats, c_moments, c_sq, c_stats_done, c_var_ready, RMS_EPS)
            vector.wait_ge(gain_ready, 1)
            for c in range(DC):
                for part in (w[:, 0:2, c, :], wk[:, :, c, :], wv[:, c, :]):
                    ins = vector.tensor_scalar(part, part, gain[:, c:c + 1], None, ALU.mult)
            ins.then_inc(scaled, 1)
            vector.wait_ge(c_var_ready, 1)
            vector.tensor_tensor(cf[:, :], c_moments[:, :, 0], c_moments[:, :, 0], ALU.mult).then_inc(c_var_ready, 1)
            vector.wait_ge(c_var_ready, 2)
            vector.tensor_tensor(c_sq[:, :], c_sq[:, :], cf[:, :], ALU.add).then_inc(c_sq_ready, 1)
            layer_norm_stats(vector, X, stats, moments, var_eps, stats_done, var_ready)
            vector.wait_ge(root_ready, 1)
            vector.wait_ge(fill_ready, 1)
            CH = 11 + 2 * GB
            with vector.Fori(0, B) as b:
                chain = Chain(vector, chain_s, PRIMED + b * CH)
                vector.wait_ge(xT_done, PRIMED + b)
                for k in range(TPB):
                    t = TPB * b + k
                    vector.tensor_scalar(xn[:, k, :], X[:, t, :], moments[:, t, 0:1], xf[:, bass.ds(t, 1)],
                                         ALU.subtract, ALU.mult)
                    ins = vector.tensor_scalar(cn[:, k, :], context[:, t, :], cf[:, bass.ds(t, 1)], None, ALU.mult)
                ins.then_inc(xn_ready, 1)
                vector.wait_ge(q_done, PRIMED + b + 1)
                halves = lambda ps: ps[:, :].rearrange("p (c s) -> p c s", s=S)
                table = lambda n: G.const(n).unsqueeze(1).to_broadcast([P, DC, S])
                chain(vector.tensor_tensor(turn[:, 0, :, :], halves(ps_x), table("cosq"), ALU.mult))
                chain(vector.tensor_tensor(turn[:, 1, :, :], halves(ps_t[0]), table("sinq"), ALU.mult))
                vector.wait_ge(score_done, PRIMED + GB * b)
                chain(vector.tensor_tensor(qT[:, :, :], turn[:, 0, :, :], turn[:, 1, :, :], ALU.add))
                vector.sem_inc(q_ready, 1)
                vector.wait_ge(k_done, PRIMED + b + 1)
                chain(vector.tensor_tensor(turn[:, 0, 0, :], ps_t[1][:, 0:S], G.const("cosk"), ALU.mult))
                chain(vector.tensor_tensor(turn[:, 1, 0, :], ps_t[1][:, S:2 * S], G.const("sink"), ALU.mult))
                chain(vector.tensor_tensor(kT[:, :], turn[:, 0, 0, :], turn[:, 1, 0, :], ALU.add))
                for i, rows in enumerate(("even", "odd")):
                    ins = vector.tensor_scalar(kTm[:, i, :], kT[:, :], G.const(rows), None, ALU.mult)
                ins.then_inc(k_ready, 1)

                def max_of(g):
                    vector.wait_ge(score_done, PRIMED + GB * b + g + 1)
                    vector.wait_ge(prob_ready, PRIMED + GB * b + max(g - 1, 0))
                    m = masked[:, g % 2, :, :]
                    rows = lambda a: a[:, bass.ds(b, 1), :].to_broadcast([P, 2, S])
                    chain(vector.tensor_tensor(m, ps_s[g % 2][:, :].rearrange("p (h s) -> p h s", s=S), rows(kept), ALU.mult))
                    chain(vector.tensor_tensor(m, m, rows(fill), ALU.add))
                    vector.tensor_reduce(nmax[:, g % 2, :], m, AX.X, ALU.min).then_inc(max_ready, 1)

                def probT_of(g):
                    vector.wait_ge(probT_done, PRIMED + GB * b + g + 1)
                    vector.wait_ge(pv_done, PRIMED + GB * b + max(g - 1, 0))
                    vector.tensor_copy(probT[:, g % 2, :, :].rearrange("p a t -> p (a t)"),
                                       ps_t[g % 2][:, :]).then_inc(probT_ready, 1)

                def enc_of(k):
                    vector.wait_ge(pv_done, PRIMED + GB * b + PAIRS * (k + 1))
                    o = ps_o[k][:, 0:HEADS * PVN].rearrange("p (h v) -> p h v", v=PVN)
                    chain(vector.reciprocal(rsum[:, k, :], o[:, :, DH]))
                    vector.wait_ge(encT_done, PRIMED + b)
                    vector.tensor_tensor(enc[:, k, :].rearrange("p (h v) -> p h v", v=DH), o[:, :, 0:DH],
                                         bcast(rsum[:, k, :], DH), ALU.mult).then_inc(enc_ready, 1)

                for g in range(GB):
                    max_of(g)
                    if g >= 1:
                        probT_of(g - 1)
                    if g == PAIRS + 1:
                        enc_of(0)
                probT_of(GB - 1)
                enc_of(1)
                vector.wait_ge(encT_done, PRIMED + b + 1)
                vector.wait_ge(out_done, PRIMED + b)
                chain(vector.tensor_copy(encT[:, :, :].rearrange("p c s -> p (c s)"), ps_x[:, :]))
                vector.sem_inc(encT_ready, 1)
                vector.wait_ge(out_done, PRIMED + b + 1)
                x = X[:, bass.ds(TPB * b, TPB), :]
                chain(vector.tensor_tensor(x, ps_q[:, :].rearrange("p (k d) -> p k d", d=D), x, ALU.add))
                vector.sem_inc(added, 1)
                assert chain.n <= CH
                for _ in range(CH - chain.n):
                    vector.sem_inc(chain_s, 1)

        @block.tensor
        def _(pe):
            prime(pe, xT_done, q_done, k_done, v_done, score_done, probT_done, pv_done, encT_done, out_done)
            ident = G.const("ident")
            pe.wait_ge(landed, 16 * LOADS)
            pe.wait_ge(scaled, 1)
            with pe.Fori(0, B) as b:
                pe.wait_ge(xn_ready, PRIMED + b + 1)
                pe.wait_ge(added, PRIMED + b)
                for source, to in ((xn, ps_x), (cn, ps_q)):
                    for c in range(DC):
                        for k in range(TPB):
                            ins = pe.transpose(to[:, c * S + k * P:c * S + (k + 1) * P],
                                               source[:, k, c * P:(c + 1) * P], ident)
                ins.then_inc(xT_done, 1)
                pe.wait_ge(xnT_ready, PRIMED + b + 1)
                pe.wait_ge(probT_ready, PRIMED + GB * b)
                for i, to in ((0, ps_x), (1, ps_t[0])):
                    for m in range(DC):
                        for c in range(DC):
                            ins = pe.matmul(to[:, m * S:(m + 1) * S], w[:, i, c, m * P:(m + 1) * P], xnT[:, c, :],
                                            start=c == 0, stop=c == DC - 1)
                ins.then_inc(q_done, 1)
                for i in range(2):
                    for c in range(DC):
                        ins = pe.matmul(ps_t[1][:, i * S:(i + 1) * S], wk[:, i, c, :], cnT[:, c, :],
                                        start=c == 0, stop=c == DC - 1)
                ins.then_inc(k_done, 1)
                pe.wait_ge(q_ready, PRIMED + b + 1)
                for k in range(TPB):
                    for c in range(DC):
                        ins = pe.matmul(ps_x[:, k * DH:(k + 1) * DH], cnT[:, c, k * P:(k + 1) * P], wv[:, c, :],
                                        start=c == 0, stop=c == DC - 1)
                ins.then_inc(v_done, 1)

                def scores(g):
                    k, j = divmod(g, PAIRS)
                    if g == 0:
                        pe.wait_ge(k_ready, PRIMED + b + 1)
                    pe.wait_ge(max_ready, PRIMED + GB * b + max(g - 1, 0))
                    pe.matmul(ps_s[g % 2][:, :], qT[:, j, k * P:(k + 1) * P], kTm[:, :, :],
                              start=True, stop=True).then_inc(score_done, 1)

                def transposes(g):
                    pe.wait_ge(prob_ready, PRIMED + GB * b + g + 1)
                    pe.wait_ge(probT_ready, PRIMED + GB * b + max(g - 1, 0))
                    for i in range(2):
                        for c in range(TPB):
                            ins = pe.transpose(ps_t[g % 2][:, (2 * i + c) * P:(2 * i + c + 1) * P],
                                               prob[:, g % 2, i, c * P:(c + 1) * P], ident)
                    ins.then_inc(probT_done, 1)

                def values(g):
                    k, j = divmod(g, PAIRS)
                    pe.wait_ge(probT_ready, PRIMED + GB * b + g + 1)
                    for i in range(2):
                        at = (2 * j + i) * PVN
                        for c in range(TPB):
                            ins = pe.matmul(ps_o[k][:, at:at + PVN], probT[:, g % 2, 2 * i + c, :],
                                            vaug[:, c, :], start=c == 0, stop=c == TPB - 1)
                    ins.then_inc(pv_done, 1)

                scores(0)
                pe.wait_ge(v_ready, PRIMED + b + 1)
                pe.wait_ge(enc_ready, PRIMED + TPB * b)
                for g in range(GB):
                    if g + 1 < GB:
                        scores(g + 1)
                    transposes(g)
                    if g >= 1:
                        values(g - 1)
                values(GB - 1)
                pe.wait_ge(enc_ready, PRIMED + TPB * (b + 1))
                for c in range(DC):
                    for k in range(TPB):
                        ins = pe.transpose(ps_x[:, c * S + k * P:c * S + (k + 1) * P],
                                           enc[:, k, c * P:(c + 1) * P], ident)
                ins.then_inc(encT_done, 1)
                pe.wait_ge(encT_ready, PRIMED + b + 1)
                for k in range(TPB):
                    for c in range(DC):
                        ins = pe.matmul(ps_q[:, k * D:(k + 1) * D], encT[:, c, k * P:(k + 1) * P], w[:, 2, c, :],
                                        start=c == 0, stop=c == DC - 1)
                ins.then_inc(out_done, 1)


def l2_attention(nc, G, a):
    HEADS, DH = 4, 64
    VW = DH + 1
    PVN = 96
    VCOLS = (HEADS - 1) * VW + PVN
    X, PS, name = G.X, G.PS, "a2_"
    NEG = -3.0e38
    with ExitStack() as ctx:
        sb = lambda n, shape, dt=F32: ctx.enter_context(nc.sbuf_tensor(name + n, shape, dt))
        sem = semaphores(nc, ctx, name)
        gates_w = sb("gates_w", [P, 3, DC, 8])
        gate_bias = sb("gate_bias", [HEADS, 2])
        out_gain = sb("out_gain", [P, D])
        ctxT = sb("ctxT", [P, DC, S])
        stats, moments = sb("stats", [P, NT, 6]), sb("moments", [P, NT, 2])
        var_eps, rstd = sb("var_eps", [P, NT]), sb("rstd", [P, NT])
        xn, xnT = sb("xn", [P, TPB, D]), sb("xnT", [P, DC, S])
        qm = sb("qm", [P, HEADS, S])
        ig, z, soft = sb("ig", [HEADS, S]), sb("z", [HEADS, S]), sb("soft", [HEADS, S])
        forget, g = sb("forget", [HEADS, S]), sb("g", [HEADS, S])
        m_rows = sb("m_rows", [P, S])
        top = sb("top", [HEADS, S])
        cols = sb("cols", [P, 2, TPB, HEADS])
        vaug = sb("vaug", [P, TPB, VCOLS])
        expo, decay = sb("expo", [P, 2, S + P]), sb("decay", [P, 2, S + P])
        cT = sb("cT", [P, 2, S + P])
        norm = sb("norm", [P, TPB, HEADS])
        h = sb("h", [P, NT, D])
        h_stats, h_moments = sb("h_stats", [P, NT * HEADS, 6]), sb("h_moments", [P, NT * HEADS, 2])
        h_root = sb("h_root", [P, NT * HEADS])
        landed, ctx_landed, v_landed = sem("landed"), sem("ctx_landed"), sem("v_landed")
        stats_done, var_ready, rstd_ready = sem("stats_done"), sem("var_ready"), sem("rstd_ready")
        setup, chain_s, xn_ready = sem("setup"), sem("chain"), sem("xn_ready")
        xT_done, xnT_ready, qm_ready = sem("xT_done"), sem("xnT_ready"), sem("qm_ready")
        gates_done, abs_ready, soft_ready = sem("gates_done"), sem("abs_ready"), sem("soft_ready")
        act_chain, rows_ready = sem("act_chain"), sem("rows_ready")
        cols_done, spread_done, norm_exp_ready = sem("cols_done"), sem("spread_done"), sem("norm_exp_ready")
        v_ready = sem("v_ready")
        expo_ready, decay_ready, qk_done, cT_ready = sem("expo_ready"), sem("decay_ready"), sem("qk_done"), sem("cT_ready")
        masked_ready, pv_done, h_ready = sem("masked_ready"), sem("pv_done"), sem("h_ready")
        h_stats_done, h_var_ready, h_root_ready = sem("h_stats_done"), sem("h_var_ready"), sem("h_root_ready")
        tail_s, gates_summed = sem("tail"), sem("gates_summed")
        ps_x, ps_g, ps_c, ps_m, ps_qk = PS[0], PS[1], PS[2], [PS[3], PS[1]], [PS[4], PS[5]]
        ps_o = [PS[6], PS[7]]
        block = ctx.enter_context(nc.Block())

        @block.sync
        def _(sync):
            for i in range(3):
                sync.dma_start(gates_w[:, i, :, :], a["gates_2"][i].rearrange("(c p) n -> p c n", p=P)).then_inc(landed, 16)
            sync.dma_start(gate_bias[:, :], a["gate_bias_2"]).then_inc(landed, 16)
            sync.dma_start(out_gain[:, :], a["out_gain_2"]).then_inc(landed, 16)
            sync.wait_ge(setup, 2)
            with sync.Fori(0, B) as b:
                sync.wait_ge(qk_done, PRIMED + HEADS * b)
                sync.dma_start(ctxT[:, :, :], a["ctxT"][b].rearrange("(c p) n -> p c n", p=P)).then_inc(ctx_landed, 16)
                sync.wait_ge(pv_done, PRIMED + HEADS * b)
                for k in range(TPB):
                    sync.dma_start(vaug[:, k, 0:HEADS * VW].rearrange("p (h v) -> p h v", v=VW)[:, :, 0:DH],
                                   a["ctx"][b, k * P:(k + 1) * P, :].rearrange("p (h v) -> p h v", v=DH)).then_inc(v_landed, 16)

        @block.gpsimd
        def _(pool):
            prime(pool, masked_ready)
            layer_norm_root(pool, G, rstd, var_eps, var_ready, rstd_ready)
            with pool.Fori(0, B) as b:
                for n in range(HEADS):
                    pool.wait_ge(cT_ready, PRIMED + HEADS * b + n + 1)
                    for at in (0, S):
                        part = cT[:, n % 2, at:at + P]
                        ins = pool.tensor_tensor(part, part, G.const("upto"), ALU.mult)
                    ins.then_inc(masked_ready, 1)
            pool.wait_ge(h_var_ready, 1)
            pool.tensor_tensor(h_root[:, :], h_root[:, :], G.const("half")[:, 0:1].to_broadcast([P, NT * HEADS]),
                               ALU.pow).then_inc(h_root_ready, 1)

        @block.scalar
        def _(act):
            prime(act, xnT_ready, act_chain, soft_ready, norm_exp_ready, decay_ready)
            with act.Fori(0, B) as b:
                act.wait_ge(xT_done, PRIMED + b + 1)
                act.wait_ge(qm_ready, PRIMED + b)
                act.wait_ge(gates_done, PRIMED + b)
                act.copy(xnT[:, :, :].rearrange("p c s -> p (c s)"), ps_x[:, :]).then_inc(xnT_ready, 1)
                act.wait_ge(abs_ready, PRIMED + b + 1)
                step = Chain(act, act_chain, PRIMED + b)
                step(act.activation(soft[:, :], soft[:, :], ACT.Exp, scale=-1.0))
                act.activation(soft[:, :], soft[:, :], ACT.Ln, bias=1.0).then_inc(soft_ready, 1)
                act.wait_ge(cols_done, PRIMED + b + 1)
                act.wait_ge(h_ready, PRIMED + b)
                act.activation(cols[:, 1, :, :], ps_c[:, TPB * HEADS:2 * TPB * HEADS].rearrange("p (k n) -> p k n", n=HEADS),
                               ACT.Exp, scale=-1.0)
                act.copy(cols[:, 0, :, :], ps_c[:, 0:TPB * HEADS].rearrange("p (k n) -> p k n", n=HEADS)).then_inc(norm_exp_ready, 1)
                for n in range(HEADS):
                    act.wait_ge(expo_ready, PRIMED + HEADS * b + n + 1)
                    act.wait_ge(cT_ready, PRIMED + HEADS * b + max(n - 1, 0))
                    act.activation(decay[:, n % 2, :], expo[:, n % 2, :], ACT.Exp).then_inc(decay_ready, 1)

        @block.vector
        def _(vector):
            prime(vector, chain_s, xn_ready, qm_ready, abs_ready, rows_ready, expo_ready, cT_ready, h_ready)
            vector.memset(vaug[:, :, :], 1.0).then_inc(setup, 1)
            vector.memset(m_rows[:, :], 0.0).then_inc(setup, 1)
            vector.wait_ge(landed, 16 * 5)
            vector.tensor_tensor(gates_w[:, 1, :, :], gates_w[:, 1, :, :], gates_w[:, 2, :, :], ALU.add).then_inc(gates_summed, 1)
            layer_norm_stats(vector, X, stats, moments, var_eps, stats_done, var_ready)
            vector.wait_ge(rstd_ready, 1)
            CH = 17
            with vector.Fori(0, B) as b:
                chain = Chain(vector, chain_s, PRIMED + b * CH)
                vector.wait_ge(xT_done, PRIMED + b)
                for k in range(TPB):
                    ins = vector.tensor_scalar(xn[:, k, :], X[:, TPB * b + k, :], moments[:, TPB * b + k, 0:1],
                                               rstd[:, bass.ds(TPB * b + k, 1)], ALU.subtract, ALU.mult)
                ins.then_inc(xn_ready, 1)
                vector.wait_ge(xnT_ready, PRIMED + b + 1)
                vector.wait_ge(qk_done, PRIMED + HEADS * b)
                for n in range(HEADS):
                    ins = vector.tensor_scalar(qm[:, n, :], xnT[:, n // 2, :], G.const(("even", "odd")[n % 2]),
                                               DH ** -0.5, ALU.mult, ALU.mult)
                ins.then_inc(qm_ready, 1)
                vector.wait_ge(gates_done, PRIMED + b + 1)
                chain(vector.tensor_scalar(ig[:, :], ps_g[0:HEADS, 0:S], gate_bias[:, 0:1], None, ALU.add))
                chain(vector.tensor_scalar(z[:, :], ps_g[0:HEADS, S:2 * S], gate_bias[:, 1:2], None, ALU.add))
                vector.scalar_tensor_tensor(out=soft[:, :], in0=z[:, :], scalar=-1.0, in1=z[:, :], op0=ALU.mult,
                                            op1=ALU.max).then_inc(abs_ready, 1)
                vector.wait_ge(soft_ready, PRIMED + b + 1)
                chain(vector.tensor_scalar(z[:, :], z[:, :], 0.0, None, ALU.min))
                chain(vector.tensor_tensor(z[:, :], z[:, :], soft[:, :], ALU.subtract))
                ones = G.const("ones")[0:HEADS, 0:1].to_broadcast([HEADS, S])
                chain(vector.tensor_tensor_scan(forget[:, :], ones, z[:, :], 0.0, ALU.mult, ALU.add))
                vector.wait_ge(cols_done, PRIMED + b)
                chain(vector.tensor_tensor(g[:, :], ig[:, :], forget[:, :], ALU.subtract))
                vector.wait_ge(spread_done, PRIMED + HEADS * b)
                chain(vector.tensor_tensor_scan(m_rows[0:HEADS, :], ones, g[:, :], NEG, ALU.mult, ALU.max))
                vector.tensor_tensor(top[:, :], forget[:, :], m_rows[0:HEADS, :], ALU.add).then_inc(rows_ready, 1)
                vector.wait_ge(norm_exp_ready, PRIMED + b + 1)

                def expo_of(n):
                    vector.wait_ge(spread_done, PRIMED + HEADS * b + n + 1)
                    vector.wait_ge(decay_ready, PRIMED + HEADS * b + max(n - 1, 0))
                    for k, to, lo in ((0, 0, 0), (1, S, P)):
                        ins = vector.tensor_scalar(expo[:, n % 2, to:to + S - lo], ps_m[n % 2][:, lo:S], -1.0,
                                                   cols[:, 0, k, n:n + 1], ALU.mult, ALU.add)
                    chain(ins)
                    vector.tensor_scalar(expo[:, n % 2, :], expo[:, n % 2, :], 0.0, None, ALU.min).then_inc(expo_ready, 1)

                def cT_of(n):
                    vector.wait_ge(qk_done, PRIMED + HEADS * b + n + 1)
                    vector.wait_ge(decay_ready, PRIMED + HEADS * b + n + 1)
                    vector.wait_ge(pv_done, PRIMED + HEADS * b + max(n - 1, 0))
                    vector.tensor_tensor(cT[:, n % 2, :], ps_qk[n % 2][:, 0:S + P], decay[:, n % 2, :],
                                         ALU.mult).then_inc(cT_ready, 1)

                for n in range(HEADS):
                    expo_of(n)
                    if n:
                        cT_of(n - 1)
                cT_of(HEADS - 1)
                vector.wait_ge(pv_done, PRIMED + HEADS * (b + 1))
                heads = lambda k: ps_o[k][:, 0:HEADS * VW].rearrange("p (h v) -> p h v", v=VW)
                for k in range(TPB):
                    chain(vector.tensor_copy(norm[:, k, :], heads(k)[:, :, DH]))
                chain(vector.scalar_tensor_tensor(out=norm[:, :, :], in0=norm[:, :, :], scalar=-1.0, in1=norm[:, :, :],
                                                  op0=ALU.mult, op1=ALU.max))
                chain(vector.tensor_tensor(norm[:, :, :], norm[:, :, :], cols[:, 1, :, :], ALU.max))
                chain(vector.tensor_scalar(norm[:, :, :], norm[:, :, :], 1e-6, None, ALU.add))
                chain(vector.reciprocal(norm[:, :, :], norm[:, :, :]))
                for k in range(TPB):
                    ins = vector.tensor_tensor(h[:, bass.ds(TPB * b + k, 1), :].rearrange("p o (h v) -> p (o h) v", v=DH),
                                               heads(k)[:, :, 0:DH], bcast(norm[:, k, :], DH), ALU.mult)
                ins.then_inc(h_ready, 1)
                assert chain.n == CH
            by_head = lambda t: t[:, :, :].rearrange("p t (h v) -> p (t h) v", v=DH)
            vector.wait_ge(h_ready, PRIMED + B)
            for i in range(NT * HEADS):
                vector.bn_stats(h_stats[:, i, :], by_head(h)[:, i, :]).then_inc(h_stats_done, 1)
            for i in range(NT * HEADS):
                vector.wait_ge(h_stats_done, i + 1)
                vector.bn_aggr(h_moments[:, i, :], h_stats[:, i, :]).then_inc(h_stats_done, 1)
            vector.wait_ge(h_stats_done, 2 * NT * HEADS)
            vector.tensor_scalar(h_root[:, :], h_moments[:, :, 1], 1e-6, None, ALU.add).then_inc(h_var_ready, 1)
            tail = Chain(vector, tail_s)
            tail(vector.tensor_tensor(by_head(h), by_head(h), h_moments[:, :, 0:1].to_broadcast([P, NT * HEADS, DH]), ALU.subtract))
            vector.wait_ge(h_root_ready, 1)
            tail(vector.tensor_tensor(by_head(h), by_head(h), bcast(h_root[:, :], DH), ALU.mult))
            tail(vector.tensor_tensor(h[:, :, :], h[:, :, :], out_gain[:, :].unsqueeze(1).to_broadcast([P, NT, D]), ALU.mult))
            tail(vector.tensor_tensor(X[:, :, :], X[:, :, :], h[:, :, :], ALU.add))

        @block.tensor
        def _(pe):
            prime(pe, xT_done, gates_done, cols_done, spread_done, qk_done, pv_done)
            ident = G.const("ident")
            pe.wait_ge(landed, 16 * 5)
            pe.wait_ge(gates_summed, 1)
            pe.wait_ge(setup, 2)
            with pe.Fori(0, B) as b:
                pe.wait_ge(xn_ready, PRIMED + b + 1)
                for c in range(DC):
                    for k in range(TPB):
                        ins = pe.transpose(ps_x[:, c * S + k * P:c * S + (k + 1) * P],
                                           xn[:, k, c * P:(c + 1) * P], ident)
                ins.then_inc(xT_done, 1)
                pe.wait_ge(ctx_landed, 16 * (b + 1))
                pe.wait_ge(xnT_ready, PRIMED + b + 1)
                for gate in range(2):
                    for i, source in enumerate((xnT, ctxT)):
                        for c in range(DC):
                            ins = pe.matmul(ps_g[0:HEADS, gate * S:(gate + 1) * S],
                                            gates_w[:, i, c, gate * HEADS:(gate + 1) * HEADS], source[:, c, :],
                                            start=i == 0 and c == 0, stop=i == 1 and c == DC - 1)
                ins.then_inc(gates_done, 1)

                def qk(n):
                    pe.wait_ge(cT_ready, PRIMED + HEADS * b + max(n - 1, 0))
                    for k, to, lo in ((0, 0, 0), (1, S, P)):
                        ins = pe.matmul(ps_qk[n % 2][:, to:to + S - lo], ctxT[:, n // 2, k * P:(k + 1) * P],
                                        qm[:, n, lo:S], start=True, stop=True)
                    ins.then_inc(qk_done, 1)

                def spread(n):
                    pe.wait_ge(expo_ready, PRIMED + HEADS * b + max(n - 1, 0))
                    pe.matmul(ps_m[n % 2][:, 0:S], G.const("pick")[:, n * P:(n + 1) * P], m_rows[:, :],
                              start=True, stop=True).then_inc(spread_done, 1)

                def values(n):
                    pe.wait_ge(masked_ready, PRIMED + HEADS * b + n + 1)
                    at = n * VW
                    for k, c, lo in ((0, 0, 0), (1, 0, P), (1, 1, S)):
                        ins = pe.matmul(ps_o[k][:, at:at + PVN], cT[:, n % 2, lo:lo + P], vaug[:, c, at:at + PVN],
                                        start=c == 0, stop=c == k)
                    ins.then_inc(pv_done, 1)

                pe.wait_ge(qm_ready, PRIMED + b + 1)
                qk(0)
                pe.wait_ge(rows_ready, PRIMED + b + 1)
                pe.wait_ge(norm_exp_ready, PRIMED + b)
                spread(0)
                for i, rows in enumerate((g[:, :], top[:, :])):
                    for k in range(TPB):
                        at = (TPB * i + k) * HEADS
                        ins = pe.transpose(ps_c[:, at:at + HEADS], rows[:, k * P:(k + 1) * P],
                                           G.const("ident")[0:HEADS, 0:HEADS])
                ins.then_inc(cols_done, 1)
                pe.wait_ge(v_landed, 32 * (b + 1))
                pe.wait_ge(h_ready, PRIMED + b)
                for n in range(HEADS):
                    if n + 1 < HEADS:
                        spread(n + 1)
                        qk(n + 1)
                    if n:
                        values(n - 1)
                values(HEADS - 1)


def l2_ffn(nc, G, a):
    X, PS, name = G.X, G.PS, "f2_"
    with ExitStack() as ctx:
        sb = lambda n, shape, dt=F32: ctx.enter_context(nc.sbuf_tensor(name + n, shape, dt))
        sem = semaphores(nc, ctx, name)
        w, mu = sb("w", [P, 3, DC, D]), sb("mu", [P, 2, DC])
        stats, moments = sb("stats", [P, NT, 6]), sb("moments", [P, NT, 2])
        var_eps, rstd = sb("var_eps", [P, NT]), sb("rstd", [P, NT])
        xn = sb("xn", [P, 2, TPB, D])
        xnT = sb("xnT", [P, 2, DC, S + 1])
        step_x = sb("step_x", [P, DC, S])
        mixed = sb("mixed", [P, 2, 2, DC, S])
        act_k = sb("act_k", [P, 2, DC, S])
        recep = sb("recep", [P, 2, TPB, D])
        out = sb("out", [P, TPB, D])
        landed, zero_ready = sem("landed"), sem("zero_ready")
        stats_done, var_ready, rstd_ready = sem("stats_done"), sem("var_ready"), sem("rstd_ready")
        chain_s, xn_ready, xT_done, xnT_ready = sem("chain"), sem("xn_ready"), sem("xT_done"), sem("xnT_ready")
        mixed_ready, k_done, relu_s, act_ready = sem("mixed_ready"), sem("k_done"), sem("relu"), sem("act_ready")
        r_done, recep_ready, v_done = sem("r_done"), sem("recep_ready"), sem("v_done")
        block = ctx.enter_context(nc.Block())

        @block.sync
        def _(sync):
            for i in range(3):
                sync.dma_start(w[:, i, :, :], a["w_mix"][i].rearrange("(c p) n -> p c n", p=P)).then_inc(landed, 16)
            sync.dma_start(mu[:, :, :].rearrange("p i c -> p (i c)"), a["mu_mix"]).then_inc(landed, 16)

        @block.gpsimd
        def _(pool):
            layer_norm_root(pool, G, rstd, var_eps, var_ready, rstd_ready)

        @block.scalar
        def _(act):
            prime(act, xnT_ready, relu_s, act_ready, recep_ready)
            act.wait_ge(zero_ready, 1)
            with act.Fori(0, B // 2) as pair:
                for q in range(2):
                    b = 2 * pair + q
                    act.wait_ge(xT_done, PRIMED + b + 1)
                    act.wait_ge(mixed_ready, PRIMED + 2 * b)
                    act.copy(xnT[:, q, :, 1:S + 1], PS[q][:, :].rearrange("p (c s) -> p c s", s=S)).then_inc(xnT_ready, 1)
                    act.wait_ge(k_done, PRIMED + b + 1)
                    act.wait_ge(v_done, PRIMED + b)
                    k = act_k[:, q, :, :].rearrange("p c s -> p (c s)")
                    act.activation(k, PS[2 + q][:, :], ACT.Relu).then_inc(relu_s, 1)
                    act.wait_ge(relu_s, PRIMED + b + 1)
                    act.activation(k, k, ACT.Square).then_inc(act_ready, 1)
                    act.wait_ge(r_done, PRIMED + b + 1)
                    act.activation(recep[:, q, :, :].rearrange("p k d -> p (k d)"), PS[4 + q][:, :],
                                   ACT.Sigmoid).then_inc(recep_ready, 1)

        @block.vector
        def _(vector):
            prime(vector, chain_s, xn_ready, mixed_ready)
            vector.memset(xnT[:, :, :, 0:1], 0.0).then_inc(zero_ready, 1)
            vector.wait_ge(landed, 16 * 4)
            layer_norm_stats(vector, X, stats, moments, var_eps, stats_done, var_ready)
            vector.wait_ge(rstd_ready, 1)
            CH = 3
            with vector.Fori(0, B // 2) as pair:
                for q in range(2):
                    b = 2 * pair + q
                    chain = Chain(vector, chain_s, PRIMED + b * CH)
                    vector.wait_ge(xT_done, PRIMED + b)
                    for k in range(TPB):
                        ins = vector.tensor_scalar(xn[:, q, k, :], X[:, TPB * b + k, :], moments[:, TPB * b + k, 0:1],
                                                   rstd[:, bass.ds(TPB * b + k, 1)], ALU.subtract, ALU.mult)
                    ins.then_inc(xn_ready, 1)
                    vector.wait_ge(xnT_ready, PRIMED + b + 1)
                    before, now = xnT[:, q, :, 0:S], xnT[:, q, :, 1:S + 1]
                    chain(vector.tensor_tensor(step_x[:, :, :], now, before, ALU.subtract))
                    vector.wait_ge(r_done, PRIMED + b)
                    for i in (1, 0):
                        for c in range(DC):
                            ins = vector.scalar_tensor_tensor(out=mixed[:, q, i, c, :], in0=step_x[:, c, :],
                                                              scalar=mu[:, i, c:c + 1], in1=before[:, c, :],
                                                              op0=ALU.mult, op1=ALU.add)
                        ins.then_inc(mixed_ready, 1)
                    vector.wait_ge(recep_ready, PRIMED + b + 1)
                    vector.wait_ge(v_done, PRIMED + b + 1)
                    chain(vector.tensor_tensor(out[:, :, :], PS[6 + q][:, :].rearrange("p (k d) -> p k d", d=D),
                                               recep[:, q, :, :], ALU.mult))
                    x = X[:, bass.ds(TPB * b, TPB), :]
                    chain(vector.tensor_tensor(x, x, out[:, :, :], ALU.add))

        @block.tensor
        def _(pe):
            prime(pe, xT_done, k_done, r_done, v_done)
            ident = G.const("ident")
            pe.wait_ge(landed, 16 * 4)
            with pe.Fori(0, B // 2) as pair:
                for q in range(2):
                    b = 2 * pair + q
                    pe.wait_ge(xn_ready, PRIMED + b + 1)
                    pe.wait_ge(xnT_ready, PRIMED + b)
                    for c in range(DC):
                        for k in range(TPB):
                            ins = pe.transpose(PS[q][:, c * S + k * P:c * S + (k + 1) * P],
                                               xn[:, q, k, c * P:(c + 1) * P], ident)
                    ins.then_inc(xT_done, 1)
                    pe.wait_ge(mixed_ready, PRIMED + 2 * b + 1)
                    pe.wait_ge(act_ready, PRIMED + b)
                    for m in range(DC):
                        for c in range(DC):
                            ins = pe.matmul(PS[2 + q][:, m * S:(m + 1) * S], w[:, 1, c, m * P:(m + 1) * P],
                                            mixed[:, q, 1, c, :], start=c == 0, stop=c == DC - 1)
                    ins.then_inc(k_done, 1)
                    pe.wait_ge(mixed_ready, PRIMED + 2 * b + 2)
                    pe.wait_ge(recep_ready, PRIMED + b)
                    for k in range(TPB):
                        for c in range(DC):
                            ins = pe.matmul(PS[4 + q][:, k * D:(k + 1) * D], mixed[:, q, 0, c, k * P:(k + 1) * P],
                                            w[:, 0, c, :], start=c == 0, stop=c == DC - 1)
                    ins.then_inc(r_done, 1)
                    pe.wait_ge(act_ready, PRIMED + b + 1)
                    pe.wait_ge(chain_s, PRIMED + 3 * b)
                    for k in range(TPB):
                        for c in range(DC):
                            ins = pe.matmul(PS[6 + q][:, k * D:(k + 1) * D], act_k[:, q, c, k * P:(k + 1) * P],
                                            w[:, 2, c, :], start=c == 0, stop=c == DC - 1)
                    ins.then_inc(v_done, 1)


class Shared:

    def __init__(self, X, consts, PS):
        self.X, self.consts, self.PS = X, consts, PS

    def const(self, name):
        lo, hi = CONST[name]
        return self.consts[:, lo:hi]

    def mhalf(self, n):
        return self.const("half")[:, 0:n]


def build(nc, a, out):
    x_rows = a["x"].rearrange("b (k p) d -> p (b k) d", p=P)
    out_rows = out.rearrange("b (k p) d -> p (b k) d", p=P)
    with ExitStack() as ctx:
        X = ctx.enter_context(nc.sbuf_tensor("X", [P, NT, D], F32))
        consts = ctx.enter_context(nc.sbuf_tensor("consts", [P, CONSTS], F32))
        PS = [ctx.enter_context(nc.psum_tensor(f"bank{i}", [P, 512], F32)) for i in range(8)]
        x_landed = ctx.enter_context(nc.semaphore("x_landed"))
        stored = ctx.enter_context(nc.semaphore("stored"))
        G = Shared(X, consts, PS)
        G.rows = nc.dram_tensor("rows", ((TILES + 1) * R, D), F32, kind="Internal").ap()
        zeroed = ctx.enter_context(nc.semaphore("zeroed"))
        zeros = ctx.enter_context(nc.sbuf_tensor("zeros", [P, D], F32))
        with nc.Block() as block:
            @block.vector
            def _(vector):
                vector.memset(zeros[:, :], 0.0).then_inc(zeroed, 1)

            @block.scalar
            def _(act):
                act.wait_ge(zeroed, 1)
                act.dma_start(G.rows.rearrange("(n p) d -> p n d", p=P),
                              zeros[:, :].unsqueeze(1).to_broadcast([P, TILES + 1, D])).then_inc(x_landed, 16)

            @block.sync
            def _(sync):
                sync.dma_start(consts[:, :], a["consts"]).then_inc(x_landed, 16)
                sync.dma_start(X[:, :, :], x_rows).then_inc(x_landed, 16)
                sync.wait_ge(x_landed, 48)

        for layer in LAYERS:
            layer(nc, G, a)

        with nc.Block() as block:
            @block.sync
            def _(sync):
                sync.dma_start(out_rows, X[:, :, :]).then_inc(stored, 16)
                sync.wait_ge(stored, 16)


LAYERS = (
    l0_attention,
    l0_ffn,
    lambda nc, G, a: mha_block(nc, G, "a1_", a["w_mha1"], a["v_mha1"], a["ctxT"]),
    l1_ffn,
    l2_attention,
    l2_ffn,
    lambda nc, G, a: mha_block(nc, G, "a3_", a["w_mha3"], a["v_mha3"], a["ctxT"]),
    l3_ffn,
)


def constants():
    c = np.zeros((P, CONSTS), np.float32)

    def put(name, value):
        lo, hi = CONST[name]
        c[:, lo:hi] = value

    p, j = np.arange(P)[:, None], np.arange(P)[None, :]
    put("ident", p == j)
    put("before", p < j)
    put("upto", p <= j)
    put("ones", 1.0)
    put("restart", np.broadcast_to(j % NT != 0, (P, P)))
    put("head", p // 16 == np.arange(8)[None, :])
    put("iota", np.broadcast_to(np.arange(8)[None, :], (P, 8)))
    put("half", -0.5)
    put("even", p < P // 2)
    put("odd", p >= P // 2)
    put("pick", (p == np.arange(4 * P)[None, :] // P))
    HEAD = 64
    scale = np.float32(10000.0) ** (np.float32(2.0 / HEAD) * np.arange(HEAD // 2, dtype=np.float32))
    row = np.arange(P) % HEAD
    sign = np.where(row < HEAD // 2, np.float32(-1), np.float32(1))[:, None]
    for q, at in (("q", S), ("k", 0)):
        angle = np.arange(at, at + S, dtype=np.float32)[None, :] / scale[row % (HEAD // 2)][:, None]
        by = np.float32(-(HEAD ** -0.5) if q == "q" else 1.0)
        put("cos" + q, np.cos(angle) * by)
        put("sin" + q, np.sin(angle) * sign * by)
    return c


def kernel(**inputs):
    import concourse.bacc as bacc
    from concourse.bass_utils import run_bass_kernel_spmd

    i = {k: np.asarray(v) for k, v in inputs.items()}
    T = lambda a: np.ascontiguousarray(a.T)
    rows = lambda a: np.broadcast_to(a.reshape(1, -1), (P, a.size))
    chunks = lambda a: T(a.reshape(-1, P))
    cat = lambda *a: np.ascontiguousarray(np.concatenate(a, axis=1))
    laid = {"x": i["x"], "consts": constants(), "ctx": i["ctx_1024"],
            "ctxT": np.ascontiguousarray(i["ctx_1024"].transpose(0, 2, 1))}
    for n in "13":
        laid["w_mha" + n] = np.stack([T(i[f"L{n}_xattn_W{m}"]) for m in "qkvo"])
        laid["v_mha" + n] = cat(chunks(i[f"L{n}_xattn_bq"]), chunks(i[f"L{n}_xattn_bk"]),
                                rows(i[f"L{n}_xattn_bv"]), rows(i[f"L{n}_xattn_bo"]))
    hidden_chunks = lambda a: np.ascontiguousarray(a.reshape(E * HC, P).T)
    laid["w_route0"], laid["b_route0"] = i["L0_ffn_Wg"], np.zeros((P, E), np.float32)
    laid["w_route1"], laid["b_route1"] = i["L1_ffn_gate_W"], rows(i["L1_ffn_gate_b"])
    laid["w_route3"], laid["b_route3"] = T(i["L3_ffn_router_w"]), rows(i["L3_ffn_router_b"])
    for n in "01":
        laid["W1_" + n], laid["W2_" + n] = i[f"L{n}_ffn_W1"], i[f"L{n}_ffn_W2"]
        laid["b1_" + n], laid["b2_" + n] = hidden_chunks(i[f"L{n}_ffn_b1"]), rows(i[f"L{n}_ffn_b2"])
    laid["W_3"], laid["V_3"], laid["Wout_3"] = i["L3_ffn_W"], i["L3_ffn_V"], i["L3_ffn_W_out"]
    laid["affine1"] = cat(rows(i["L1_ffn_ln_gamma"]), rows(i["L1_ffn_ln_beta"]))
    wq = i["L0_xattn_q_w"].transpose(1, 0, 2)
    wk, wv = i["L0_xattn_kv_w"][0, 0], i["L0_xattn_kv_w"][1, 0]
    swap = lambda w: np.concatenate([w[..., 32:], w[..., :32]], axis=-1)
    laid["w_att0"] = np.stack([wq.reshape(D, D), swap(wq).reshape(D, D), i["L0_xattn_out_w"].reshape(D, D)])
    laid["wk_att0"] = np.stack([cat(wk, wk), cat(swap(wk), swap(wk))])
    laid["wv_att0"] = wv
    laid["gain_att0"] = chunks(i["L0_xattn_rms_scale"])
    laid["kept"] = i["mask_BxS2_bk0"].reshape(1, -1)
    both = cat(i["L2_xattn_ig_kernel"], i["L2_xattn_fg_kernel"])
    laid["gates_2"] = both.reshape(3, D, 8)
    laid["gate_bias_2"] = np.stack([i["L2_xattn_ig_bias"], i["L2_xattn_fg_bias"]], axis=1)
    laid["out_gain_2"] = rows(i["L2_xattn_outnorm_weight"])
    laid["w_mix"] = np.stack([T(i["L2_ffn_W_" + m]) for m in "rkv"])
    laid["mu_mix"] = cat(chunks(i["L2_ffn_mu_r"]), chunks(i["L2_ffn_mu_k"]))
    nc = bacc.Bacc("TRN2", target_bir_lowering=False, num_devices=1)
    aps = {}
    for name, value in laid.items():
        laid[name] = np.ascontiguousarray(value)
        aps[name] = nc.dram_tensor("in_" + name, value.shape, mybir.dt.from_np(value.dtype), kind="ExternalInput").ap()
    out = nc.dram_tensor("out", (B, S, D), F32, kind="ExternalOutput").ap()
    build(nc, aps, out)
    r = run_bass_kernel_spmd(nc, [{"in_" + name: value for name, value in laid.items()}], core_ids=[0])
    return r.results[0]["out"]
```

```python
from contextlib import ExitStack

import numpy as np

import concourse.bass as bass
from concourse import mybir

F32 = mybir.dt.float32
I32 = mybir.dt.int32
U32 = mybir.dt.uint32
U8 = mybir.dt.uint8
ALU = mybir.AluOpType
ACT = mybir.ActivationFunctionType
AX = mybir.AxisListType

P = 128
B, S, D = 8, 256, 256
TPB = S // P
NT = B * TPB
DC = D // P
LN_EPS = 1e-5
E, H = 8, 512
HC = H // P
R = 128
TILES = 2 * B * S // R + E
CAPACITY = 512

CONST = {}
_at = 0
for _name, _width in (("ident", P), ("before", P), ("ones", P), ("upto", P), ("restart", P), ("head", 8),
                      ("iota", 8), ("even", 1), ("odd", 1), ("even8", 1), ("odd8", 1), ("pick", 4 * P), ("half", 16), ("cosq", S), ("sinq", S), ("cosk", S), ("sink", S)):
    CONST[_name] = (_at, _at + _width)
    _at += _width
CONSTS = _at


PRIMED = 1


def prime(eng, *sems):
    for sem in sems:
        eng.sem_inc(sem, PRIMED)


def semaphores(nc, ctx, name):
    made = []

    def clear():
        nc.clear_and_free_semaphores(made)
        nc.all_engine_barrier(sem_only=True)

    ctx.callback(clear)

    def sem(n):
        made.append(nc.alloc_semaphore(name + n))
        return made[-1]

    return sem


class Chain:

    def __init__(self, eng, sem, base=0):
        self.eng, self.sem, self.base, self.n = eng, sem, base, 0

    def __call__(self, ins):
        self.n += 1
        ins.then_inc(self.sem, 1)
        self.eng.wait_ge(self.sem, self.base + self.n)


def bcast(ap, n):
    return ap.unsqueeze(2).to_broadcast([ap.shape[0], ap.shape[1], n])


def layer_norm_stats(vector, X, stats, moments, var_eps, stats_done, ready, eps=LN_EPS):
    for t in range(NT):
        vector.bn_stats(stats[:, t, :], X[:, t, :]).then_inc(stats_done, 1)
    for t in range(NT):
        vector.wait_ge(stats_done, t + 1)
        vector.bn_aggr(moments[:, t, :], stats[:, t, :]).then_inc(stats_done, 1)
    vector.wait_ge(stats_done, 2 * NT)
    vector.tensor_scalar(var_eps[:, :], moments[:, :, 1], eps, None, ALU.add).then_inc(ready, 1)


def layer_norm_root(pool, G, rstd, var_eps, var_ready, rstd_ready):
    pool.wait_ge(var_ready, 1)
    pool.tensor_tensor(rstd[:, :], var_eps[:, :], G.mhalf(NT), ALU.pow).then_inc(rstd_ready, 1)


def over_batches(eng, front, pair, pairs, finish):
    def body(b, q, before, after):
        for g in range(pairs):
            pair(b, q, g, before)
            if after is not None and g in front:
                front[g](after, 1 - q)
            if before is not None and g in finish:
                finish[g](before, 1 - q)

    for piece in front.values():
        piece(0, 0)
    body(0, 0, None, 1)
    with eng.Fori(0, B // 2 - 1) as two:
        for q in (1, 0):
            b = 2 * two + 2 - q
            body(b, q, b - 1, b + 1)
    body(B - 1, 1, B - 2, None)
    pair(B, 0, 0, B - 1)
    for piece in finish.values():
        piece(B - 1, 1)


def mha_block(nc, G, layer, ctx_t):
    HEADS, DH = 16, D // 16
    PAIRS = HEADS // 2
    GB = TPB * PAIRS
    VW = DH + 1
    PVN = 6 * VW
    VCOLS = (HEADS - 1) * VW + PVN
    X, PS, name = G.X, G.PS, layer + "_"
    w, vec, w_landed = G.weights["w_" + layer], G.weights["v_" + layer], G.landed[layer]
    with ExitStack() as ctx:
        sb = lambda n, shape, dt=F32: ctx.enter_context(nc.sbuf_tensor(name + n, shape, dt))
        sem = semaphores(nc, ctx, name)
        nbq = sb("nbq", [P, DC])
        ctxT = sb("ctxT", [P, DC, S])
        stats, moments = sb("stats", [P, NT, 6]), sb("moments", [P, NT, 2])
        var_eps, rstd = sb("var_eps", [P, NT]), sb("rstd", [P, NT])
        xn = sb("xn", [P, TPB, D])
        xnT = sb("xnT", [P, DC, S])
        qT, kT = sb("qT", [P, 2, DC, S]), sb("kT", [P, DC, S])
        kTm = sb("kTm", [P, 2, HEADS, S])
        vaug = sb("vaug", [P, 2, TPB, VCOLS])
        nmax = sb("nmax", [P, 2, 2])
        prob = sb("prob", [P, 2, 2, S])
        probT = sb("probT", [P, 2, 4, P])
        rsum = sb("rsum", [P, TPB, HEADS])
        enc, encT = sb("enc", [P, TPB, D]), sb("encT", [P, DC, S])
        ctx_landed = sem("ctx_landed")
        stats_done, chain_s, kmask_s = sem("stats_done"), sem("chain"), sem("kmask_done")
        var_ready, rstd_ready, xn_ready = sem("var_ready"), sem("rstd_ready"), sem("xn_ready")
        xT_done, xnT_ready = sem("xT_done"), sem("xnT_ready")
        q_done, q_ready = sem("q_done"), sem("q_ready")
        k_done, k_ready = sem("k_done"), sem("k_ready")
        v_done, v_ready = sem("v_done"), sem("v_ready")
        score_done, max_ready, prob_ready = sem("score_done"), sem("max_ready"), sem("prob_ready")
        probT_done, probT_ready, pv_done = sem("probT_done"), sem("probT_ready"), sem("pv_done")
        enc_ready, encT_done, encT_ready = sem("enc_ready"), sem("encT_done"), sem("encT_ready")
        out_done, added, nbq_ready, ones_ready = sem("out_done"), sem("added"), sem("nbq_ready"), sem("ones_ready")
        bq, bk = vec[:, 0:DC], vec[:, DC:2 * DC]
        bv, bo = vec[:, 2 * DC:2 * DC + D], vec[:, 2 * DC + D:2 * DC + 2 * D]
        ps_x, ps_q = PS[0], PS[1]
        ps_s, ps_t, ps_o = [PS[2], PS[3]], [PS[4], PS[5]], [PS[6], PS[7]]
        LAST = GB - 1
        CH = TPB + 1
        block = ctx.enter_context(nc.Block())

        @block.sync
        def _(sync):
            with sync.Fori(0, B) as b:
                sync.wait_ge(v_done, PRIMED + b)
                sync.dma_start(ctxT[:, :, :], ctx_t[b].rearrange("(c p) n -> p c n", p=P)).then_inc(ctx_landed, 16)

        @block.gpsimd
        def _(pool):
            prime(pool, kmask_s)
            layer_norm_root(pool, G, rstd, var_eps, var_ready, rstd_ready)

            def mask_keys(b, q):
                pool.wait_ge(k_ready, PRIMED + b + 1)
                if not isinstance(b, int) or b >= 2:
                    pool.wait_ge(score_done, PRIMED + GB * (b - 1))
                for h in range(HEADS):
                    rows_of_head = G.const("head")[:, h % 8:h % 8 + 1].to_broadcast([P, S])
                    ins = pool.tensor_tensor(kTm[:, q, h, :], kT[:, h // 8, :], rows_of_head, ALU.mult)
                    if h % 2:
                        ins.then_inc(kmask_s, 1)

            mask_keys(0, 0)
            mask_keys(1, 1)
            with pool.Fori(1, B // 2) as two:
                for q in range(2):
                    mask_keys(2 * two + q, q)

        @block.scalar
        def _(act):
            prime(act, q_ready, prob_ready)
            act.wait_ge(w_landed, 16 * 2)
            act.mul(nbq[:, :], bq, -0.25).then_inc(nbq_ready, 1)
            act.wait_ge(nbq_ready, 1)

            def queries(b, q):
                act.wait_ge(q_done, PRIMED + b + 1)
                if not isinstance(b, int) or b >= 2:
                    act.wait_ge(score_done, PRIMED + GB * (b - 1))
                for c in range(DC):
                    ins = act.activation(qT[:, q, c, :], ps_q[:, c * S:(c + 1) * S], ACT.Identity,
                                         bias=nbq[:, c:c + 1], scale=-0.25)
                ins.then_inc(q_ready, 1)

            def exponents(b, q, g, before):
                if isinstance(b, int) and b == B:
                    return
                act.wait_ge(max_ready, PRIMED + GB * b + g + 1)
                if before is not None or g >= 2:
                    act.wait_ge(probT_done, PRIMED + GB * b + g - 1)
                for i in range(2):
                    ins = act.activation(prob[:, g % 2, i, :], ps_s[g % 2][:, i * S:(i + 1) * S], ACT.Exp,
                                         bias=nmax[:, g % 2, i:i + 1], scale=-1.0)
                ins.then_inc(prob_ready, 1)

            over_batches(act, {10: queries}, exponents, GB, {})

        @block.vector
        def _(vector):
            prime(vector, chain_s, xn_ready, xnT_ready, k_ready, v_ready, max_ready, probT_ready, enc_ready, encT_ready, added)
            vector.memset(vaug[:, :, :, :], 1.0).then_inc(ones_ready, 1)
            layer_norm_stats(vector, X, stats, moments, var_eps, stats_done, var_ready)
            vector.wait_ge(w_landed, 16 * 2)
            vector.wait_ge(ones_ready, 1)
            vector.wait_ge(rstd_ready, 1)

            def normalize(b, q):
                vector.wait_ge(xT_done, PRIMED + b)
                for k in range(TPB):
                    t = TPB * b + k
                    ins = vector.tensor_scalar(xn[:, k, :], X[:, bass.ds(t, 1), :].rearrange("p o d -> p (o d)"),
                                               moments[:, bass.ds(t, 1), 0], rstd[:, bass.ds(t, 1)],
                                               ALU.subtract, ALU.mult)
                ins.then_inc(xn_ready, 1)

            def x_turned(b, q):
                vector.wait_ge(xT_done, PRIMED + b + 1)
                vector.wait_ge(q_done, PRIMED + b)
                vector.tensor_copy(xnT[:, :, :].rearrange("p c s -> p (c s)"), ps_x[:, :]).then_inc(xnT_ready, 1)

            def keys(b, q):
                vector.wait_ge(k_done, PRIMED + b + 1)
                vector.wait_ge(kmask_s, PRIMED + PAIRS * b)
                for c in range(DC):
                    ins = vector.tensor_scalar(kT[:, c, :], ps_x[:, c * S:(c + 1) * S], bk[:, c:c + 1], None, ALU.add)
                ins.then_inc(k_ready, 1)

            def values(b, q):
                vector.wait_ge(v_done, PRIMED + b + 1)
                if not isinstance(b, int) or b >= 2:
                    vector.wait_ge(pv_done, PRIMED + GB * (b - 1))
                for k in range(TPB):
                    ins = vector.tensor_tensor(
                        vaug[:, q, k, 0:HEADS * VW].rearrange("p (h v) -> p h v", v=VW)[:, :, 0:DH],
                        ps_q[:, k * D:(k + 1) * D].rearrange("p (h v) -> p h v", v=DH),
                        bv.rearrange("p (h v) -> p h v", v=DH), ALU.add)
                ins.then_inc(v_ready, 1)

            def turn_probabilities(b, g):
                vector.wait_ge(probT_done, PRIMED + GB * b + g + 1)
                if not isinstance(b, int) or b > 0 or g >= 2:
                    vector.wait_ge(pv_done, PRIMED + GB * b + g - 1)
                vector.tensor_copy(probT[:, g % 2, :, :].rearrange("p a t -> p (a t)"),
                                   ps_t[g % 2][:, :]).then_inc(probT_ready, 1)

            def encode(b, k):
                chain = Chain(vector, chain_s, PRIMED + b * CH + k)
                vector.wait_ge(pv_done, PRIMED + GB * b + PAIRS * (k + 1))
                o = ps_o[k][:, 0:HEADS * VW].rearrange("p (h v) -> p h v", v=VW)
                chain(vector.reciprocal(rsum[:, k, :], o[:, :, DH]))
                vector.wait_ge(encT_done, PRIMED + b)
                vector.tensor_tensor(enc[:, k, :].rearrange("p (h v) -> p h v", v=DH), o[:, :, 0:DH],
                                     bcast(rsum[:, k, :], DH), ALU.mult).then_inc(enc_ready, 1)

            def pair(b, q, g, before):
                if not isinstance(b, int) or b < B:
                    vector.wait_ge(score_done, PRIMED + GB * b + g + 1)
                    if before is not None or g >= 2:
                        vector.wait_ge(prob_ready, PRIMED + GB * b + g - 1)
                    vector.tensor_reduce(nmax[:, g % 2, :], ps_s[g % 2][:, :].rearrange("p (h s) -> p h s", s=S),
                                         AX.X, ALU.min).then_inc(max_ready, 1)
                if g:
                    turn_probabilities(b, g - 1)
                elif before is not None:
                    turn_probabilities(before, LAST)
                if g == PAIRS + 1:
                    encode(b, 0)

            def enc_turned(b, q):
                vector.wait_ge(encT_done, PRIMED + b + 1)
                vector.wait_ge(out_done, PRIMED + b)
                vector.tensor_copy(encT[:, :, :].rearrange("p c s -> p (c s)"), ps_x[:, :]).then_inc(encT_ready, 1)

            def add(b, q):
                chain = Chain(vector, chain_s, PRIMED + b * CH + TPB)
                vector.wait_ge(out_done, PRIMED + b + 1)
                x = X[:, bass.ds(TPB * b, TPB), :]
                chain(vector.tensor_tensor(x, ps_q[:, :].rearrange("p (k d) -> p k d", d=D), x, ALU.add))
                vector.tensor_tensor(x, x, bo.unsqueeze(1).to_broadcast([P, TPB, D]), ALU.add).then_inc(added, 1)

            over_batches(vector, {6: normalize, 8: x_turned, 10: keys, 12: values}, pair, GB,
                         {1: lambda b, q: encode(b, 1), 4: enc_turned, 6: add})

        @block.tensor
        def _(pe):
            prime(pe, xT_done, q_done, k_done, v_done, score_done, probT_done, pv_done, encT_done, out_done)
            ident = G.const("ident")
            pe.wait_ge(w_landed, 16 * 2)

            def turn(source, to):
                for c in range(DC):
                    for k in range(TPB):
                        ins = pe.transpose(to[:, c * S + k * P:c * S + (k + 1) * P],
                                           source[:, k, c * P:(c + 1) * P], ident)
                return ins

            def turn_x(b, q):
                pe.wait_ge(xn_ready, PRIMED + b + 1)
                if not isinstance(b, int) or b >= 2:
                    pe.wait_ge(encT_ready, PRIMED + b - 1)
                turn(xn, ps_x).then_inc(xT_done, 1)

            def project_qk(b, q):
                pe.wait_ge(xnT_ready, PRIMED + b + 1)
                if not isinstance(b, int) or b >= 2:
                    pe.wait_ge(added, PRIMED + b - 1)
                pe.wait_ge(ctx_landed, 16 * (b + 1))
                for i, source, to, done in ((0, xnT, ps_q, q_done), (1, ctxT, ps_x, k_done)):
                    for m in range(DC):
                        for c in range(DC):
                            ins = pe.matmul(to[:, m * S:(m + 1) * S], w[:, i, c, m * P:(m + 1) * P], source[:, c, :],
                                            start=c == 0, stop=c == DC - 1)
                    ins.then_inc(done, 1)

            def project_v(b, q):
                pe.wait_ge(q_ready, PRIMED + b + 1)
                for k in range(TPB):
                    for c in range(DC):
                        ins = pe.matmul(ps_q[:, k * D:(k + 1) * D], ctxT[:, c, k * P:(k + 1) * P], w[:, 2, c, :],
                                        start=c == 0, stop=c == DC - 1)
                ins.then_inc(v_done, 1)

            def scores(b, q, g):
                k, j = divmod(g, PAIRS)
                if k == 0:
                    pe.wait_ge(kmask_s, PRIMED + PAIRS * b + j + 1)
                if g == 0:
                    pe.wait_ge(q_ready, PRIMED + b + 1)
                if not isinstance(b, int) or b > 0 or g >= 2:
                    pe.wait_ge(prob_ready, PRIMED + GB * b + g - 1)
                pe.matmul(ps_s[g % 2][:, :], qT[:, q, j // 4, k * P:(k + 1) * P], kTm[:, q, 2 * j:2 * j + 2, :],
                          start=True, stop=True).then_inc(score_done, 1)

            def transposes(b, g):
                pe.wait_ge(prob_ready, PRIMED + GB * b + g + 1)
                if not isinstance(b, int) or b > 0 or g >= 2:
                    pe.wait_ge(probT_ready, PRIMED + GB * b + g - 1)
                for i in range(2):
                    for c in range(TPB):
                        ins = pe.transpose(ps_t[g % 2][:, (2 * i + c) * P:(2 * i + c + 1) * P],
                                           prob[:, g % 2, i, c * P:(c + 1) * P], ident)
                ins.then_inc(probT_done, 1)

            def values(b, q, g):
                k, j = divmod(g, PAIRS)
                pe.wait_ge(probT_ready, PRIMED + GB * b + g + 1)
                if j == 0 and (not isinstance(b, int) or b > 0):
                    pe.wait_ge(enc_ready, PRIMED + TPB * (b - 1) + k + 1)
                if g == 0:
                    pe.wait_ge(v_ready, PRIMED + b + 1)
                for i in range(2):
                    at = (2 * j + i) * VW
                    for c in range(TPB):
                        ins = pe.matmul(ps_o[k][:, at:at + PVN], probT[:, g % 2, 2 * i + c, :],
                                        vaug[:, q, c, at:at + PVN], start=c == 0, stop=c == TPB - 1)
                ins.then_inc(pv_done, 1)

            def pair(b, q, g, before):
                if not isinstance(b, int) or b < B:
                    if before is None and g == 0:
                        scores(b, q, 0)
                    if g < LAST:
                        scores(b, q, g + 1)
                    elif not (isinstance(b, int) and b == B - 1):
                        scores(b + 1, 1 - q, 0)
                    transposes(b, g)
                if g:
                    values(b, q, g - 1)
                elif before is not None:
                    values(before, 1 - q, LAST)

            def turn_enc(b, q):
                pe.wait_ge(enc_ready, PRIMED + TPB * (b + 1))
                pe.wait_ge(k_ready, PRIMED + b + 1 + (0 if isinstance(b, int) and b == B - 1 else 1))
                turn(enc, ps_x).then_inc(encT_done, 1)

            def project_out(b, q):
                pe.wait_ge(encT_ready, PRIMED + b + 1)
                pe.wait_ge(v_ready, PRIMED + b + 1 + (0 if isinstance(b, int) and b == B - 1 else 1))
                for k in range(TPB):
                    for c in range(DC):
                        ins = pe.matmul(ps_q[:, k * D:(k + 1) * D], encT[:, c, k * P:(k + 1) * P], w[:, 3, c, :],
                                        start=c == 0, stop=c == DC - 1)
                ins.then_inc(out_done, 1)

            over_batches(pe, {7: turn_x, 9: project_qk, 11: project_v}, pair, GB, {3: turn_enc, 5: project_out})


class Routing:

    def __init__(self, nc, ctx, name):
        sb = lambda n, shape, dt=F32: ctx.enter_context(nc.sbuf_tensor(name + n, shape, dt))
        self.xn = sb("xn", [P, NT, D])
        self.slots = sb("slots", [P, 2, NT], U32)
        self.share = sb("share", [P, 2, NT])
        self.bounds = sb("bounds", [P, 2, 2, E], I32)
        self.took = [sb("took0", [P, NT, D]), sb("took1", [P, NT, D])]


def scatter_rows(pool, G, source, slots, ready, scattered):
    pool.wait_ge(ready, 1)
    pool.wait_ge(G.rows_filled, 16)
    for t in range(NT):
        pool.indirect_dma_start(G.rows[:, :], bass.IndirectOffsetOnAxis(slots[:, t:t + 1], 0),
                                source[:, t, :], None).then_inc(scattered, 16)


def router_block(nc, G, name, rt, w_router, bias, joint, over_all, capacity):
    X, PS = G.X, G.PS
    with ExitStack() as ctx:
        sb = lambda n, shape, dt=F32: ctx.enter_context(nc.sbuf_tensor(name + n, shape, dt))
        sem = semaphores(nc, ctx, name)
        w, bias_sb = sb("w", [P, DC, E]), sb("bias", [P, E])
        stats, moments = sb("stats", [P, NT, 6]), sb("moments", [P, NT, 2])
        var_eps, rstd = sb("var_eps", [P, NT]), sb("rstd", [P, NT])
        xT = sb("xT", [P, 2, DC, P])
        logits, best = sb("logits", [P, NT, E]), sb("best", [P, NT, 8])
        best_at = sb("best_at", [P, NT, 8], U32)
        weight, total = sb("weight", [P, NT, 8]), sb("total", [P, NT])
        chosen_at = sb("chosen_at", [P, 2, NT])
        chosen = sb("chosen", [P, 3, NT, E])
        tile_sum, running = sb("tile_sum", [P, E, NT]), sb("running", [P, E, NT])
        rank = sb("rank", [P, NT, E])
        picked = sb("picked", [P, NT, E])
        tiles, tiles_i, end = sb("tiles", [P, E]), sb("tiles_i", [P, E], I32), sb("end", [P, E])
        first = sb("first", [P, E])
        slot_f, keep = sb("slot_f", [P, NT]), sb("keep", [P, NT])
        landed, stats_done, chain_s = sem("landed"), sem("stats_done"), sem("chain")
        var_ready, rstd_ready, xn_ready = sem("var_ready"), sem("rstd_ready"), sem("xn_ready")
        xT_done, xT_ready, logits_done = sem("xT_done"), sem("xT_ready"), sem("logits_done")
        shifted, weight_ready = sem("shifted"), sem("weight_ready")
        chosen_ready, counted = sem("chosen_ready"), sem("counted")
        slots_ready, scattered = sem("slots_ready"), sem("scattered")
        ps_logits, ps_within, ps_tile = PS[2], PS[3], PS[4]
        dispatches = [(2, (0, 1))] if joint else [(0, (0,)), (1, (1,))]
        block = ctx.enter_context(nc.Block())

        @block.sync
        def _(sync):
            sync.dma_start(w[:, :, :], w_router.rearrange("(c p) e -> p c e", p=P)).then_inc(landed, 16)
            sync.dma_start(bias_sb[:, :], bias).then_inc(landed, 16)

        @block.gpsimd
        def _(pool):
            layer_norm_root(pool, G, rstd, var_eps, var_ready, rstd_ready)
            pool.wait_ge(xn_ready, NT)
            for k in range(2 if joint else 1):
                scatter_rows(pool, G, rt.xn, rt.slots[:, k, :], slots_ready, scattered)
            pool.wait_ge(scattered, 16 * NT * (2 if joint else 1))

        @block.scalar
        def _(act):
            for t in range(NT):
                act.wait_ge(xT_done, t + 1)
                if t >= 2:
                    act.wait_ge(logits_done, t - 1)
                act.copy(xT[:, t % 2, :, :].rearrange("p c s -> p (c s)"), PS[t % 2][:, 0:D]).then_inc(xT_ready, 1)
            act.wait_ge(shifted, 1)
            act.activation(weight[:, :, :], weight[:, :, :], ACT.Exp).then_inc(weight_ready, 1)

        @block.tensor
        def _(pe):
            pe.wait_ge(landed, 32)

            def logits_of(t):
                pe.wait_ge(xT_ready, t + 1)
                for c in range(DC):
                    ins = pe.matmul(ps_logits[:, t * E:(t + 1) * E], xT[:, t % 2, c, :], w[:, c, :],
                                    start=c == 0, stop=c == DC - 1)
                ins.then_inc(logits_done, 1)

            for t in range(NT):
                pe.wait_ge(xn_ready, t + 1)
                if t >= 2:
                    pe.wait_ge(xT_ready, t - 1)
                for c in range(DC):
                    ins = pe.transpose(PS[t % 2][:, c * P:(c + 1) * P], rt.xn[:, t, c * P:(c + 1) * P],
                                       G.const("ident"))
                ins.then_inc(xT_done, 1)
                if t:
                    logits_of(t - 1)
            logits_of(NT - 1)
            for n, (which, _) in enumerate(dispatches):
                pe.wait_ge(chosen_ready, 1)
                rhs = chosen[:, which, :, :].rearrange("p t e -> p (t e)")
                pe.matmul(ps_within[:, n * P:(n + 1) * P], G.const("before"), rhs, start=True, stop=True)
                pe.matmul(ps_tile[:, n * P:(n + 1) * P], G.const("ones"), rhs, start=True, stop=True).then_inc(counted, 1)

        @block.vector
        def _(vector):
            chain = Chain(vector, chain_s)
            layer_norm_stats(vector, X, stats, moments, var_eps, stats_done, var_ready)
            vector.wait_ge(rstd_ready, 1)
            for t in range(NT):
                vector.tensor_scalar(rt.xn[:, t, :], X[:, t, :], moments[:, t, 0:1], rstd[:, t:t + 1],
                                     ALU.subtract, ALU.mult).then_inc(xn_ready, 1)
            vector.wait_ge(landed, 32)
            vector.wait_ge(logits_done, NT)
            chain(vector.tensor_tensor(logits[:, :, :], ps_logits[:, 0:NT * E].rearrange("p (t e) -> p t e", e=E),
                                       bias_sb[:, :].unsqueeze(1).to_broadcast([P, NT, E]), ALU.add))
            for t in range(NT):
                ins = vector.max(best[:, t, :], logits[:, t, :])
                if t == NT - 1:
                    chain(ins)
            for t in range(NT):
                ins = vector.max_index(best_at[:, t, :], best[:, t, :], logits[:, t, :])
            vector.tensor_tensor(weight[:, :, :], best[:, :, :], best[:, :, 0:1].to_broadcast([P, NT, 8]),
                                 ALU.subtract).then_inc(shifted, 1)
            vector.wait_ge(shifted, 1)
            chain(vector.tensor_copy(chosen_at[:, :, :], best_at[:, :, 0:2].rearrange("p t k -> p k t")))
            iota = G.const("iota").unsqueeze(1).to_broadcast([P, NT, E])
            for k in range(2):
                chain(vector.tensor_tensor(chosen[:, k, :, :], iota, bcast(chosen_at[:, k, :], E), ALU.is_equal))
            vector.tensor_tensor(chosen[:, 2, :, :], chosen[:, 0, :, :], chosen[:, 1, :, :],
                                 ALU.add).then_inc(chosen_ready, 1)
            vector.wait_ge(weight_ready, 1)
            chain(vector.tensor_reduce(total[:, :], weight[:, :, :] if over_all else weight[:, :, 0:2], AX.X, ALU.add))
            chain(vector.reciprocal(total[:, :], total[:, :]))
            for k in range(2):
                chain(vector.tensor_tensor(rt.share[:, k, :], weight[:, :, k], total[:, :], ALU.mult))
            for n, (which, ks) in enumerate(dispatches):
                vector.wait_ge(counted, len(dispatches))
                within = ps_within[:, n * P:(n + 1) * P].rearrange("p (t e) -> p t e", e=E)
                chain(vector.tensor_copy(tile_sum[:, :, :],
                                         ps_tile[:, n * P:(n + 1) * P].rearrange("p (t e) -> p e t", e=E)))
                flat = lambda a: a.rearrange("p e t -> p (e t)")
                chain(vector.tensor_tensor_scan(flat(running[:, :, :]), G.const("restart"), flat(tile_sum[:, :, :]),
                                                0.0, ALU.mult, ALU.add))
                chain(vector.tensor_scalar(tiles[:, :], running[:, :, NT - 1], float(R - 1), 1.0 / R, ALU.add, ALU.mult))
                chain(vector.tensor_scalar(tiles_i[:, :], tiles[:, :], -0.498, None, ALU.add))
                chain(vector.tensor_scalar(tiles[:, :], tiles_i[:, :], 1.0, None, ALU.max))
                chain(vector.tensor_tensor_scan(end[:, :], G.const("ones")[:, 0:E], tiles[:, :], 0.0, ALU.mult, ALU.add))
                chain(vector.tensor_tensor(first[:, :], end[:, :], tiles[:, :], ALU.subtract))
                chain(vector.tensor_copy(rt.bounds[:, n, 0, :], first[:, :]))
                chain(vector.tensor_copy(rt.bounds[:, n, 1, :], end[:, :]))
                chain(vector.tensor_tensor(running[:, :, :], running[:, :, :], tile_sum[:, :, :], ALU.subtract))
                chain(vector.tensor_tensor(rank[:, :, :], within, running[:, :, :].rearrange("p e t -> p t e"), ALU.add))
                if capacity:
                    for k in ks:
                        chain(vector.tensor_tensor(picked[:, :, :], rank[:, :, :], chosen[:, k, :, :], ALU.mult))
                        chain(vector.tensor_reduce(keep[:, :], picked[:, :, :], AX.X, ALU.add))
                        chain(vector.tensor_scalar(keep[:, :], keep[:, :], float(capacity), None, ALU.is_lt))
                        chain(vector.tensor_tensor(rt.share[:, k, :], rt.share[:, k, :], keep[:, :], ALU.mult))
                chain(vector.tensor_scalar(first[:, :], first[:, :], float(R), None, ALU.mult))
                chain(vector.tensor_tensor(rank[:, :, :], rank[:, :, :],
                                           first[:, :].unsqueeze(1).to_broadcast([P, NT, E]), ALU.add))
                for k in ks:
                    chain(vector.tensor_tensor(picked[:, :, :], rank[:, :, :], chosen[:, k, :, :], ALU.mult))
                    chain(vector.tensor_reduce(slot_f[:, :], picked[:, :, :], AX.X, ALU.add))
                    chain(vector.tensor_copy(rt.slots[:, k, :], slot_f[:, :]))
                if n == 0:
                    vector.tensor_scalar(total[:, :], total[:, :], 1.0, None, ALU.mult).then_inc(slots_ready, 1)


def experts_block(nc, G, name, rt, n, weights, biases):
    GLU = len(weights) == 3
    UP = len(weights) - 1
    WB = 3
    HALVES = ((0, 1), (2, 3))
    PS = G.PS
    with ExitStack() as ctx:
        sb = lambda m, shape, dt=F32: ctx.enter_context(nc.sbuf_tensor(name + m, shape, dt))
        sem = semaphores(nc, ctx, name)
        up = [[sb(f"up{q}{i}", [P, DC, H]) for i in range(UP)] for q in range(WB)]
        down = [sb(f"down{q}", [P, HC, D]) for q in range(WB)]
        b1, b2 = sb("b1", [P, E, HC]), sb("b2", [P, E, D])
        xt, xT = sb("xt", [P, D]), sb("xT", [P, DC, R])
        hT, gate = sb("hT", [P, HC, R]), sb("gate", [P, HC, R])
        y = sb("y", [P, D])
        biases_landed, x_landed = sem("biases_landed"), sem("x_landed")
        weights_landed = [sem(f"weights{q}_landed") for q in range(WB)]
        stored = sem("stored")
        xT_done, xT_ready = sem("xT_done"), sem("xT_ready")
        h_done = sem("h_done")
        hT_ready = [sem("hT0_ready"), sem("hT1_ready")]
        y_done, y_ready = sem("y_done"), sem("y_ready")
        gate_ready, gated = sem("gate_ready"), sem("gated")
        ps_t, ps_y, ps_h = PS[0], PS[1], [PS[2], PS[3]]
        block = ctx.enter_context(nc.Block())

        def each_expert(eng, body):
            ends = [eng.value_load(rt.bounds[0:1, n, 1, e:e + 1], min_val=0, max_val=TILES) for e in range(E)]
            for e in range(E):
                body(e, ends[e - 1] if e else 0, ends[e])
            return ends[-1]

        @block.sync
        def _(sync):
            prime(sync, x_landed)

            def load(j):
                sync.dma_start(xt[:, :], G.rows[bass.ds(j * R, R), :]).then_inc(x_landed, 16)

            load(0)
            if biases is not None:
                sync.dma_start(b1[:, :, :].rearrange("p e c -> p (e c)"), biases[0]).then_inc(biases_landed, 16)
                sync.dma_start(b2[:, :, :].rearrange("p e d -> p (e d)"), biases[1]).then_inc(biases_landed, 16)
            count = sync.value_load(rt.bounds[0:1, n, 1, E - 1:E], min_val=0, max_val=TILES)
            with sync.Fori(0, count) as j:
                sync.wait_ge(xT_done, PRIMED + j + 1)
                load(j + 1)

        @block.scalar
        def _(act):
            prime(act, gate_ready, stored)
            if not GLU:
                prime(act, hT_ready[0])

            def load(e):
                q = e % WB
                for i in reversed(range(UP)):
                    act.dma_start(up[q][i][:, :, :], weights[i][e].rearrange("(c p) n -> p c n", p=P)).then_inc(weights_landed[q], 16)
                act.dma_start(down[q][:, :, :], weights[UP][e].rearrange("(c p) n -> p c n", p=P)).then_inc(weights_landed[q], 16)

            for e in range(WB - 1):
                load(e)
            if not GLU:
                act.wait_ge(biases_landed, 32)

            def expert(e, lo, hi):
                if e + WB - 1 < E:
                    if e:
                        act.wait_ge(y_done, PRIMED + lo)
                    load(e + WB - 1)
                with act.Fori(lo, hi) as j:
                    act.wait_ge(h_done, PRIMED + 2 * j + 1)
                    if GLU:
                        act.wait_ge(gated, PRIMED + j)
                        act.activation(gate[:, :, :].rearrange("p c r -> p (c r)"), ps_h[1][:, :],
                                       ACT.Sigmoid).then_inc(gate_ready, 1)
                    else:
                        for m in HALVES[0]:
                            ins = act.activation(hT[:, m, :], ps_h[0][:, m * R:(m + 1) * R], ACT.Relu,
                                                 bias=b1[:, e, m:m + 1])
                        ins.then_inc(hT_ready[0], 1)
                    act.wait_ge(y_ready, PRIMED + j + 1)
                    act.dma_start(G.rows[bass.ds(j * R, R), :], y[:, :]).then_inc(stored, 16)

            each_expert(act, expert)

        @block.vector
        def _(vector):
            prime(vector, xT_ready, hT_ready[1], y_ready, gated)
            if GLU:
                prime(vector, hT_ready[0])
            else:
                vector.wait_ge(biases_landed, 32)

            def xT_of(j):
                vector.wait_ge(xT_done, PRIMED + j + 1)
                vector.wait_ge(h_done, PRIMED + 2 * j)
                vector.tensor_copy(xT[:, :, :].rearrange("p c r -> p (c r)"), ps_t[:, 0:D]).then_inc(xT_ready, 1)

            xT_of(0)

            def expert(e, lo, hi):
                with vector.Fori(lo, hi) as j:
                    if GLU:
                        flat = lambda a: a[:, :, :].rearrange("p c r -> p (c r)")
                        vector.wait_ge(gate_ready, PRIMED + j + 1)
                        vector.wait_ge(y_done, PRIMED + j)
                        vector.tensor_tensor(flat(hT), ps_h[1][:, :], flat(gate), ALU.mult).then_inc(gated, 1)
                        vector.wait_ge(gated, PRIMED + j + 1)
                        vector.wait_ge(h_done, PRIMED + 2 * j + 2)
                        for i, (m, _) in enumerate(HALVES):
                            part = flat(hT)[:, m * R:(m + 2) * R]
                            vector.tensor_tensor(part, ps_h[0][:, m * R:(m + 2) * R], part, ALU.mult).then_inc(hT_ready[i], 1)
                    else:
                        vector.wait_ge(h_done, PRIMED + 2 * j + 2)
                        for m in HALVES[1]:
                            ins = vector.tensor_scalar(hT[:, m, :], ps_h[1][:, (m - 2) * R:(m - 1) * R],
                                                       b1[:, e, m:m + 1], 0.0, ALU.add, ALU.max)
                        ins.then_inc(hT_ready[1], 1)
                    xT_of(j + 1)
                    vector.wait_ge(y_done, PRIMED + j + 1)
                    vector.wait_ge(stored, PRIMED + 16 * j)
                    if biases is None:
                        vector.tensor_copy(y[:, :], ps_y[:, 0:D]).then_inc(y_ready, 1)
                    else:
                        vector.tensor_tensor(y[:, :], ps_y[:, 0:D], b2[:, e, :], ALU.add).then_inc(y_ready, 1)

            count = each_expert(vector, expert)
            vector.wait_ge(stored, PRIMED + 16 * count)
            vector.memset(y[:, 0:1], 0.0)

        @block.tensor
        def _(pe):
            prime(pe, xT_done, h_done, y_done)

            def transposes(j):
                pe.wait_ge(x_landed, PRIMED + 16 * j + 16)
                pe.wait_ge(xT_ready, PRIMED + j)
                for c in range(DC):
                    ins = pe.transpose(ps_t[:, c * R:(c + 1) * R], xt[:, c * P:(c + 1) * P], G.const("ident"))
                ins.then_inc(xT_done, 1)

            transposes(0)

            def expert(e, lo, hi):
                q = e % WB
                pe.wait_ge(weights_landed[q], 16 * (UP + 1) * (e // WB + 1))
                with pe.Fori(lo, hi) as j:
                    pe.wait_ge(xT_ready, PRIMED + j + 1)
                    for half in hT_ready:
                        pe.wait_ge(half, PRIMED + j)
                    for i in reversed(range(UP)):
                        for m in range(HC):
                            to = ps_h[i][:, m * R:(m + 1) * R] if GLU else ps_h[m // 2][:, m % 2 * R:(m % 2 + 1) * R]
                            for c in range(DC):
                                ins = pe.matmul(to, up[q][i][:, c, m * P:(m + 1) * P],
                                                xT[:, c, :], start=c == 0, stop=c == DC - 1)
                            if GLU and m == HC - 1 or not GLU and m % 2:
                                ins.then_inc(h_done, 1)
                    transposes(j + 1)
                    pe.wait_ge(y_ready, PRIMED + j)
                    for i, half in enumerate(HALVES):
                        pe.wait_ge(hT_ready[i], PRIMED + j + 1)
                        for m in half:
                            ins = pe.matmul(ps_y[:, 0:D], hT[:, m, :], down[q][:, m, :], start=m == 0, stop=m == HC - 1)
                    ins.then_inc(y_done, 1)

            each_expert(pe, expert)


def combine_block(nc, G, name, rt):
    with ExitStack() as ctx:
        sem = semaphores(nc, ctx, name)
        gathered = [sem(f"gathered{t}") for t in range(4)]
        added = sem("added")
        block = ctx.enter_context(nc.Block())

        @block.gpsimd
        def _(pool):
            for t in range(NT):
                for k in range(2):
                    pool.indirect_dma_start(rt.took[k][:, t, :], None, G.rows[:, :],
                                            bass.IndirectOffsetOnAxis(rt.slots[:, k, t:t + 1], 0)
                                            ).then_inc(gathered[t % 4], 16)
                if t >= 3:
                    pool.wait_ge(gathered[(t - 3) % 4], 32 * ((t - 3) // 4 + 1))

        @block.vector
        def _(vector):
            for k in range(2):
                for t in range(NT):
                    if k == 0:
                        vector.wait_ge(gathered[t % 4], 32 * (t // 4 + 1))
                    else:
                        vector.wait_ge(added, t + 1)
                    ins = vector.scalar_tensor_tensor(out=G.X[:, t, :], in0=rt.took[k][:, t, :],
                                                      scalar=rt.share[:, k, t:t + 1], in1=G.X[:, t, :],
                                                      op0=ALU.mult, op1=ALU.add)
                    if k == 0:
                        ins.then_inc(added, 1)


def l0_ffn(nc, G, a):
    with ExitStack() as ctx:
        rt = Routing(nc, ctx, "f0_")
        router_block(nc, G, "f0r_", rt, a["w_route0"], a["b_route0"], joint=True, over_all=True, capacity=None)
        experts_block(nc, G, "f0e_", rt, 0, (a["W1_0"], a["W2_0"]), (a["b1_0"], a["b2_0"]))
        combine_block(nc, G, "f0c_", rt)


def l3_ffn(nc, G, a):
    with ExitStack() as ctx:
        rt = Routing(nc, ctx, "f3_")
        router_block(nc, G, "f3r_", rt, a["w_route3"], a["b_route3"], joint=True, over_all=False, capacity=CAPACITY)
        experts_block(nc, G, "f3e_", rt, 0, (a["W_3"], a["V_3"], a["Wout_3"]), None)
        combine_block(nc, G, "f3c_", rt)


def boost_block(nc, G, name, rt):
    with ExitStack() as ctx:
        sem = semaphores(nc, ctx, name)
        gathered = [sem(f"gathered{t}") for t in range(4)]
        boosted, scattered = sem("boosted"), sem("scattered")
        block = ctx.enter_context(nc.Block())

        @block.gpsimd
        def _(pool):
            def scatter(t):
                pool.wait_ge(boosted, t + 1)
                pool.indirect_dma_start(G.rows[:, :], bass.IndirectOffsetOnAxis(rt.slots[:, 1, t:t + 1], 0),
                                        rt.took[1][:, t, :], None).then_inc(scattered, 16)

            for t in range(NT):
                pool.indirect_dma_start(rt.took[0][:, t, :], None, G.rows[:, :],
                                        bass.IndirectOffsetOnAxis(rt.slots[:, 0, t:t + 1], 0)
                                        ).then_inc(gathered[t % 4], 16)
                if t >= 3:
                    pool.wait_ge(gathered[(t - 3) % 4], 16 * ((t - 3) // 4 + 1))
            for i in range(4):
                pool.wait_ge(gathered[i], 16 * (NT // 4))
            for t in range(NT):
                scatter(t)
            pool.wait_ge(scattered, 16 * NT)

        @block.vector
        def _(vector):
            for t in range(NT):
                vector.wait_ge(gathered[t % 4], 16 * (t // 4 + 1))
                vector.scalar_tensor_tensor(out=rt.took[1][:, t, :], in0=rt.took[0][:, t, :], scalar=0.5,
                                            in1=rt.xn[:, t, :], op0=ALU.mult, op1=ALU.add).then_inc(boosted, 1)


def fuse_block(nc, G, name, rt, affine):
    X = G.X
    with ExitStack() as ctx:
        sb = lambda m, shape, dt=F32: ctx.enter_context(nc.sbuf_tensor(name + m, shape, dt))
        sem = semaphores(nc, ctx, name)
        gamma_beta = sb("gamma_beta", [P, 2, D])
        stats, moments = sb("stats", [P, NT, 6]), sb("moments", [P, NT, 2])
        var_eps, rstd = sb("var_eps", [P, NT]), sb("rstd", [P, NT])
        gathered = [sem(f"gathered{t}") for t in range(4)]
        landed, first_added, both_added = sem("landed"), sem("first_added"), sem("both_added")
        stats_done, var_ready, rstd_ready = sem("stats_done"), sem("var_ready"), sem("rstd_ready")
        normed, scaled, moved = sem("normed"), sem("scaled"), sem("moved")
        block = ctx.enter_context(nc.Block())

        @block.sync
        def _(sync):
            sync.dma_start(gamma_beta[:, :, :].rearrange("p i d -> p (i d)"), affine).then_inc(landed, 16)

        @block.gpsimd
        def _(pool):
            for t in range(NT):
                pool.indirect_dma_start(rt.took[1][:, t, :], None, G.rows[:, :],
                                        bass.IndirectOffsetOnAxis(rt.slots[:, 1, t:t + 1], 0)
                                        ).then_inc(gathered[t % 4], 16)
                if t >= 3:
                    pool.wait_ge(gathered[(t - 3) % 4], 16 * ((t - 3) // 4 + 1))
            layer_norm_root(pool, G, rstd, var_eps, var_ready, rstd_ready)
            pool.wait_ge(landed, 16)
            for t in range(NT):
                pool.wait_ge(normed, t + 1)
                pool.tensor_tensor(rt.took[0][:, t, :], rt.took[0][:, t, :], gamma_beta[:, 0, :], ALU.mult).then_inc(scaled, 1)
                pool.wait_ge(scaled, t + 1)
                pool.tensor_tensor(rt.took[0][:, t, :], rt.took[0][:, t, :], gamma_beta[:, 1, :], ALU.add).then_inc(moved, 1)

        @block.vector
        def _(vector):
            for t in range(NT):
                vector.scalar_tensor_tensor(out=rt.xn[:, t, :], in0=rt.took[0][:, t, :], scalar=rt.share[:, 0, t:t + 1],
                                            in1=rt.xn[:, t, :], op0=ALU.mult, op1=ALU.add).then_inc(first_added, 1)
            for t in range(NT):
                vector.wait_ge(first_added, t + 1)
                vector.wait_ge(gathered[t % 4], 16 * (t // 4 + 1))
                vector.scalar_tensor_tensor(out=rt.xn[:, t, :], in0=rt.took[1][:, t, :], scalar=rt.share[:, 1, t:t + 1],
                                            in1=rt.xn[:, t, :], op0=ALU.mult, op1=ALU.add).then_inc(both_added, 1)
            vector.wait_ge(both_added, NT)
            layer_norm_stats(vector, rt.xn, stats, moments, var_eps, stats_done, var_ready)
            vector.wait_ge(rstd_ready, 1)
            for t in range(NT):
                vector.tensor_scalar(rt.took[0][:, t, :], rt.xn[:, t, :], moments[:, t, 0:1], rstd[:, t:t + 1],
                                     ALU.subtract, ALU.mult).then_inc(normed, 1)
            for t in range(NT):
                vector.wait_ge(moved, t + 1)
                vector.tensor_tensor(X[:, t, :], X[:, t, :], rt.took[0][:, t, :], ALU.add)


def l1_ffn(nc, G, a):
    with ExitStack() as ctx:
        rt = Routing(nc, ctx, "f1_")
        w, b = (a["W1_1"], a["W2_1"]), (a["b1_1"], a["b2_1"])
        router_block(nc, G, "f1r_", rt, a["w_route1"], a["b_route1"], joint=False, over_all=True, capacity=None)
        experts_block(nc, G, "f1e0_", rt, 0, w, b)
        boost_block(nc, G, "f1b_", rt)
        experts_block(nc, G, "f1e1_", rt, 1, w, b)
        fuse_block(nc, G, "f1c_", rt, a["affine1"])


MASK_FILL = 2.3819763e38
NO_FLOOR = -3.4e38


def l0_attention(nc, G, a):
    HEADS, DH = 4, 64
    PAIRS = HEADS // 2
    GB = TPB * PAIRS
    PVN = 96
    RMS_EPS = 1e-6
    X, PS, name = G.X, G.PS, "a0_"
    with ExitStack() as ctx:
        sb = lambda n, shape, dt=F32: ctx.enter_context(nc.sbuf_tensor(name + n, shape, dt))
        sem = semaphores(nc, ctx, name)
        w, wk, wv, gain = (G.weights[n] for n in ("w_att0", "wk_att0", "wv_att0", "gain_att0"))
        context = G.context
        kept_u8 = sb("kept_u8", [P, B, S], U8)
        kept, floor = sb("kept", [P, B, S]), sb("floor", [P, B, S])
        stats, moments = sb("stats", [P, NT, 6]), sb("moments", [P, NT, 2])
        c_stats, c_moments = sb("c_stats", [P, NT, 6]), sb("c_moments", [P, NT, 2])
        var_eps, c_sq = sb("var_eps", [P, NT]), sb("c_sq", [P, NT])
        rstd, xf, cf = sb("rstd", [P, NT]), sb("xf", [P, NT]), sb("cf", [P, NT])
        xn, cn = sb("xn", [P, TPB, D]), sb("cn", [P, TPB, D])
        xnT, cnT = sb("xnT", [P, DC, S]), sb("cnT", [P, DC, S])
        turn = sb("turn", [P, 2, DC, S])
        qT, kT, kTm = sb("qT", [P, DC, S]), sb("kT", [P, S]), sb("kTm", [P, 2, S])
        vaug = sb("vaug", [P, 2, TPB, PVN])
        masked = sb("masked", [P, 2, 2, S])
        nmax = sb("nmax", [P, 2, 2])
        prob, probT = sb("prob", [P, 2, 2, S]), sb("probT", [P, 2, 4, P])
        rsum = sb("rsum", [P, TPB, HEADS])
        enc, encT = sb("enc", [P, TPB, D]), sb("encT", [P, DC, S])
        mask_landed, gain_ready, scaled, ones_ready = sem("mask_landed"), sem("gain_ready"), sem("scaled"), sem("ones_ready")
        stats_done, c_stats_done, var_ready, c_var_ready = sem("stats_done"), sem("c_stats_done"), sem("var_ready"), sem("c_var_ready")
        c_sq_ready, root_s, root_ready = sem("c_sq_ready"), sem("root_steps"), sem("root_ready")
        kept_ready, fill_ready = sem("kept_ready"), sem("fill_ready")
        xn_ready, xT_done, xnT_ready = sem("xn_ready"), sem("xT_done"), sem("xnT_ready")
        q_turn, k_turn, recip_s, masked_ready = sem("q_turn"), sem("k_turn"), sem("reciprocals"), sem("masked_ready")
        q_done, q_ready, k_done, k_ready = sem("q_done"), sem("q_ready"), sem("k_done"), sem("k_ready")
        v_done, v_ready = sem("v_done"), sem("v_ready")
        score_done, max_ready, prob_ready = sem("score_done"), sem("max_ready"), sem("prob_ready")
        probT_done, probT_ready, pv_done = sem("probT_done"), sem("probT_ready"), sem("pv_done")
        enc_ready, encT_done, encT_ready = sem("enc_ready"), sem("encT_done"), sem("encT_ready")
        out_done, added = sem("out_done"), sem("added")
        ps_x, ps_q, ps_f, ps_s, ps_t, ps_o = PS[0], PS[1], PS[2], PS[3], [PS[4], PS[5]], [PS[6], PS[7]]
        LAST = GB - 1
        block = ctx.enter_context(nc.Block())

        @block.sync
        def _(sync):
            sync.dma_start(kept_u8[:, :, :].rearrange("p b s -> p (b s)"), a["kept"].to_broadcast([P, B * S])).then_inc(mask_landed, 16)

        @block.gpsimd
        def _(pool):
            step = Chain(pool, root_s)
            half = G.mhalf(NT)
            pool.wait_ge(var_ready, 1)
            step(pool.tensor_tensor(rstd[:, :], var_eps[:, :], half, ALU.pow))
            step(pool.tensor_tensor(xf[:, :], rstd[:, :], rstd[:, :], ALU.mult))
            step(pool.tensor_tensor(xf[:, :], xf[:, :], moments[:, :, 1], ALU.mult))
            step(pool.tensor_scalar(xf[:, :], xf[:, :], RMS_EPS, None, ALU.add))
            step(pool.tensor_tensor(xf[:, :], xf[:, :], half, ALU.pow))
            pool.tensor_tensor(xf[:, :], xf[:, :], rstd[:, :], ALU.mult).then_inc(root_ready, 1)
            pool.wait_ge(c_sq_ready, 1)
            pool.tensor_tensor(cf[:, :], c_sq[:, :], half, ALU.pow).then_inc(root_ready, 1)

        @block.scalar
        def _(act):
            prime(act, xnT_ready, v_ready, prob_ready)

            def x_turned(b, q):
                act.wait_ge(xT_done, PRIMED + b + 1)
                act.wait_ge(v_done, PRIMED + b)
                act.copy(xnT[:, :, :].rearrange("p c s -> p (c s)"), ps_x[:, :])
                act.copy(cnT[:, :, :].rearrange("p c s -> p (c s)"), ps_q[:, :]).then_inc(xnT_ready, 1)

            def values(b, q):
                act.wait_ge(v_done, PRIMED + b + 1)
                if not isinstance(b, int) or b >= 2:
                    act.wait_ge(pv_done, PRIMED + GB * (b - 1))
                act.copy(vaug[:, q, :, 0:DH], ps_q[:, 0:TPB * DH].rearrange("p (k v) -> p k v", v=DH)).then_inc(v_ready, 1)

            def exponents(b, q, g, before):
                if isinstance(b, int) and b == B:
                    return
                act.wait_ge(max_ready, PRIMED + GB * b + g + 1)
                if before is not None or g >= 2:
                    act.wait_ge(probT_done, PRIMED + GB * b + g - 1)
                for i in range(2):
                    ins = act.activation(prob[:, g % 2, i, :], masked[:, g % 2, i, :], ACT.Exp,
                                         bias=nmax[:, g % 2, i:i + 1], scale=-1.0)
                ins.then_inc(prob_ready, 1)

            act.wait_ge(mask_landed, 16)
            act.copy(kept[:, :, :], kept_u8[:, :, :]).then_inc(kept_ready, 1)
            act.wait_ge(ones_ready, 1)
            over_batches(act, {1: x_turned, 3: values}, exponents, GB, {})

        @block.vector
        def _(vector):
            prime(vector, q_turn, k_turn, recip_s, masked_ready, xn_ready, q_ready, k_ready, max_ready, probT_ready, enc_ready, encT_ready, added)
            vector.memset(vaug[:, :, :, :], 1.0).then_inc(ones_ready, 1)
            layer_norm_stats(vector, X, stats, moments, var_eps, stats_done, var_ready)
            vector.wait_ge(G.landed["att0"], 16 * 4)
            vector.tensor_scalar(gain[:, :], gain[:, :], 1.0, None, ALU.add).then_inc(gain_ready, 1)
            vector.wait_ge(G.context_landed, 16)
            layer_norm_stats(vector, context, c_stats, c_moments, c_sq, c_stats_done, c_var_ready, RMS_EPS)
            vector.wait_ge(gain_ready, 1)
            for c in range(DC):
                for part in (w[:, 0:2, c, :], wk[:, :, c, :], wv[:, c, :]):
                    ins = vector.tensor_scalar(part, part, gain[:, c:c + 1], None, ALU.mult)
            ins.then_inc(scaled, 1)
            vector.wait_ge(c_var_ready, 1)
            vector.tensor_tensor(cf[:, :], c_moments[:, :, 0], c_moments[:, :, 0], ALU.mult).then_inc(c_var_ready, 1)
            vector.wait_ge(c_var_ready, 2)
            vector.tensor_tensor(c_sq[:, :], c_sq[:, :], cf[:, :], ALU.add).then_inc(c_sq_ready, 1)
            vector.wait_ge(kept_ready, 1)
            vector.tensor_scalar(floor[:, :, :], kept[:, :, :], -MASK_FILL, MASK_FILL, ALU.mult, ALU.add).then_inc(fill_ready, 1)
            vector.wait_ge(fill_ready, 1)
            vector.scalar_tensor_tensor(out=floor[:, :, :], in0=kept[:, :, :], scalar=NO_FLOOR, in1=floor[:, :, :],
                                        op0=ALU.mult, op1=ALU.add).then_inc(fill_ready, 1)
            vector.wait_ge(root_ready, 2)
            vector.wait_ge(fill_ready, 2)

            def normalize(b, q):
                vector.wait_ge(xT_done, PRIMED + b)
                for k in range(TPB):
                    t = TPB * b + k
                    vector.tensor_scalar(xn[:, k, :], X[:, t, :], moments[:, t, 0:1], xf[:, bass.ds(t, 1)],
                                         ALU.subtract, ALU.mult)
                    ins = vector.tensor_scalar(cn[:, k, :], context[:, t, :], cf[:, bass.ds(t, 1)], None, ALU.mult)
                ins.then_inc(xn_ready, 1)

            def rotate_q(b, q):
                vector.wait_ge(q_done, PRIMED + b + 1)
                halves = lambda ps: ps[:, :].rearrange("p (c s) -> p c s", s=S)
                for i, ps, factor in ((0, ps_x, "cosq"), (1, ps_q, "sinq")):
                    vector.tensor_tensor(turn[:, i, :, :], halves(ps), G.const(factor).unsqueeze(1).to_broadcast([P, DC, S]),
                                         ALU.mult).then_inc(q_turn, 1)
                vector.wait_ge(score_done, PRIMED + GB * b)
                vector.wait_ge(q_turn, PRIMED + 2 * (b + 1))
                vector.tensor_tensor(qT[:, :, :], turn[:, 0, :, :], turn[:, 1, :, :], ALU.add).then_inc(q_ready, 1)

            def rotate_k(b, q):
                vector.wait_ge(k_done, PRIMED + b + 1)
                vector.wait_ge(q_ready, PRIMED + b + 1)
                for i, factor in enumerate(("cosk", "sink")):
                    vector.tensor_tensor(turn[:, i, 0, :], ps_x[:, i * S:(i + 1) * S], G.const(factor), ALU.mult).then_inc(k_turn, 1)
                vector.wait_ge(k_turn, PRIMED + 3 * b + 2)
                vector.tensor_tensor(kT[:, :], turn[:, 0, 0, :], turn[:, 1, 0, :], ALU.add).then_inc(k_turn, 1)
                vector.wait_ge(k_turn, PRIMED + 3 * b + 3)
                for i, rows in enumerate(("even", "odd")):
                    ins = vector.tensor_scalar(kTm[:, i, :], kT[:, :], G.const(rows), None, ALU.mult)
                ins.then_inc(k_ready, 1)

            def turn_probabilities(b, g):
                vector.wait_ge(probT_done, PRIMED + GB * b + g + 1)
                if not isinstance(b, int) or b > 0 or g >= 2:
                    vector.wait_ge(pv_done, PRIMED + GB * b + g - 1)
                vector.tensor_copy(probT[:, g % 2, :, :].rearrange("p a t -> p (a t)"),
                                   ps_t[g % 2][:, :]).then_inc(probT_ready, 1)

            def encode(b, k):
                vector.wait_ge(pv_done, PRIMED + GB * b + PAIRS * (k + 1))
                o = ps_o[k][:, 0:HEADS * PVN].rearrange("p (h v) -> p h v", v=PVN)
                vector.reciprocal(rsum[:, k, :], o[:, :, DH]).then_inc(recip_s, 1)
                vector.wait_ge(encT_done, PRIMED + b)
                vector.wait_ge(recip_s, PRIMED + TPB * b + k + 1)
                vector.tensor_tensor(enc[:, k, :].rearrange("p (h v) -> p h v", v=DH), o[:, :, 0:DH],
                                     bcast(rsum[:, k, :], DH), ALU.mult).then_inc(enc_ready, 1)

            def pair(b, q, g, before):
                if not isinstance(b, int) or b < B:
                    vector.wait_ge(score_done, PRIMED + GB * b + g + 1)
                    if before is not None or g >= 2:
                        vector.wait_ge(prob_ready, PRIMED + GB * b + g - 1)
                    m = masked[:, g % 2, :, :]
                    vector.tensor_tensor(m, ps_s[:, :].rearrange("p (h s) -> p h s", s=S),
                                         floor[:, bass.ds(b, 1), :].to_broadcast([P, 2, S]), ALU.max).then_inc(masked_ready, 1)
                    vector.wait_ge(masked_ready, PRIMED + GB * b + g + 1)
                    vector.tensor_reduce(nmax[:, g % 2, :], m, AX.X, ALU.min).then_inc(max_ready, 1)
                if g:
                    turn_probabilities(b, g - 1)
                elif before is not None:
                    turn_probabilities(before, LAST)
                if g == LAST:
                    encode(b, 0)

            def enc_turned(b, q):
                vector.wait_ge(encT_done, PRIMED + b + 1)
                vector.wait_ge(out_done, PRIMED + b)
                vector.tensor_copy(encT[:, :, :].rearrange("p c s -> p (c s)"), ps_f[:, :]).then_inc(encT_ready, 1)

            def add(b, q):
                vector.wait_ge(out_done, PRIMED + b + 1)
                x = X[:, bass.ds(TPB * b, TPB), :]
                vector.tensor_tensor(x, ps_f[:, :].rearrange("p (k d) -> p k d", d=D), x, ALU.add).then_inc(added, 1)

            over_batches(vector, {0: normalize, 2: rotate_q, 3: rotate_k}, pair, GB,
                         {0: lambda b, q: encode(b, 1), 1: enc_turned, 3: add})

        @block.tensor
        def _(pe):
            prime(pe, xT_done, q_done, k_done, v_done, score_done, probT_done, pv_done, encT_done, out_done)
            ident = G.const("ident")
            pe.wait_ge(scaled, 1)

            def turn_x(b, q):
                pe.wait_ge(xn_ready, PRIMED + b + 1)
                if not isinstance(b, int) or b >= 1:
                    pe.wait_ge(k_ready, PRIMED + b)
                    pe.wait_ge(v_ready, PRIMED + b)
                for source, to in ((xn, ps_x), (cn, ps_q)):
                    for c in range(DC):
                        for k in range(TPB):
                            ins = pe.transpose(to[:, c * S + k * P:c * S + (k + 1) * P],
                                               source[:, k, c * P:(c + 1) * P], ident)
                ins.then_inc(xT_done, 1)

            def project_q(b, q):
                pe.wait_ge(xnT_ready, PRIMED + b + 1)
                for i, to in ((0, ps_x), (1, ps_q)):
                    for m in range(DC):
                        for c in range(DC):
                            ins = pe.matmul(to[:, m * S:(m + 1) * S], w[:, i, c, m * P:(m + 1) * P], xnT[:, c, :],
                                            start=c == 0, stop=c == DC - 1)
                ins.then_inc(q_done, 1)

            def project_kv(b, q):
                pe.wait_ge(q_ready, PRIMED + b + 1)
                for i in range(2):
                    for c in range(DC):
                        ins = pe.matmul(ps_x[:, i * S:(i + 1) * S], wk[:, i, c, :], cnT[:, c, :],
                                        start=c == 0, stop=c == DC - 1)
                ins.then_inc(k_done, 1)
                for k in range(TPB):
                    for c in range(DC):
                        ins = pe.matmul(ps_q[:, k * DH:(k + 1) * DH], cnT[:, c, k * P:(k + 1) * P], wv[:, c, :],
                                        start=c == 0, stop=c == DC - 1)
                ins.then_inc(v_done, 1)

            def scores(b, q, g):
                k, j = divmod(g, PAIRS)
                if g == 0:
                    pe.wait_ge(k_ready, PRIMED + b + 1)
                if not isinstance(b, int) or b > 0 or g > 0:
                    pe.wait_ge(masked_ready, PRIMED + GB * b + g)
                pe.matmul(ps_s[:, :], qT[:, j, k * P:(k + 1) * P], kTm[:, :, :],
                          start=True, stop=True).then_inc(score_done, 1)

            def transposes(b, g):
                pe.wait_ge(prob_ready, PRIMED + GB * b + g + 1)
                if not isinstance(b, int) or b > 0 or g >= 2:
                    pe.wait_ge(probT_ready, PRIMED + GB * b + g - 1)
                for i in range(2):
                    for c in range(TPB):
                        ins = pe.transpose(ps_t[g % 2][:, (2 * i + c) * P:(2 * i + c + 1) * P],
                                           prob[:, g % 2, i, c * P:(c + 1) * P], ident)
                ins.then_inc(probT_done, 1)

            def values(b, q, g):
                k, j = divmod(g, PAIRS)
                pe.wait_ge(probT_ready, PRIMED + GB * b + g + 1)
                if j == 0 and (not isinstance(b, int) or b > 0):
                    pe.wait_ge(enc_ready, PRIMED + TPB * (b - 1) + k + 1)
                if g == 0:
                    pe.wait_ge(v_ready, PRIMED + b + 1)
                for i in range(2):
                    at = (2 * j + i) * PVN
                    for c in range(TPB):
                        ins = pe.matmul(ps_o[k][:, at:at + PVN], probT[:, g % 2, 2 * i + c, :],
                                        vaug[:, q, c, :], start=c == 0, stop=c == TPB - 1)
                ins.then_inc(pv_done, 1)

            def pair(b, q, g, before):
                if not isinstance(b, int) or b < B:
                    if before is None and g == 0:
                        scores(b, q, 0)
                    if g < LAST:
                        scores(b, q, g + 1)
                    transposes(b, g)
                    if g == LAST and not (isinstance(b, int) and b == B - 1):
                        scores(b + 1, 1 - q, 0)
                if g:
                    values(b, q, g - 1)
                elif before is not None:
                    values(before, 1 - q, LAST)

            def turn_enc(b, q):
                pe.wait_ge(enc_ready, PRIMED + TPB * (b + 1))
                if not isinstance(b, int) or b > 0:
                    pe.wait_ge(added, PRIMED + b)
                for c in range(DC):
                    for k in range(TPB):
                        ins = pe.transpose(ps_f[:, c * S + k * P:c * S + (k + 1) * P],
                                           enc[:, k, c * P:(c + 1) * P], ident)
                ins.then_inc(encT_done, 1)

            def project_out(b, q):
                pe.wait_ge(encT_ready, PRIMED + b + 1)
                for k in range(TPB):
                    for c in range(DC):
                        ins = pe.matmul(ps_f[:, k * D:(k + 1) * D], encT[:, c, k * P:(k + 1) * P], w[:, 2, c, :],
                                        start=c == 0, stop=c == DC - 1)
                ins.then_inc(out_done, 1)

            over_batches(pe, {0: turn_x, 1: project_q, 2: project_kv}, pair, GB, {1: turn_enc, 3: project_out})


FORGET, GATE_COLS = 32, 36


def l2_attention(nc, G, a):
    HEADS, DH = 4, 64
    VW = DH + 1
    PVN = 96
    VCOLS = (HEADS - 1) * VW + PVN
    LAST = HEADS - 1
    X, PS, name = G.X, G.PS, "a2_"
    BIG = 3.0e38
    with ExitStack() as ctx:
        sb = lambda n, shape, dt=F32: ctx.enter_context(nc.sbuf_tensor(name + n, shape, dt))
        sem = semaphores(nc, ctx, name)
        gates_w, gate_bias, out_gain = (G.weights[n] for n in ("gates_2", "gate_bias_2", "out_gain_2"))
        ctxT = sb("ctxT", [P, B, DC, S])
        stats, moments = sb("stats", [P, NT, 6]), sb("moments", [P, NT, 2])
        var_eps, rstd = sb("var_eps", [P, NT]), sb("rstd", [P, NT])
        xn, xnT = sb("xn", [P, TPB, D]), sb("xnT", [P, B, DC, S])
        ig, z, soft = (sb(n, [HEADS, B, S]) for n in ("ig", "z", "soft"))
        forget = sb("forget", [HEADS, B, S])
        go_on, apart = sb("go_on", [HEADS, B, S]), sb("apart", [HEADS, B, S])
        m_rows = sb("m_rows", [P, B, S])
        cols = sb("cols", [P, 2, NT, HEADS])
        vaug = sb("vaug", [P, NT, VCOLS])
        kTm = sb("kTm", [P, 2, 2, DC, S])
        expo, decay = sb("expo", [P, 2, S + P]), sb("decay", [P, 2, S + P])
        cT = sb("cT", [P, 2, S + P])
        norm = sb("norm", [P, TPB, HEADS])
        h, square = sb("h", [P, TPB, D]), sb("square", [P, TPB, D])
        mean, root = sb("mean", [P, TPB * HEADS]), sb("root", [P, TPB * HEADS])
        ctx_landed, zeros_ready, vaug_s = sem("ctx_landed"), sem("zeros_ready"), sem("vaug_ready")
        stats_done, var_ready, rstd_ready = sem("stats_done"), sem("var_ready"), sem("rstd_ready")
        gates_summed, xn_ready, xT_done, xnT_ready = sem("gates_summed"), sem("xn_ready"), sem("xT_done"), sem("xnT_ready")
        gates_done, gates_ready, abs_ready, soft_ready = sem("gates_done"), sem("gates_ready"), sem("abs_ready"), sem("soft_ready")
        row_s, act_s, rows_ready, cols_done, cols_ready = sem("row_steps"), sem("act_steps"), sem("rows_ready"), sem("cols_done"), sem("cols_ready")
        kTm_ready, spread_done, qk_done = sem("kTm_ready"), sem("spread_done"), sem("qk_done")
        expo_ready, decay_ready, cT_ready = sem("expo_ready"), sem("decay_ready"), sem("cT_ready")
        masked_ready, pv_done, h_ready = sem("masked_ready"), sem("pv_done"), sem("h_ready")
        chain_s, square_ready, var2_ready, root_ready = sem("chain"), sem("square_ready"), sem("h_var_ready"), sem("root_ready")
        scaled_ready, gained, added = sem("scaled_ready"), sem("gained"), sem("added")
        ps_x, ps_g, ps_c = PS[0], PS[1], PS[2]
        ps_qk, ps_m, ps_o = [PS[2], PS[3]], [PS[4], PS[5]], [[PS[6], PS[7]], [PS[0], PS[1]]]
        flat = lambda t: t.rearrange("p b s -> p (b s)")
        by_head = lambda t: t[:, :, :].rearrange("p k (h v) -> p (k h) v", v=DH)
        block = ctx.enter_context(nc.Block())

        @block.sync
        def _(sync):
            sync.dma_start(ctxT[:, :, :, :].rearrange("p b c s -> p (b c) s"),
                           a["ctxT"].rearrange("b (c p) s -> p (b c) s", p=P)).then_inc(ctx_landed, 16)

        @block.gpsimd
        def _(pool):
            prime(pool, kTm_ready, masked_ready, root_ready, gained, added)
            pool.memset(m_rows[:, :, :], 0.0).then_inc(zeros_ready, 1)
            pool.memset(vaug[:, :, :], 1.0).then_inc(vaug_s, 1)
            layer_norm_root(pool, G, rstd, var_eps, var_ready, rstd_ready)
            pool.wait_ge(vaug_s, 1)
            pool.wait_ge(G.context_landed, 16)
            for t in range(0, NT, 4):
                ins = pool.tensor_copy(vaug[:, t:t + 4, 0:HEADS * VW].rearrange("p t (h v) -> p t h v", v=VW)[:, :, :, 0:DH],
                                       G.context[:, t:t + 4, :].rearrange("p t (h v) -> p t h v", v=DH))
            ins.then_inc(vaug_s, 1)
            pool.wait_ge(ctx_landed, 16)

            def keys(b, q):
                if not isinstance(b, int) or b >= 2:
                    pool.wait_ge(qk_done, PRIMED + HEADS * (b - 1))
                for i, rows in enumerate(("even8", "odd8")):
                    ins = pool.tensor_tensor(kTm[:, q, i, :, :].rearrange("p c s -> p (c s)"),
                                             ctxT[:, bass.ds(b, 1), :, :].rearrange("p o c s -> p (o c s)"),
                                             G.const(rows).to_broadcast([P, DC * S]), ALU.mult)
                ins.then_inc(kTm_ready, 1)

            def mask(b, n):
                pool.wait_ge(cT_ready, PRIMED + HEADS * b + n + 1)
                for at in (0, S):
                    part = cT[:, n % 2, at:at + P]
                    ins = pool.tensor_tensor(part, part, G.const("upto"), ALU.mult)
                ins.then_inc(masked_ready, 1)

            def pair(b, q, n, before):
                if n:
                    mask(b, n - 1)
                elif before is not None:
                    mask(before, LAST)

            def root_of(b, q):
                pool.wait_ge(var2_ready, PRIMED + b + 1)
                pool.tensor_tensor(root[:, :], root[:, :], G.const("half")[:, 0:TPB * HEADS], ALU.pow).then_inc(root_ready, 1)

            def add(b, q):
                pool.wait_ge(scaled_ready, PRIMED + b + 1)
                pool.tensor_tensor(h[:, :, :], h[:, :, :], out_gain[:, :].unsqueeze(1).to_broadcast([P, TPB, D]),
                                   ALU.mult).then_inc(gained, 1)
                pool.wait_ge(gained, PRIMED + b + 1)
                x = X[:, bass.ds(TPB * b, TPB), :]
                pool.tensor_tensor(x, x, h[:, :, :], ALU.add).then_inc(added, 1)

            over_batches(pool, {1: keys}, pair, HEADS, {2: root_of, 3: add})

        @block.scalar
        def _(act):
            prime(act, xnT_ready, decay_ready, square_ready)
            with act.Fori(0, B) as b:
                act.wait_ge(xT_done, PRIMED + b + 1)
                act.copy(xnT[:, bass.ds(b, 1), :, :].rearrange("p o c s -> p (o c s)"), ps_x[:, :]).then_inc(xnT_ready, 1)
            act.wait_ge(abs_ready, 1)
            act.activation(soft[:, :, :], soft[:, :, :], ACT.Exp, scale=-1.0).then_inc(act_s, 1)
            act.wait_ge(act_s, 1)
            act.activation(soft[:, :, :], soft[:, :, :], ACT.Ln, bias=1.0).then_inc(soft_ready, 1)
            act.wait_ge(cols_done, 1)
            rows_of = lambda i: ps_c[:, i * NT * HEADS:(i + 1) * NT * HEADS]
            act.activation(cols[:, 1, :, :].rearrange("p t n -> p (t n)"), rows_of(1), ACT.Exp, scale=-1.0)
            act.mul(cols[:, 0, :, :].rearrange("p t n -> p (t n)"), rows_of(0), -1.0).then_inc(cols_ready, 1)

            def exponents(b, q, n, before):
                if isinstance(b, int) and b == B:
                    return
                act.wait_ge(expo_ready, PRIMED + HEADS * b + n + 1)
                if before is not None or n >= 2:
                    act.wait_ge(cT_ready, PRIMED + HEADS * b + n - 1)
                act.activation(decay[:, n % 2, :], expo[:, n % 2, :], ACT.Exp).then_inc(decay_ready, 1)

            def squares(b, q):
                act.wait_ge(h_ready, PRIMED + b + 1)
                act.activation(square[:, :, :], h[:, :, :], ACT.Square).then_inc(square_ready, 1)

            over_batches(act, {}, exponents, HEADS, {1: squares})

        @block.vector
        def _(vector):
            prime(vector, xn_ready, gates_ready, chain_s, expo_ready, cT_ready, h_ready, var2_ready, scaled_ready)
            layer_norm_stats(vector, X, stats, moments, var_eps, stats_done, var_ready)
            vector.wait_ge(G.landed["mlstm"], 16 * 3)
            vector.tensor_tensor(gates_w[:, 1, :, :], gates_w[:, 1, :, :], gates_w[:, 2, :, :], ALU.add).then_inc(gates_summed, 1)
            row = Chain(vector, row_s)
            row(vector.memset(go_on[:, :, :], 1.0))
            row(vector.memset(go_on[:, :, 0:1], 0.0))
            row(vector.memset(apart[:, :, :], 0.0))
            row(vector.memset(apart[:, :, 0:1], BIG))
            vector.wait_ge(rstd_ready, 1)

            def normalize(b):
                vector.wait_ge(xT_done, PRIMED + b)
                for k in range(TPB):
                    ins = vector.tensor_scalar(xn[:, k, :], X[:, TPB * b + k, :], moments[:, TPB * b + k, 0:1],
                                               rstd[:, bass.ds(TPB * b + k, 1)], ALU.subtract, ALU.mult)
                ins.then_inc(xn_ready, 1)

            def gates(b):
                vector.wait_ge(gates_done, PRIMED + b + 1)
                for to, at in ((ig, 0), (z, FORGET)):
                    ins = vector.tensor_scalar(to[:, bass.ds(b, 1), :].rearrange("p o s -> p (o s)"),
                                               ps_g[at:at + HEADS, 0:S], gate_bias[at:at + HEADS, 0:1], None, ALU.add)
                ins.then_inc(gates_ready, 1)

            normalize(0)
            with vector.Fori(1, B) as b:
                normalize(b)
                gates(b - 1)
            gates(B - 1)
            vector.wait_ge(gates_ready, PRIMED + B)
            vector.scalar_tensor_tensor(out=soft[:, :, :], in0=z[:, :, :], scalar=-1.0, in1=z[:, :, :], op0=ALU.mult,
                                        op1=ALU.max).then_inc(abs_ready, 1)
            vector.wait_ge(abs_ready, 1)
            row(vector.tensor_scalar(z[:, :, :], z[:, :, :], 0.0, None, ALU.min))
            vector.wait_ge(soft_ready, 1)
            row(vector.tensor_tensor(z[:, :, :], z[:, :, :], soft[:, :, :], ALU.subtract))
            row(vector.tensor_tensor_scan(flat(forget[:, :, :]), flat(go_on[:, :, :]), flat(z[:, :, :]), 0.0, ALU.mult, ALU.add))
            row(vector.tensor_tensor(ig[:, :, :], forget[:, :, :], ig[:, :, :], ALU.subtract))
            vector.wait_ge(zeros_ready, 1)
            row(vector.tensor_tensor_scan(flat(m_rows[0:HEADS, :, :]), flat(apart[:, :, :]), flat(ig[:, :, :]), 0.0, ALU.add, ALU.min))
            vector.tensor_tensor(z[:, :, :], forget[:, :, :], m_rows[0:HEADS, :, :], ALU.subtract).then_inc(rows_ready, 1)
            vector.wait_ge(cols_ready, 1)

            def expo_of(b, n):
                vector.wait_ge(spread_done, PRIMED + HEADS * b + n + 1)
                if not isinstance(b, int) or b > 0 or n >= 2:
                    vector.wait_ge(decay_ready, PRIMED + HEADS * b + n - 1)
                for k, to, lo in ((0, 0, 0), (1, S, P)):
                    ins = vector.tensor_scalar(expo[:, n % 2, to:to + S - lo], ps_m[n % 2][:, lo:S],
                                               cols[:, 0, bass.ds(TPB * b + k, 1), n], 0.0, ALU.add, ALU.min)
                ins.then_inc(expo_ready, 1)

            def cT_of(b, n):
                vector.wait_ge(qk_done, PRIMED + HEADS * b + n + 1)
                vector.wait_ge(decay_ready, PRIMED + HEADS * b + n + 1)
                if not isinstance(b, int) or b > 0 or n >= 2:
                    vector.wait_ge(pv_done, PRIMED + HEADS * b + n - 1)
                vector.tensor_tensor(cT[:, n % 2, :], ps_qk[n % 2][:, 0:S + P], decay[:, n % 2, :],
                                     ALU.mult).then_inc(cT_ready, 1)

            def pair(b, q, n, before):
                if not isinstance(b, int) or b < B:
                    expo_of(b, n)
                if n:
                    cT_of(b, n - 1)
                elif before is not None:
                    cT_of(before, LAST)

            CH = 11

            def outputs(b, q):
                chain = Chain(vector, chain_s, PRIMED + CH * b)
                heads = lambda k: ps_o[q][k][:, 0:HEADS * VW].rearrange("p (h v) -> p h v", v=VW)
                vector.wait_ge(pv_done, PRIMED + HEADS * (b + 1))
                for k in range(TPB):
                    chain(vector.tensor_copy(norm[:, k, :], heads(k)[:, :, DH]))
                chain(vector.scalar_tensor_tensor(out=norm[:, :, :], in0=norm[:, :, :], scalar=-1.0, in1=norm[:, :, :],
                                                  op0=ALU.mult, op1=ALU.max))
                chain(vector.tensor_tensor(norm[:, :, :], norm[:, :, :], cols[:, 1, bass.ds(TPB * b, TPB), :], ALU.max))
                chain(vector.tensor_scalar(norm[:, :, :], norm[:, :, :], 1e-6, None, ALU.add))
                chain(vector.reciprocal(norm[:, :, :], norm[:, :, :]))
                vector.wait_ge(added, PRIMED + b)
                for k in range(TPB):
                    ins = vector.tensor_tensor(h[:, k, :].rearrange("p (h v) -> p h v", v=DH),
                                               heads(k)[:, :, 0:DH], bcast(norm[:, k, :], DH), ALU.mult)
                chain(ins)
                chain(vector.tensor_reduce(mean[:, :], by_head(h), AX.X, ALU.add))
                chain(vector.tensor_scalar(mean[:, :], mean[:, :], 1.0 / DH, None, ALU.mult))
                vector.tensor_tensor(by_head(h), by_head(h), bcast(mean[:, :], DH), ALU.subtract).then_inc(h_ready, 1)

            def variance(b, q):
                chain = Chain(vector, chain_s, PRIMED + CH * b + 9)
                vector.wait_ge(square_ready, PRIMED + b + 1)
                chain(vector.tensor_reduce(root[:, :], by_head(square), AX.X, ALU.add))
                vector.tensor_scalar(root[:, :], root[:, :], 1.0 / DH, 1e-6, ALU.mult, ALU.add).then_inc(var2_ready, 1)
                vector.sem_inc(chain_s, 1)

            def scale(b, q):
                vector.wait_ge(root_ready, PRIMED + b + 1)
                vector.tensor_tensor(by_head(h), by_head(h), bcast(root[:, :], DH), ALU.mult).then_inc(scaled_ready, 1)

            over_batches(vector, {}, pair, HEADS, {1: outputs, 2: variance, 3: scale})

        @block.tensor
        def _(pe):
            prime(pe, xT_done, gates_done, spread_done, qk_done, pv_done)
            ident = G.const("ident")
            pe.wait_ge(gates_summed, 1)
            pe.wait_ge(ctx_landed, 16)

            def turn_x(b):
                pe.wait_ge(xn_ready, PRIMED + b + 1)
                pe.wait_ge(xnT_ready, PRIMED + b)
                for c in range(DC):
                    for k in range(TPB):
                        ins = pe.transpose(ps_x[:, c * S + k * P:c * S + (k + 1) * P],
                                           xn[:, k, c * P:(c + 1) * P], ident)
                ins.then_inc(xT_done, 1)

            def gates(b):
                pe.wait_ge(xnT_ready, PRIMED + b + 1)
                pe.wait_ge(gates_ready, PRIMED + b)
                for i, source in enumerate((xnT, ctxT)):
                    for c in range(DC):
                        ins = pe.matmul(ps_g[0:GATE_COLS, 0:S], gates_w[:, i, c, :],
                                        source[:, bass.ds(b, 1), c, :].rearrange("p o s -> p (o s)"),
                                        start=i == 0 and c == 0, stop=i == 1 and c == DC - 1)
                ins.then_inc(gates_done, 1)

            turn_x(0)
            with pe.Fori(1, B) as b:
                turn_x(b)
                gates(b - 1)
            gates(B - 1)
            pe.wait_ge(rows_ready, 1)
            for i, rows in enumerate((ig, z)):
                for t in range(NT):
                    at = (NT * i + t) * HEADS
                    ins = pe.transpose(ps_c[:, at:at + HEADS], flat(rows[:, :, :])[:, t * P:(t + 1) * P],
                                       G.const("ident")[0:HEADS, 0:HEADS])
            ins.then_inc(cols_done, 1)
            pe.wait_ge(cols_ready, 1)
            pe.wait_ge(vaug_s, 2)

            def spread(b, n):
                if not isinstance(b, int) or b > 0 or n >= 2:
                    pe.wait_ge(expo_ready, PRIMED + HEADS * b + n - 1)
                pe.matmul(ps_m[n % 2][:, 0:S], G.const("pick")[:, n * P:(n + 1) * P],
                          m_rows[:, bass.ds(b, 1), :].rearrange("p o s -> p (o s)"),
                          start=True, stop=True).then_inc(spread_done, 1)

            def qk(b, q, n):
                if n == 0:
                    pe.wait_ge(kTm_ready, PRIMED + b + 1)
                if not isinstance(b, int) or b > 0 or n >= 2:
                    pe.wait_ge(cT_ready, PRIMED + HEADS * b + n - 1)
                for k, to, lo in ((0, 0, 0), (1, S, P)):
                    ins = pe.matmul(ps_qk[n % 2][:, to:to + S - lo], kTm[:, q, n % 2, n // 2, k * P:(k + 1) * P],
                                    xnT[:, bass.ds(b, 1), n // 2, lo:S].rearrange("p o s -> p (o s)"), start=True, stop=True)
                ins.then_inc(qk_done, 1)

            def values(b, q, n):
                pe.wait_ge(masked_ready, PRIMED + HEADS * b + n + 1)
                if n == 0 and (not isinstance(b, int) or b >= 2):
                    pe.wait_ge(h_ready, PRIMED + b - 1)
                at = n * VW
                for k, c, lo in ((0, 0, 0), (1, 0, P), (1, 1, S)):
                    ins = pe.matmul(ps_o[q][k][:, at:at + PVN], cT[:, n % 2, lo:lo + P],
                                    vaug[:, bass.ds(TPB * b + c, 1), at:at + PVN].rearrange("p o v -> p (o v)"),
                                    start=c == 0, stop=c == k)
                ins.then_inc(pv_done, 1)

            def pair(b, q, n, before):
                if not isinstance(b, int) or b < B:
                    if before is None and n == 0:
                        spread(b, 0)
                        qk(b, q, 0)
                    if n < LAST:
                        spread(b, n + 1)
                        qk(b, q, n + 1)
                    elif not (isinstance(b, int) and b == B - 1):
                        spread(b + 1, 0)
                        qk(b + 1, 1 - q, 0)
                if n:
                    values(b, q, n - 1)
                elif before is not None:
                    values(before, 1 - q, LAST)

            over_batches(pe, {}, pair, HEADS, {})


def l2_ffn(nc, G, a):
    X, PS, name = G.X, G.PS, "f2_"
    with ExitStack() as ctx:
        sb = lambda n, shape, dt=F32: ctx.enter_context(nc.sbuf_tensor(name + n, shape, dt))
        sem = semaphores(nc, ctx, name)
        w, mu = sb("w", [P, 3, DC, D]), sb("mu", [P, 2, DC])
        stats, moments = sb("stats", [P, NT, 6]), sb("moments", [P, NT, 2])
        var_eps, rstd = sb("var_eps", [P, NT]), sb("rstd", [P, NT])
        xn = sb("xn", [P, 2, TPB, D])
        xnT = sb("xnT", [P, 2, DC, S + 1])
        step_x = sb("step_x", [P, DC, S])
        mixed = sb("mixed", [P, 2, 2, DC, S])
        act_k = sb("act_k", [P, 2, DC, S])
        recep = sb("recep", [P, 2, TPB, D])
        out = sb("out", [P, TPB, D])
        landed, zero_ready = sem("landed"), sem("zero_ready")
        stats_done, var_ready, rstd_ready = sem("stats_done"), sem("var_ready"), sem("rstd_ready")
        chain_s, xn_ready, xT_done, xnT_ready = sem("chain"), sem("xn_ready"), sem("xT_done"), sem("xnT_ready")
        mixed_ready, k_done, relu_s, act_ready = sem("mixed_ready"), sem("k_done"), sem("relu"), sem("act_ready")
        r_done, recep_ready, v_done = sem("r_done"), sem("recep_ready"), sem("v_done")
        block = ctx.enter_context(nc.Block())

        @block.sync
        def _(sync):
            for i in range(3):
                sync.dma_start(w[:, i, :, :], a["w_mix"][i].rearrange("(c p) n -> p c n", p=P)).then_inc(landed, 16)
            sync.dma_start(mu[:, :, :].rearrange("p i c -> p (i c)"), a["mu_mix"]).then_inc(landed, 16)

        @block.gpsimd
        def _(pool):
            layer_norm_root(pool, G, rstd, var_eps, var_ready, rstd_ready)

        @block.scalar
        def _(act):
            prime(act, xnT_ready, relu_s, act_ready, recep_ready)
            act.wait_ge(zero_ready, 1)
            with act.Fori(0, B // 2) as pair:
                for q in range(2):
                    b = 2 * pair + q
                    act.wait_ge(xT_done, PRIMED + b + 1)
                    act.wait_ge(mixed_ready, PRIMED + 2 * b)
                    act.copy(xnT[:, q, :, 1:S + 1], PS[q][:, :].rearrange("p (c s) -> p c s", s=S)).then_inc(xnT_ready, 1)
                    act.wait_ge(k_done, PRIMED + b + 1)
                    act.wait_ge(v_done, PRIMED + b)
                    k = act_k[:, q, :, :].rearrange("p c s -> p (c s)")
                    act.activation(k, PS[2 + q][:, :], ACT.Relu).then_inc(relu_s, 1)
                    act.wait_ge(relu_s, PRIMED + b + 1)
                    act.activation(k, k, ACT.Square).then_inc(act_ready, 1)
                    act.wait_ge(r_done, PRIMED + b + 1)
                    act.activation(recep[:, q, :, :].rearrange("p k d -> p (k d)"), PS[4 + q][:, :],
                                   ACT.Sigmoid).then_inc(recep_ready, 1)

        @block.vector
        def _(vector):
            prime(vector, chain_s, xn_ready, mixed_ready)
            vector.memset(xnT[:, :, :, 0:1], 0.0).then_inc(zero_ready, 1)
            vector.wait_ge(landed, 16 * 4)
            layer_norm_stats(vector, X, stats, moments, var_eps, stats_done, var_ready)
            vector.wait_ge(rstd_ready, 1)
            CH = 3
            with vector.Fori(0, B // 2) as pair:
                for q in range(2):
                    b = 2 * pair + q
                    chain = Chain(vector, chain_s, PRIMED + b * CH)
                    vector.wait_ge(xT_done, PRIMED + b)
                    for k in range(TPB):
                        ins = vector.tensor_scalar(xn[:, q, k, :], X[:, TPB * b + k, :], moments[:, TPB * b + k, 0:1],
                                                   rstd[:, bass.ds(TPB * b + k, 1)], ALU.subtract, ALU.mult)
                    ins.then_inc(xn_ready, 1)
                    vector.wait_ge(xnT_ready, PRIMED + b + 1)
                    before, now = xnT[:, q, :, 0:S], xnT[:, q, :, 1:S + 1]
                    chain(vector.tensor_tensor(step_x[:, :, :], now, before, ALU.subtract))
                    vector.wait_ge(r_done, PRIMED + b)
                    for i in (1, 0):
                        for c in range(DC):
                            ins = vector.scalar_tensor_tensor(out=mixed[:, q, i, c, :], in0=step_x[:, c, :],
                                                              scalar=mu[:, i, c:c + 1], in1=before[:, c, :],
                                                              op0=ALU.mult, op1=ALU.add)
                        ins.then_inc(mixed_ready, 1)
                    vector.wait_ge(recep_ready, PRIMED + b + 1)
                    vector.wait_ge(v_done, PRIMED + b + 1)
                    chain(vector.tensor_tensor(out[:, :, :], PS[6 + q][:, :].rearrange("p (k d) -> p k d", d=D),
                                               recep[:, q, :, :], ALU.mult))
                    x = X[:, bass.ds(TPB * b, TPB), :]
                    chain(vector.tensor_tensor(x, x, out[:, :, :], ALU.add))

        @block.tensor
        def _(pe):
            prime(pe, xT_done, k_done, r_done, v_done)
            ident = G.const("ident")
            pe.wait_ge(landed, 16 * 4)
            with pe.Fori(0, B // 2) as pair:
                for q in range(2):
                    b = 2 * pair + q
                    pe.wait_ge(xn_ready, PRIMED + b + 1)
                    pe.wait_ge(xnT_ready, PRIMED + b)
                    for c in range(DC):
                        for k in range(TPB):
                            ins = pe.transpose(PS[q][:, c * S + k * P:c * S + (k + 1) * P],
                                               xn[:, q, k, c * P:(c + 1) * P], ident)
                    ins.then_inc(xT_done, 1)
                    pe.wait_ge(mixed_ready, PRIMED + 2 * b + 1)
                    pe.wait_ge(act_ready, PRIMED + b)
                    for m in range(DC):
                        for c in range(DC):
                            ins = pe.matmul(PS[2 + q][:, m * S:(m + 1) * S], w[:, 1, c, m * P:(m + 1) * P],
                                            mixed[:, q, 1, c, :], start=c == 0, stop=c == DC - 1)
                    ins.then_inc(k_done, 1)
                    pe.wait_ge(mixed_ready, PRIMED + 2 * b + 2)
                    pe.wait_ge(recep_ready, PRIMED + b)
                    for k in range(TPB):
                        for c in range(DC):
                            ins = pe.matmul(PS[4 + q][:, k * D:(k + 1) * D], mixed[:, q, 0, c, k * P:(k + 1) * P],
                                            w[:, 0, c, :], start=c == 0, stop=c == DC - 1)
                    ins.then_inc(r_done, 1)
                    pe.wait_ge(act_ready, PRIMED + b + 1)
                    pe.wait_ge(chain_s, PRIMED + 3 * b)
                    for k in range(TPB):
                        for c in range(DC):
                            ins = pe.matmul(PS[6 + q][:, k * D:(k + 1) * D], act_k[:, q, c, k * P:(k + 1) * P],
                                            w[:, 2, c, :], start=c == 0, stop=c == DC - 1)
                    ins.then_inc(v_done, 1)


class Shared:

    def __init__(self, X, consts, PS):
        self.X, self.consts, self.PS = X, consts, PS

    def const(self, name):
        lo, hi = CONST[name]
        return self.consts[:, lo:hi]

    def mhalf(self, n):
        return self.const("half")[:, 0:n]


KEPT = {"att0": (("w_att0", [3, DC, D]), ("wk_att0", [2, DC, P]), ("wv_att0", [DC, 64]), ("gain_att0", [DC])),
        "mha1": (("w_mha1", [4, DC, D]), ("v_mha1", [2 * DC + 2 * D])),
        "mlstm": (("gates_2", [3, DC, GATE_COLS]), ("gate_bias_2", [1]), ("out_gain_2", [D])),
        "mha3": (("w_mha3", [4, DC, D]), ("v_mha3", [2 * DC + 2 * D]))}


def build(nc, a, out):
    x_rows = a["x"].rearrange("b (k p) d -> p (b k) d", p=P)
    out_rows = out.rearrange("b (k p) d -> p (b k) d", p=P)
    with ExitStack() as ctx:
        X = ctx.enter_context(nc.sbuf_tensor("X", [P, NT, D], F32))
        consts = ctx.enter_context(nc.sbuf_tensor("consts", [P, CONSTS], F32))
        PS = [ctx.enter_context(nc.psum_tensor(f"bank{i}", [P, 512], F32)) for i in range(8)]
        x_landed = ctx.enter_context(nc.semaphore("x_landed"))
        stored = ctx.enter_context(nc.semaphore("stored"))
        G = Shared(X, consts, PS)
        G.context = ctx.enter_context(nc.sbuf_tensor("context", [P, NT, D], F32))
        G.context_landed = ctx.enter_context(nc.semaphore("context_landed"))
        G.weights, G.landed = {}, {}
        for layer, parts in KEPT.items():
            G.landed[layer] = ctx.enter_context(nc.semaphore(f"weights_{layer}_landed"))
            for n, shape in parts:
                G.weights[n] = ctx.enter_context(nc.sbuf_tensor("kept_" + n, [P] + shape, F32))
        G.rows = nc.dram_tensor("rows", ((TILES + 1) * R, D), F32, kind="Internal").ap()
        zeroed = ctx.enter_context(nc.semaphore("zeroed"))
        G.rows_filled = ctx.enter_context(nc.semaphore("rows_filled"))
        zeros = ctx.enter_context(nc.sbuf_tensor("zeros", [P, D], F32))
        with nc.Block() as block:
            @block.vector
            def _(vector):
                vector.memset(zeros[:, :], 0.0).then_inc(zeroed, 1)

            def keep(eng, layer):
                for n, shape in KEPT[layer]:
                    to, source = G.weights[n], a[n]
                    if len(shape) == 3:
                        to, source = to[:, :, :, :].rearrange("p i c n -> p (i c) n"), source.rearrange("i (c p) n -> p (i c) n", p=P)
                    elif len(shape) == 2:
                        to, source = to[:, :, :], source.rearrange("(c p) n -> p c n", p=P)
                    else:
                        to = to[:, :]
                    eng.dma_start(to, source).then_inc(G.landed[layer], 16)

            @block.scalar
            def _(act):
                act.dma_start(G.context[:, :, :], a["ctx"].rearrange("b (k p) d -> p (b k) d", p=P)).then_inc(G.context_landed, 16)
                act.wait_ge(zeroed, 1)
                act.dma_start(G.rows.rearrange("(n p) d -> p n d", p=P),
                              zeros[:, :].unsqueeze(1).to_broadcast([P, TILES + 1, D])).then_inc(G.rows_filled, 16)
                keep(act, "mha1")
                keep(act, "mlstm")
                keep(act, "mha3")

            @block.sync
            def _(sync):
                sync.dma_start(X[:, :, :], x_rows).then_inc(x_landed, 16)
                sync.dma_start(consts[:, :], a["consts"]).then_inc(x_landed, 16)
                keep(sync, "att0")
                sync.wait_ge(x_landed, 32)

        for layer in LAYERS:
            layer(nc, G, a)

        with nc.Block() as block:
            @block.sync
            def _(sync):
                sync.dma_start(out_rows, X[:, :, :]).then_inc(stored, 16)
                sync.wait_ge(stored, 16)
                sync.wait_ge(G.rows_filled, 16)
                sync.wait_ge(G.context_landed, 16)
                for layer, parts in KEPT.items():
                    sync.wait_ge(G.landed[layer], 16 * len(parts))


LAYERS = (
    l0_attention,
    l0_ffn,
    lambda nc, G, a: mha_block(nc, G, "mha1", a["ctxT"]),
    l1_ffn,
    l2_attention,
    l2_ffn,
    lambda nc, G, a: mha_block(nc, G, "mha3", a["ctxT"]),
    l3_ffn,
)


def constants():
    c = np.zeros((P, CONSTS), np.float32)

    def put(name, value):
        lo, hi = CONST[name]
        c[:, lo:hi] = value

    p, j = np.arange(P)[:, None], np.arange(P)[None, :]
    put("ident", p == j)
    put("before", p < j)
    put("upto", p <= j)
    put("ones", 1.0)
    put("restart", np.broadcast_to(j % NT != 0, (P, P)))
    put("head", p // 16 == np.arange(8)[None, :])
    put("iota", np.broadcast_to(np.arange(8)[None, :], (P, 8)))
    put("half", -0.5)
    put("even", p < P // 2)
    put("odd", p >= P // 2)
    put("even8", (p < P // 2) / 8)
    put("odd8", (p >= P // 2) / 8)
    put("pick", (p == np.arange(4 * P)[None, :] // P))
    HEAD = 64
    scale = np.float32(10000.0) ** (np.float32(2.0 / HEAD) * np.arange(HEAD // 2, dtype=np.float32))
    row = np.arange(P) % HEAD
    sign = np.where(row < HEAD // 2, np.float32(-1), np.float32(1))[:, None]
    for q, at in (("q", S), ("k", 0)):
        angle = np.arange(at, at + S, dtype=np.float32)[None, :] / scale[row % (HEAD // 2)][:, None]
        by = np.float32(-(HEAD ** -0.5) if q == "q" else 1.0)
        put("cos" + q, np.cos(angle) * by)
        put("sin" + q, np.sin(angle) * sign * by)
    return c


def kernel(**inputs):
    import concourse.bacc as bacc
    from concourse.bass_utils import run_bass_kernel_spmd

    i = {k: np.asarray(v) for k, v in inputs.items()}
    T = lambda a: np.ascontiguousarray(a.T)
    rows = lambda a: np.broadcast_to(a.reshape(1, -1), (P, a.size))
    chunks = lambda a: T(a.reshape(-1, P))
    cat = lambda *a: np.ascontiguousarray(np.concatenate(a, axis=1))
    laid = {"x": i["x"], "consts": constants(), "ctx": i["ctx_1024"],
            "ctxT": np.ascontiguousarray(i["ctx_1024"].transpose(0, 2, 1))}
    for n in "13":
        laid["w_mha" + n] = np.stack([T(i[f"L{n}_xattn_W{m}"]) for m in "qkvo"])
        laid["v_mha" + n] = cat(chunks(i[f"L{n}_xattn_bq"]), chunks(i[f"L{n}_xattn_bk"]),
                                rows(i[f"L{n}_xattn_bv"]), rows(i[f"L{n}_xattn_bo"]))
    hidden_chunks = lambda a: np.ascontiguousarray(a.reshape(E * HC, P).T)
    laid["w_route0"], laid["b_route0"] = i["L0_ffn_Wg"], np.zeros((P, E), np.float32)
    laid["w_route1"], laid["b_route1"] = i["L1_ffn_gate_W"], rows(i["L1_ffn_gate_b"])
    laid["w_route3"], laid["b_route3"] = T(i["L3_ffn_router_w"]), rows(i["L3_ffn_router_b"])
    for n in "01":
        laid["W1_" + n], laid["W2_" + n] = i[f"L{n}_ffn_W1"], i[f"L{n}_ffn_W2"]
        laid["b1_" + n], laid["b2_" + n] = hidden_chunks(i[f"L{n}_ffn_b1"]), rows(i[f"L{n}_ffn_b2"])
    laid["W_3"], laid["V_3"], laid["Wout_3"] = i["L3_ffn_W"], i["L3_ffn_V"], i["L3_ffn_W_out"]
    laid["affine1"] = cat(rows(i["L1_ffn_ln_gamma"]), rows(i["L1_ffn_ln_beta"]))
    wq = i["L0_xattn_q_w"].transpose(1, 0, 2)
    wk, wv = i["L0_xattn_kv_w"][0, 0], i["L0_xattn_kv_w"][1, 0]
    swap = lambda w: np.concatenate([w[..., 32:], w[..., :32]], axis=-1)
    laid["w_att0"] = np.stack([wq.reshape(D, D), swap(wq).reshape(D, D), i["L0_xattn_out_w"].reshape(D, D)])
    laid["wk_att0"] = np.stack([cat(wk, wk), cat(swap(wk), swap(wk))])
    laid["wv_att0"] = wv
    laid["gain_att0"] = chunks(i["L0_xattn_rms_scale"])
    laid["kept"] = i["mask_BxS2_bk0"].reshape(1, -1)
    gates = np.zeros((3, D, GATE_COLS), np.float32)
    gates[:, :, 0:4] = i["L2_xattn_ig_kernel"].reshape(3, D, 4)
    gates[:, :, FORGET:FORGET + 4] = i["L2_xattn_fg_kernel"].reshape(3, D, 4)
    laid["gates_2"], laid["gate_bias_2"] = gates, np.zeros((P, 1), np.float32)
    laid["gate_bias_2"][0:4, 0], laid["gate_bias_2"][FORGET:FORGET + 4, 0] = i["L2_xattn_ig_bias"], i["L2_xattn_fg_bias"]
    laid["out_gain_2"] = rows(i["L2_xattn_outnorm_weight"])
    laid["w_mix"] = np.stack([T(i["L2_ffn_W_" + m]) for m in "rkv"])
    laid["mu_mix"] = cat(chunks(i["L2_ffn_mu_r"]), chunks(i["L2_ffn_mu_k"]))
    nc = bacc.Bacc("TRN2", target_bir_lowering=False, num_devices=1)
    aps = {}
    for name, value in laid.items():
        laid[name] = np.ascontiguousarray(value)
        aps[name] = nc.dram_tensor("in_" + name, value.shape, mybir.dt.from_np(value.dtype), kind="ExternalInput").ap()
    out = nc.dram_tensor("out", (B, S, D), F32, kind="ExternalOutput").ap()
    build(nc, aps, out)
    r = run_bass_kernel_spmd(nc, [{"in_" + name: value for name, value in laid.items()}], core_ids=[0])
    return r.results[0]["out"]
```

```python
from contextlib import ExitStack

import numpy as np

import concourse.bass as bass
from concourse import mybir

F32 = mybir.dt.float32
BF16 = mybir.dt.bfloat16
I32 = mybir.dt.int32
U32 = mybir.dt.uint32
U8 = mybir.dt.uint8
ALU = mybir.AluOpType
ACT = mybir.ActivationFunctionType
AX = mybir.AxisListType

P = 128
B, S, D = 8, 256, 256
TPB = S // P
NT = B * TPB
DC = D // P
LN_EPS = 1e-5
E, H = 8, 512
HC = H // P
R = 128
TILES = 2 * B * S // R + E
CAPACITY = 512

CONST = {}
_at = 0
for _name, _width in (("ident", P), ("before", P), ("ones", P), ("upto", P), ("restart", P), ("head", 8),
                      ("iota", 8), ("even", 1), ("odd", 1), ("even8", 1), ("odd8", 1), ("pick", 4 * P), ("half", 16), ("cosq", S), ("sinq", S), ("cosk", S), ("sink", S)):
    CONST[_name] = (_at, _at + _width)
    _at += _width
CONSTS = _at


PRIMED = 1


def prime(eng, *sems):
    for sem in sems:
        eng.sem_inc(sem, PRIMED)


def semaphores(nc, ctx, name):
    made = []

    def clear():
        nc.clear_and_free_semaphores(made)
        nc.all_engine_barrier(sem_only=True)

    ctx.callback(clear)

    def sem(n):
        made.append(nc.alloc_semaphore(name + n))
        return made[-1]

    return sem


class Chain:

    def __init__(self, eng, sem, base=0):
        self.eng, self.sem, self.base, self.n = eng, sem, base, 0

    def __call__(self, ins):
        self.n += 1
        ins.then_inc(self.sem, 1)
        self.eng.wait_ge(self.sem, self.base + self.n)


def bcast(ap, n):
    return ap.unsqueeze(2).to_broadcast([ap.shape[0], ap.shape[1], n])


def layer_norm_stats(vector, X, stats, moments, var_eps, stats_done, ready, eps=LN_EPS):
    for t in range(NT):
        vector.bn_stats(stats[:, t, :], X[:, t, :]).then_inc(stats_done, 1)
    for t in range(NT):
        vector.wait_ge(stats_done, t + 1)
        vector.bn_aggr(moments[:, t, :], stats[:, t, :]).then_inc(stats_done, 1)
    vector.wait_ge(stats_done, 2 * NT)
    vector.tensor_scalar(var_eps[:, :], moments[:, :, 1], eps, None, ALU.add).then_inc(ready, 1)


def layer_norm_root(pool, G, rstd, var_eps, var_ready, rstd_ready):
    pool.wait_ge(var_ready, 1)
    pool.tensor_tensor(rstd[:, :], var_eps[:, :], G.mhalf(NT), ALU.pow).then_inc(rstd_ready, 1)


def over_batches(eng, front, pair, pairs, finish):
    def body(b, q, before, after):
        for g in range(pairs):
            pair(b, q, g, before)
            if before is not None and g in finish:
                finish[g](before, 1 - q)
            if after is not None and g in front:
                front[g](after, 1 - q)

    for piece in front.values():
        piece(0, 0)
    body(0, 0, None, 1)
    with eng.Fori(0, B // 2 - 1) as two:
        for q in (1, 0):
            b = 2 * two + 2 - q
            body(b, q, b - 1, b + 1)
    body(B - 1, 1, B - 2, None)
    pair(B, 0, 0, B - 1)
    for piece in finish.values():
        piece(B - 1, 1)


def mha_block(nc, G, layer, ctx_t):
    HEADS, DH = 16, D // 16
    PAIRS = HEADS // 2
    GB = TPB * PAIRS
    VW = DH + 1
    PVN = 6 * VW
    VCOLS = (HEADS - 1) * VW + PVN
    STACK_Q = (0, 0, 0, 1, 1, 2)
    ROWS = 6 * DH
    LOADS = len(STACK_Q) + 3
    X, PS, name = G.X, G.PS, layer + "_"
    w, vec, w_landed = G.weights["w_" + layer], G.weights["v_" + layer], G.landed[layer]
    with ExitStack() as ctx:
        sb = lambda n, shape, dt=F32: ctx.enter_context(nc.sbuf_tensor(name + n, shape, dt))
        sem = semaphores(nc, ctx, name)
        nbq = sb("nbq", [P, DC])
        ctxT = sb("ctxT", [P, DC, S])
        stats, moments, var_eps, rstd = G.stats, G.moments, G.var_eps, sb("rstd", [P, NT])
        xn = sb("xn", [P, TPB, D])
        xnT = sb("xnT", [P, DC, S])
        qT, kT = sb("qT", [P, DC, S]), sb("kT", [P, DC, S])
        rest = sb("rest", [P, DC, S])
        pieces = sb("pieces", [P, 2, 3, DC, S], BF16)
        stack = sb("stack", [ROWS, 2, 2, HEADS, S], BF16)
        pieces_dram = nc.dram_tensor(name + "pieces_dram", (2, 3, D, S), BF16, kind="Internal").ap()
        vaug = sb("vaug", [P, 2, TPB, VCOLS])
        nmax = sb("nmax", [P, 2, 2])
        prob = sb("prob", [P, 2, 2, S])
        probT = sb("probT", [P, 2, 4, P])
        rsum = sb("rsum", [P, TPB, HEADS])
        enc, encT = sb("enc", [P, TPB, D]), sb("encT", [P, DC, S])
        ctx_landed = sem("ctx_landed")
        stats_done, recip_s, sum_s = sem("stats_done"), sem("reciprocals"), sem("sums")
        split_s, pieces_ready, written, stack_landed = sem("split_steps"), sem("pieces_ready"), [sem("q_written"), sem("k_written")], sem("stack_landed")
        var_ready, rstd_ready, xn_ready = sem("var_ready"), sem("rstd_ready"), sem("xn_ready")
        xT_done, xnT_ready = sem("xT_done"), sem("xnT_ready")
        q_done, q_ready = sem("q_done"), sem("q_ready")
        k_done, k_ready = sem("k_done"), sem("k_ready")
        v_done, v_ready = sem("v_done"), sem("v_ready")
        score_done, max_ready, prob_ready = sem("score_done"), sem("max_ready"), sem("prob_ready")
        probT_done, probT_ready, pv_done = sem("probT_done"), sem("probT_ready"), sem("pv_done")
        enc_ready, encT_done, encT_ready = sem("enc_ready"), sem("encT_done"), sem("encT_ready")
        out_done, added, nbq_ready, ones_ready = sem("out_done"), sem("added"), sem("nbq_ready"), sem("ones_ready")
        bq, bk = vec[:, 0:DC], vec[:, DC:2 * DC]
        bv, bo = vec[:, 2 * DC:2 * DC + D], vec[:, 2 * DC + D:2 * DC + 2 * D]
        ps_x, ps_q = PS[0], PS[1]
        ps_s, ps_t, ps_o = [PS[2], PS[3]], [PS[4], PS[5]], [PS[6], PS[7]]
        LAST = GB - 1
        block = ctx.enter_context(nc.Block())

        @block.sync
        def _(sync):
            def load(b, q):
                sync.wait_ge(v_done, PRIMED + b)
                sync.dma_start(ctxT[:, :, :], ctx_t[b].rearrange("(c p) n -> p c n", p=P)).then_inc(ctx_landed, 16)
                sync.wait_ge(stack_landed, PRIMED + 16 * LOADS * b)
                for n, i in enumerate((1, 0)):
                    sync.wait_ge(pieces_ready, PRIMED + 2 * b + n + 1)
                    sync.dma_start(pieces_dram[i].rearrange("j (c p) s -> p (j c) s", p=P),
                                   pieces[:, i, :, :, :].rearrange("p j c s -> p (j c) s")).then_inc(written[i], 16)
                if not isinstance(b, int) or b >= 2:
                    sync.wait_ge(score_done, PRIMED + GB * (b - 1))
                for i in (1, 0):
                    sync.wait_ge(written[i], PRIMED + 16 * (b + 1))
                    rows = pieces_dram[i].rearrange("j (e h) s -> (j e) h s", h=HEADS)
                    at = 0
                    for first, count in (((j, 1) for j in STACK_Q) if i == 0 else ((0, 3), (0, 2), (0, 1))):
                        sync.dma_start(stack[at:at + count * DH, q, i, :, :],
                                       rows[first * DH:(first + count) * DH]).then_inc(stack_landed, 16)
                        at += count * DH

            prime(sync, stack_landed, *written)
            load(0, 0)
            load(1, 1)
            with sync.Fori(1, B // 2) as two:
                for q in range(2):
                    load(2 * two + q, q)

        @block.gpsimd
        def _(pool):
            prime(pool, split_s, pieces_ready)
            layer_norm_root(pool, G, rstd, var_eps, var_ready, rstd_ready)
            with pool.Fori(0, B) as b:
                step = Chain(pool, split_s, PRIMED + 6 * b)
                flat = lambda t: t.rearrange("p c s -> p (c s)")
                for n, (i, source, ready) in enumerate(((1, kT, k_ready), (0, qT, q_ready))):
                    pool.wait_ge(ready, PRIMED + b + 1)
                    pool.wait_ge(written[i], PRIMED + 16 * b)
                    piece = lambda j: flat(pieces[:, i, j, :, :])
                    one = G.const("ones")[:, 0:1].to_broadcast([P, DC * S])
                    step(pool.tensor_tensor(piece(0), flat(source[:, :, :]), one, ALU.mult))
                    step(pool.tensor_tensor(flat(rest[:, :, :]), flat(source[:, :, :]), piece(0), ALU.subtract))
                    step(pool.tensor_tensor(piece(1), flat(rest[:, :, :]), one, ALU.mult))
                    pool.tensor_tensor(piece(2), flat(rest[:, :, :]), piece(1), ALU.subtract).then_inc(pieces_ready, 1)
                    pool.wait_ge(pieces_ready, PRIMED + 2 * b + n + 1)

        @block.scalar
        def _(act):
            prime(act, q_ready, prob_ready)
            act.wait_ge(w_landed, 16 * 2)
            act.mul(nbq[:, :], bq, -0.25).then_inc(nbq_ready, 1)
            act.wait_ge(nbq_ready, 1)

            def queries(b, q):
                act.wait_ge(q_done, PRIMED + b + 1)
                act.wait_ge(pieces_ready, PRIMED + 2 * b)
                for c in range(DC):
                    ins = act.activation(qT[:, c, :], ps_q[:, c * S:(c + 1) * S], ACT.Identity,
                                         bias=nbq[:, c:c + 1], scale=-0.25)
                ins.then_inc(q_ready, 1)

            def exponents(b, q, g, before):
                if isinstance(b, int) and b == B:
                    return
                act.wait_ge(max_ready, PRIMED + GB * b + g + 1)
                if before is not None or g >= 2:
                    act.wait_ge(probT_done, PRIMED + GB * b + g - 1)
                for i in range(2):
                    ins = act.activation(prob[:, g % 2, i, :], ps_s[g % 2][:, i * S:(i + 1) * S], ACT.Exp,
                                         bias=nmax[:, g % 2, i:i + 1], scale=-1.0)
                ins.then_inc(prob_ready, 1)

            over_batches(act, {6: queries}, exponents, GB, {})

        @block.vector
        def _(vector):
            prime(vector, recip_s, sum_s, xn_ready, xnT_ready, k_ready, v_ready, max_ready, probT_ready, enc_ready, encT_ready, added)
            if G.moments_made:
                vector.sem_inc(var_ready, 1)
            else:
                layer_norm_stats(vector, X, stats, moments, var_eps, stats_done, var_ready)
            G.moments_made = False
            vector.memset(vaug[:, :, :, :], 1.0).then_inc(ones_ready, 1)
            vector.wait_ge(w_landed, 16 * 2)
            vector.wait_ge(ones_ready, 1)

            def normalize(b, q):
                vector.wait_ge(xT_done, PRIMED + b)
                for k in range(TPB):
                    t = TPB * b + k
                    ins = vector.tensor_scalar(xn[:, k, :], X[:, bass.ds(t, 1), :].rearrange("p o d -> p (o d)"),
                                               moments[:, bass.ds(t, 1), 0], rstd[:, bass.ds(t, 1)],
                                               ALU.subtract, ALU.mult)
                ins.then_inc(xn_ready, 1)

            def x_turned(b, q):
                vector.wait_ge(xT_done, PRIMED + b + 1)
                vector.wait_ge(q_done, PRIMED + b)
                vector.tensor_copy(xnT[:, :, :].rearrange("p c s -> p (c s)"), ps_x[:, :]).then_inc(xnT_ready, 1)

            def keys(b, q):
                vector.wait_ge(k_done, PRIMED + b + 1)
                vector.wait_ge(pieces_ready, PRIMED + 2 * b)
                for c in range(DC):
                    ins = vector.tensor_scalar(kT[:, c, :], ps_q[:, c * S:(c + 1) * S], bk[:, c:c + 1], None, ALU.add)
                ins.then_inc(k_ready, 1)

            def keys_of_later(b, q):
                if not (isinstance(b, int) and b == 0):
                    keys(b, q)

            def values(b, q):
                vector.wait_ge(v_done, PRIMED + b + 1)
                if not isinstance(b, int) or b >= 2:
                    vector.wait_ge(pv_done, PRIMED + GB * (b - 1))
                for k in range(TPB):
                    ins = vector.tensor_tensor(
                        vaug[:, q, k, 0:HEADS * VW].rearrange("p (h v) -> p h v", v=VW)[:, :, 0:DH],
                        ps_q[:, k * D:(k + 1) * D].rearrange("p (h v) -> p h v", v=DH),
                        bv.rearrange("p (h v) -> p h v", v=DH), ALU.add)
                ins.then_inc(v_ready, 1)

            def turn_probabilities(b, g):
                vector.wait_ge(probT_done, PRIMED + GB * b + g + 1)
                if not isinstance(b, int) or b > 0 or g >= 2:
                    vector.wait_ge(pv_done, PRIMED + GB * b + g - 1)
                vector.tensor_copy(probT[:, g % 2, :, :].rearrange("p a t -> p (a t)"),
                                   ps_t[g % 2][:, :]).then_inc(probT_ready, 1)

            def encode(b, k):
                vector.wait_ge(pv_done, PRIMED + GB * b + PAIRS * (k + 1))
                o = ps_o[k][:, 0:HEADS * VW].rearrange("p (h v) -> p h v", v=VW)
                vector.reciprocal(rsum[:, k, :], o[:, :, DH]).then_inc(recip_s, 1)
                vector.wait_ge(encT_done, PRIMED + b)
                vector.wait_ge(recip_s, PRIMED + TPB * b + k + 1)
                vector.tensor_tensor(enc[:, k, :].rearrange("p (h v) -> p h v", v=DH), o[:, :, 0:DH],
                                     bcast(rsum[:, k, :], DH), ALU.mult).then_inc(enc_ready, 1)

            def maxima(b, g):
                vector.wait_ge(score_done, PRIMED + GB * b + g + 1)
                if not isinstance(b, int) or b > 0 or g >= 2:
                    vector.wait_ge(prob_ready, PRIMED + GB * b + g - 1)
                vector.tensor_reduce(nmax[:, g % 2, :], ps_s[g % 2][:, :].rearrange("p (h s) -> p h s", s=S),
                                     AX.X, ALU.min).then_inc(max_ready, 1)

            def pair(b, q, g, before):
                if isinstance(b, int) and b == B:
                    return
                if before is None and g == 0:
                    maxima(b, 0)
                if g < LAST:
                    maxima(b, g + 1)
                elif not (isinstance(b, int) and b == B - 1):
                    maxima(b + 1, 0)
                turn_probabilities(b, g)
                if g == PAIRS + 1:
                    encode(b, 0)

            def enc_turned(b, q):
                vector.wait_ge(encT_done, PRIMED + b + 1)
                vector.wait_ge(out_done, PRIMED + b)
                vector.tensor_copy(encT[:, :, :].rearrange("p c s -> p (c s)"), ps_x[:, :]).then_inc(encT_ready, 1)

            def add(b, q):
                vector.wait_ge(out_done, PRIMED + b + 1)
                x = X[:, bass.ds(TPB * b, TPB), :]
                vector.tensor_tensor(x, ps_q[:, :].rearrange("p (k d) -> p k d", d=D), x, ALU.add).then_inc(sum_s, 1)
                vector.wait_ge(sum_s, PRIMED + b + 1)
                vector.tensor_tensor(x, x, bo.unsqueeze(1).to_broadcast([P, TPB, D]), ALU.add).then_inc(added, 1)

            keys(0, 0)
            vector.wait_ge(rstd_ready, 1)
            over_batches(vector, {0: normalize, 2: keys_of_later, 3: x_turned, 7: values}, pair, GB,
                         {1: lambda b, q: encode(b, 1), 8: enc_turned, 10: add})

        @block.tensor
        def _(pe):
            prime(pe, xT_done, q_done, k_done, v_done, score_done, probT_done, pv_done, encT_done, out_done)
            ident = G.const("ident")
            pe.wait_ge(w_landed, 16 * 2)

            def turn(source, to):
                for c in range(DC):
                    for k in range(TPB):
                        ins = pe.transpose(to[:, c * S + k * P:c * S + (k + 1) * P],
                                           source[:, k, c * P:(c + 1) * P], ident)
                return ins

            def turn_x(b, q):
                pe.wait_ge(xn_ready, PRIMED + b + 1)
                if not isinstance(b, int) or b >= 2:
                    pe.wait_ge(encT_ready, PRIMED + b - 2)
                turn(xn, ps_x).then_inc(xT_done, 1)

            def project(i, source):
                for m in range(DC):
                    for c in range(DC):
                        ins = pe.matmul(ps_q[:, m * S:(m + 1) * S], w[:, i, c, m * P:(m + 1) * P], source[:, c, :],
                                        start=c == 0, stop=c == DC - 1)
                return ins

            def project_k(b, q):
                if not isinstance(b, int) or b >= 2:
                    pe.wait_ge(added, PRIMED + b - 2)
                pe.wait_ge(ctx_landed, 16 * (b + 1))
                project(1, ctxT).then_inc(k_done, 1)

            def project_q(b, q):
                pe.wait_ge(xnT_ready, PRIMED + b + 1)
                pe.wait_ge(k_ready, PRIMED + b + 1)
                project(0, xnT).then_inc(q_done, 1)

            def project_v(b, q):
                pe.wait_ge(q_ready, PRIMED + b + 1)
                for k in range(TPB):
                    for c in range(DC):
                        ins = pe.matmul(ps_q[:, k * D:(k + 1) * D], ctxT[:, c, k * P:(k + 1) * P], w[:, 2, c, :],
                                        start=c == 0, stop=c == DC - 1)
                ins.then_inc(v_done, 1)

            def scores(b, q, g):
                k, j = divmod(g, PAIRS)
                if g == 0:
                    pe.wait_ge(stack_landed, PRIMED + 16 * LOADS * (b + 1))
                if not isinstance(b, int) or b > 0 or g >= 2:
                    pe.wait_ge(prob_ready, PRIMED + GB * b + g - 1)
                for i in range(2):
                    ins = pe.matmul(ps_s[g % 2][:, i * S:(i + 1) * S], stack[:, q, 0, 2 * j + i, k * P:(k + 1) * P],
                                    stack[:, q, 1, 2 * j + i, :], start=True, stop=True)
                ins.then_inc(score_done, 1)

            def transposes(b, g):
                pe.wait_ge(prob_ready, PRIMED + GB * b + g + 1)
                if not isinstance(b, int) or b > 0 or g >= 2:
                    pe.wait_ge(probT_ready, PRIMED + GB * b + g - 1)
                for i in range(2):
                    for c in range(TPB):
                        ins = pe.transpose(ps_t[g % 2][:, (2 * i + c) * P:(2 * i + c + 1) * P],
                                           prob[:, g % 2, i, c * P:(c + 1) * P], ident)
                ins.then_inc(probT_done, 1)

            def values(b, q, g):
                k, j = divmod(g, PAIRS)
                pe.wait_ge(probT_ready, PRIMED + GB * b + g + 1)
                if j == 0 and (not isinstance(b, int) or b > 0):
                    pe.wait_ge(enc_ready, PRIMED + TPB * (b - 1) + k + 1)
                if g == 0:
                    pe.wait_ge(v_ready, PRIMED + b + 1)
                for i in range(2):
                    at = (2 * j + i) * VW
                    for c in range(TPB):
                        ins = pe.matmul(ps_o[k][:, at:at + PVN], probT[:, g % 2, 2 * i + c, :],
                                        vaug[:, q, c, at:at + PVN], start=c == 0, stop=c == TPB - 1)
                ins.then_inc(pv_done, 1)

            def pair(b, q, g, before):
                if not isinstance(b, int) or b < B:
                    if before is None and g == 0:
                        scores(b, q, 0)
                        scores(b, q, 1)
                    transposes(b, g)
                    if g + 2 < GB:
                        scores(b, q, g + 2)
                    elif not (isinstance(b, int) and b == B - 1):
                        scores(b + 1, 1 - q, g + 2 - GB)
                if g:
                    values(b, q, g - 1)
                elif before is not None:
                    values(before, 1 - q, LAST)

            def fronts(b):
                return min(b + 3, B) if isinstance(b, int) else b + 3

            def turn_enc(b, q):
                pe.wait_ge(enc_ready, PRIMED + TPB * (b + 1))
                pe.wait_ge(xnT_ready, PRIMED + fronts(b))
                turn(enc, ps_x).then_inc(encT_done, 1)

            def project_out(b, q):
                pe.wait_ge(encT_ready, PRIMED + b + 1)
                pe.wait_ge(v_ready, PRIMED + fronts(b))
                for k in range(TPB):
                    for c in range(DC):
                        ins = pe.matmul(ps_q[:, k * D:(k + 1) * D], encT[:, c, k * P:(k + 1) * P], w[:, 3, c, :],
                                        start=c == 0, stop=c == DC - 1)
                ins.then_inc(out_done, 1)

            over_batches(pe, {1: project_k, 2: turn_x, 4: project_q, 6: project_v}, pair, GB, {7: turn_enc, 9: project_out})


class Routing:

    def __init__(self, nc, ctx, name):
        sb = lambda n, shape, dt=F32: ctx.enter_context(nc.sbuf_tensor(name + n, shape, dt))
        self.xn = sb("xn", [P, NT, D])
        self.slots = sb("slots", [P, 2, NT], U32)
        self.share = sb("share", [P, 2, NT])
        self.bounds = sb("bounds", [P, 2, 2, E], I32)
        self.took = [sb("took0", [P, NT, D]), sb("took1", [P, NT, D])]


def scatter_rows(pool, G, source, slots, ready, scattered):
    pool.wait_ge(ready, 1)
    pool.wait_ge(G.rows_filled, 16)
    for t in range(NT):
        pool.indirect_dma_start(G.rows[:, :], bass.IndirectOffsetOnAxis(slots[:, t:t + 1], 0),
                                source[:, t, :], None).then_inc(scattered, 16)


def router_block(nc, G, name, rt, w_router, bias, joint, over_all, capacity):
    X, PS = G.X, G.PS
    with ExitStack() as ctx:
        sb = lambda n, shape, dt=F32: ctx.enter_context(nc.sbuf_tensor(name + n, shape, dt))
        sem = semaphores(nc, ctx, name)
        w, bias_sb = sb("w", [P, DC, E]), sb("bias", [P, E])
        stats, moments = sb("stats", [P, NT, 6]), sb("moments", [P, NT, 2])
        var_eps, rstd = sb("var_eps", [P, NT]), sb("rstd", [P, NT])
        xT = sb("xT", [P, 2, DC, P])
        logits, best = sb("logits", [P, NT, E]), sb("best", [P, NT, 8])
        best_at = sb("best_at", [P, NT, 8], U32)
        weight, total = sb("weight", [P, NT, 8]), sb("total", [P, NT])
        chosen_at = sb("chosen_at", [P, 2, NT])
        chosen = sb("chosen", [P, 3, NT, E])
        tile_sum, running = sb("tile_sum", [P, E, NT]), sb("running", [P, E, NT])
        rank = sb("rank", [P, NT, E])
        picked = sb("picked", [P, NT, E])
        tiles, tiles_i, end = sb("tiles", [P, E]), sb("tiles_i", [P, E], I32), sb("end", [P, E])
        first = sb("first", [P, E])
        slot_f, keep = sb("slot_f", [P, NT]), sb("keep", [P, NT])
        landed, stats_done, chain_s = sem("landed"), sem("stats_done"), sem("chain")
        var_ready, rstd_ready, xn_ready = sem("var_ready"), sem("rstd_ready"), sem("xn_ready")
        xT_done, xT_ready, logits_done = sem("xT_done"), sem("xT_ready"), sem("logits_done")
        shifted, weight_ready = sem("shifted"), sem("weight_ready")
        chosen_ready, counted = sem("chosen_ready"), sem("counted")
        slots_ready, scattered = sem("slots_ready"), sem("scattered")
        ps_logits, ps_within, ps_tile = PS[2], PS[3], PS[4]
        dispatches = [(2, (0, 1))] if joint else [(0, (0,)), (1, (1,))]
        block = ctx.enter_context(nc.Block())

        @block.sync
        def _(sync):
            sync.dma_start(w[:, :, :], w_router.rearrange("(c p) e -> p c e", p=P)).then_inc(landed, 16)
            sync.dma_start(bias_sb[:, :], bias).then_inc(landed, 16)

        @block.gpsimd
        def _(pool):
            layer_norm_root(pool, G, rstd, var_eps, var_ready, rstd_ready)
            pool.wait_ge(xn_ready, NT)
            for k in range(2 if joint else 1):
                scatter_rows(pool, G, rt.xn, rt.slots[:, k, :], slots_ready, scattered)
            pool.wait_ge(scattered, 16 * NT * (2 if joint else 1))

        @block.scalar
        def _(act):
            for t in range(NT):
                act.wait_ge(xT_done, t + 1)
                if t >= 2:
                    act.wait_ge(logits_done, t - 1)
                act.copy(xT[:, t % 2, :, :].rearrange("p c s -> p (c s)"), PS[t % 2][:, 0:D]).then_inc(xT_ready, 1)
            act.wait_ge(shifted, 1)
            act.activation(weight[:, :, :], weight[:, :, :], ACT.Exp).then_inc(weight_ready, 1)

        @block.tensor
        def _(pe):
            pe.wait_ge(landed, 32)

            def logits_of(t):
                pe.wait_ge(xT_ready, t + 1)
                for c in range(DC):
                    ins = pe.matmul(ps_logits[:, t * E:(t + 1) * E], xT[:, t % 2, c, :], w[:, c, :],
                                    start=c == 0, stop=c == DC - 1)
                ins.then_inc(logits_done, 1)

            for t in range(NT):
                pe.wait_ge(xn_ready, t + 1)
                if t >= 2:
                    pe.wait_ge(xT_ready, t - 1)
                for c in range(DC):
                    ins = pe.transpose(PS[t % 2][:, c * P:(c + 1) * P], rt.xn[:, t, c * P:(c + 1) * P],
                                       G.const("ident"))
                ins.then_inc(xT_done, 1)
                if t:
                    logits_of(t - 1)
            logits_of(NT - 1)
            for n, (which, _) in enumerate(dispatches):
                pe.wait_ge(chosen_ready, 1)
                rhs = chosen[:, which, :, :].rearrange("p t e -> p (t e)")
                pe.matmul(ps_within[:, n * P:(n + 1) * P], G.const("before"), rhs, start=True, stop=True)
                pe.matmul(ps_tile[:, n * P:(n + 1) * P], G.const("ones"), rhs, start=True, stop=True).then_inc(counted, 1)

        @block.vector
        def _(vector):
            chain = Chain(vector, chain_s)
            layer_norm_stats(vector, X, stats, moments, var_eps, stats_done, var_ready)
            vector.wait_ge(rstd_ready, 1)
            for t in range(NT):
                vector.tensor_scalar(rt.xn[:, t, :], X[:, t, :], moments[:, t, 0:1], rstd[:, t:t + 1],
                                     ALU.subtract, ALU.mult).then_inc(xn_ready, 1)
            vector.wait_ge(landed, 32)
            vector.wait_ge(logits_done, NT)
            chain(vector.tensor_tensor(logits[:, :, :], ps_logits[:, 0:NT * E].rearrange("p (t e) -> p t e", e=E),
                                       bias_sb[:, :].unsqueeze(1).to_broadcast([P, NT, E]), ALU.add))
            for t in range(NT):
                ins = vector.max(best[:, t, :], logits[:, t, :])
                if t == NT - 1:
                    chain(ins)
            for t in range(NT):
                ins = vector.max_index(best_at[:, t, :], best[:, t, :], logits[:, t, :])
            vector.tensor_tensor(weight[:, :, :], best[:, :, :], best[:, :, 0:1].to_broadcast([P, NT, 8]),
                                 ALU.subtract).then_inc(shifted, 1)
            vector.wait_ge(shifted, 1)
            chain(vector.tensor_copy(chosen_at[:, :, :], best_at[:, :, 0:2].rearrange("p t k -> p k t")))
            iota = G.const("iota").unsqueeze(1).to_broadcast([P, NT, E])
            for k in range(2):
                chain(vector.tensor_tensor(chosen[:, k, :, :], iota, bcast(chosen_at[:, k, :], E), ALU.is_equal))
            vector.tensor_tensor(chosen[:, 2, :, :], chosen[:, 0, :, :], chosen[:, 1, :, :],
                                 ALU.add).then_inc(chosen_ready, 1)
            vector.wait_ge(weight_ready, 1)
            chain(vector.tensor_reduce(total[:, :], weight[:, :, :] if over_all else weight[:, :, 0:2], AX.X, ALU.add))
            chain(vector.reciprocal(total[:, :], total[:, :]))
            for k in range(2):
                chain(vector.tensor_tensor(rt.share[:, k, :], weight[:, :, k], total[:, :], ALU.mult))
            for n, (which, ks) in enumerate(dispatches):
                vector.wait_ge(counted, len(dispatches))
                within = ps_within[:, n * P:(n + 1) * P].rearrange("p (t e) -> p t e", e=E)
                chain(vector.tensor_copy(tile_sum[:, :, :],
                                         ps_tile[:, n * P:(n + 1) * P].rearrange("p (t e) -> p e t", e=E)))
                flat = lambda a: a.rearrange("p e t -> p (e t)")
                chain(vector.tensor_tensor_scan(flat(running[:, :, :]), G.const("restart"), flat(tile_sum[:, :, :]),
                                                0.0, ALU.mult, ALU.add))
                chain(vector.tensor_scalar(tiles[:, :], running[:, :, NT - 1], float(R - 1), 1.0 / R, ALU.add, ALU.mult))
                chain(vector.tensor_scalar(tiles_i[:, :], tiles[:, :], -0.498, None, ALU.add))
                chain(vector.tensor_scalar(tiles[:, :], tiles_i[:, :], 1.0, None, ALU.max))
                chain(vector.tensor_tensor_scan(end[:, :], G.const("ones")[:, 0:E], tiles[:, :], 0.0, ALU.mult, ALU.add))
                chain(vector.tensor_tensor(first[:, :], end[:, :], tiles[:, :], ALU.subtract))
                chain(vector.tensor_copy(rt.bounds[:, n, 0, :], first[:, :]))
                chain(vector.tensor_copy(rt.bounds[:, n, 1, :], end[:, :]))
                chain(vector.tensor_tensor(running[:, :, :], running[:, :, :], tile_sum[:, :, :], ALU.subtract))
                chain(vector.tensor_tensor(rank[:, :, :], within, running[:, :, :].rearrange("p e t -> p t e"), ALU.add))
                if capacity:
                    for k in ks:
                        chain(vector.tensor_tensor(picked[:, :, :], rank[:, :, :], chosen[:, k, :, :], ALU.mult))
                        chain(vector.tensor_reduce(keep[:, :], picked[:, :, :], AX.X, ALU.add))
                        chain(vector.tensor_scalar(keep[:, :], keep[:, :], float(capacity), None, ALU.is_lt))
                        chain(vector.tensor_tensor(rt.share[:, k, :], rt.share[:, k, :], keep[:, :], ALU.mult))
                chain(vector.tensor_scalar(first[:, :], first[:, :], float(R), None, ALU.mult))
                chain(vector.tensor_tensor(rank[:, :, :], rank[:, :, :],
                                           first[:, :].unsqueeze(1).to_broadcast([P, NT, E]), ALU.add))
                for k in ks:
                    chain(vector.tensor_tensor(picked[:, :, :], rank[:, :, :], chosen[:, k, :, :], ALU.mult))
                    chain(vector.tensor_reduce(slot_f[:, :], picked[:, :, :], AX.X, ALU.add))
                    chain(vector.tensor_copy(rt.slots[:, k, :], slot_f[:, :]))
                if n == 0:
                    vector.tensor_scalar(total[:, :], total[:, :], 1.0, None, ALU.mult).then_inc(slots_ready, 1)


def experts_block(nc, G, name, rt, n, weights, biases):
    GLU = len(weights) == 3
    UP = len(weights) - 1
    WB = 3
    HALVES = ((0, 1), (2, 3))
    PS = G.PS
    with ExitStack() as ctx:
        sb = lambda m, shape, dt=F32: ctx.enter_context(nc.sbuf_tensor(name + m, shape, dt))
        sem = semaphores(nc, ctx, name)
        up = [[sb(f"up{q}{i}", [P, DC, H]) for i in range(UP)] for q in range(WB)]
        down = [sb(f"down{q}", [P, HC, D]) for q in range(WB)]
        b1, b2 = sb("b1", [P, E, HC]), sb("b2", [P, E, D])
        xt, xT = sb("xt", [P, D]), sb("xT", [P, DC, R])
        hT, gate = sb("hT", [P, HC, R]), sb("gate", [P, HC, R])
        y = sb("y", [P, D])
        biases_landed, x_landed = sem("biases_landed"), sem("x_landed")
        weights_landed = [sem(f"weights{q}_landed") for q in range(WB)]
        stored = sem("stored")
        xT_done, xT_ready = sem("xT_done"), sem("xT_ready")
        h_done = sem("h_done")
        hT_ready = [sem("hT0_ready"), sem("hT1_ready")]
        y_done, y_ready = sem("y_done"), sem("y_ready")
        gate_ready, gated = sem("gate_ready"), sem("gated")
        ps_t, ps_y, ps_h = PS[0], PS[1], [PS[2], PS[3]]
        block = ctx.enter_context(nc.Block())

        def each_expert(eng, body):
            ends = [eng.value_load(rt.bounds[0:1, n, 1, e:e + 1], min_val=0, max_val=TILES) for e in range(E)]
            for e in range(E):
                body(e, ends[e - 1] if e else 0, ends[e])
            return ends[-1]

        @block.sync
        def _(sync):
            prime(sync, x_landed, stored)

            def load(j):
                sync.dma_start(xt[:, :], G.rows[bass.ds(j * R, R), :]).then_inc(x_landed, 16)

            load(0)
            if biases is not None:
                sync.dma_start(b1[:, :, :].rearrange("p e c -> p (e c)"), biases[0]).then_inc(biases_landed, 16)
                sync.dma_start(b2[:, :, :].rearrange("p e d -> p (e d)"), biases[1]).then_inc(biases_landed, 16)
            count = sync.value_load(rt.bounds[0:1, n, 1, E - 1:E], min_val=E, max_val=TILES)

            def load_next(j):
                sync.wait_ge(xT_done, PRIMED + j + 1)
                load(j + 1)

            def store(j):
                sync.wait_ge(y_ready, PRIMED + j + 1)
                sync.dma_start(G.rows[bass.ds(j * R, R), :], y[:, :]).then_inc(stored, 16)

            load_next(0)
            with sync.Fori(1, count) as j:
                load_next(j)
                store(j - 1)
            store(count - 1)

        @block.scalar
        def _(act):
            prime(act, gate_ready)
            if not GLU:
                prime(act, hT_ready[0])

            def load(e):
                q = e % WB
                for i in reversed(range(UP)):
                    act.dma_start(up[q][i][:, :, :], weights[i][e].rearrange("(c p) n -> p c n", p=P)).then_inc(weights_landed[q], 16)
                act.dma_start(down[q][:, :, :], weights[UP][e].rearrange("(c p) n -> p c n", p=P)).then_inc(weights_landed[q], 16)

            for e in range(WB - 1):
                load(e)
            if not GLU:
                act.wait_ge(biases_landed, 32)

            def expert(e, lo, hi):
                if e + WB - 1 < E:
                    if e:
                        act.wait_ge(y_done, PRIMED + lo)
                    load(e + WB - 1)
                with act.Fori(lo, hi) as j:
                    act.wait_ge(h_done, PRIMED + 2 * j + 1)
                    if GLU:
                        act.wait_ge(gated, PRIMED + j)
                        act.activation(gate[:, :, :].rearrange("p c r -> p (c r)"), ps_h[1][:, :],
                                       ACT.Sigmoid).then_inc(gate_ready, 1)
                    else:
                        for m in HALVES[0]:
                            ins = act.activation(hT[:, m, :], ps_h[0][:, m * R:(m + 1) * R], ACT.Relu,
                                                 bias=b1[:, e, m:m + 1])
                        ins.then_inc(hT_ready[0], 1)

            each_expert(act, expert)

        @block.vector
        def _(vector):
            prime(vector, xT_ready, hT_ready[1], y_ready, gated)
            if GLU:
                prime(vector, hT_ready[0])
            else:
                vector.wait_ge(biases_landed, 32)

            def xT_of(j):
                vector.wait_ge(xT_done, PRIMED + j + 1)
                vector.wait_ge(h_done, PRIMED + 2 * j)
                vector.tensor_copy(xT[:, :, :].rearrange("p c r -> p (c r)"), ps_t[:, 0:D]).then_inc(xT_ready, 1)

            xT_of(0)

            def expert(e, lo, hi):
                with vector.Fori(lo, hi) as j:
                    if GLU:
                        flat = lambda a: a[:, :, :].rearrange("p c r -> p (c r)")
                        vector.wait_ge(gate_ready, PRIMED + j + 1)
                        vector.wait_ge(y_done, PRIMED + j)
                        vector.tensor_tensor(flat(hT), ps_h[1][:, :], flat(gate), ALU.mult).then_inc(gated, 1)
                        vector.wait_ge(gated, PRIMED + j + 1)
                        vector.wait_ge(h_done, PRIMED + 2 * j + 2)
                        for i, (m, _) in enumerate(HALVES):
                            part = flat(hT)[:, m * R:(m + 2) * R]
                            vector.tensor_tensor(part, ps_h[0][:, m * R:(m + 2) * R], part, ALU.mult).then_inc(hT_ready[i], 1)
                    else:
                        vector.wait_ge(h_done, PRIMED + 2 * j + 2)
                        for m in HALVES[1]:
                            ins = vector.tensor_scalar(hT[:, m, :], ps_h[1][:, (m - 2) * R:(m - 1) * R],
                                                       b1[:, e, m:m + 1], 0.0, ALU.add, ALU.max)
                        ins.then_inc(hT_ready[1], 1)
                    xT_of(j + 1)
                    vector.wait_ge(y_done, PRIMED + j + 1)
                    vector.wait_ge(stored, PRIMED + 16 * j)
                    if biases is None:
                        vector.tensor_copy(y[:, :], ps_y[:, 0:D]).then_inc(y_ready, 1)
                    else:
                        vector.tensor_tensor(y[:, :], ps_y[:, 0:D], b2[:, e, :], ALU.add).then_inc(y_ready, 1)

            count = each_expert(vector, expert)
            vector.wait_ge(stored, PRIMED + 16 * count)
            vector.memset(y[:, 0:1], 0.0)

        @block.tensor
        def _(pe):
            prime(pe, xT_done, h_done, y_done)

            def transposes(j):
                pe.wait_ge(x_landed, PRIMED + 16 * j + 16)
                pe.wait_ge(xT_ready, PRIMED + j)
                for c in range(DC):
                    ins = pe.transpose(ps_t[:, c * R:(c + 1) * R], xt[:, c * P:(c + 1) * P], G.const("ident"))
                ins.then_inc(xT_done, 1)

            transposes(0)

            def expert(e, lo, hi):
                q = e % WB
                pe.wait_ge(weights_landed[q], 16 * (UP + 1) * (e // WB + 1))
                with pe.Fori(lo, hi) as j:
                    pe.wait_ge(xT_ready, PRIMED + j + 1)
                    for i in reversed(range(UP)):
                        for m in range(HC):
                            to = ps_h[i][:, m * R:(m + 1) * R] if GLU else ps_h[m // 2][:, m % 2 * R:(m % 2 + 1) * R]
                            for c in range(DC):
                                ins = pe.matmul(to, up[q][i][:, c, m * P:(m + 1) * P],
                                                xT[:, c, :], start=c == 0, stop=c == DC - 1)
                            if GLU and m == HC - 1 or not GLU and m % 2:
                                ins.then_inc(h_done, 1)
                    transposes(j + 1)
                    pe.wait_ge(y_ready, PRIMED + j)
                    for i, half in enumerate(HALVES):
                        pe.wait_ge(hT_ready[i], PRIMED + j + 1)
                        for m in half:
                            ins = pe.matmul(ps_y[:, 0:D], hT[:, m, :], down[q][:, m, :], start=m == 0, stop=m == HC - 1)
                    ins.then_inc(y_done, 1)

            each_expert(pe, expert)


def moments_step(vector, X, stats, moments, step, made, stats_done):
    if 0 <= step - 2 < NT:
        t = step - 2
        vector.wait_ge(made, t + 1)
        vector.bn_stats(stats[:, t, :], X[:, t, :]).then_inc(stats_done, 1)
    if 0 <= step - 3 < NT:
        t = step - 3
        vector.wait_ge(stats_done, max(2 * t, 1))
        vector.bn_aggr(moments[:, t, :], stats[:, t, :]).then_inc(stats_done, 1)


def combine_block(nc, G, name, rt):
    with ExitStack() as ctx:
        sem = semaphores(nc, ctx, name)
        gathered = [sem(f"gathered{t}") for t in range(4)]
        added, stats_done = [sem("first_added"), sem("both_added")], sem("stats_done")
        block = ctx.enter_context(nc.Block())

        @block.gpsimd
        def _(pool):
            for t in range(NT):
                for k in range(2):
                    pool.indirect_dma_start(rt.took[k][:, t, :], None, G.rows[:, :],
                                            bass.IndirectOffsetOnAxis(rt.slots[:, k, t:t + 1], 0)
                                            ).then_inc(gathered[t % 4], 16)
                if t >= 3:
                    pool.wait_ge(gathered[(t - 3) % 4], 32 * ((t - 3) // 4 + 1))

        @block.vector
        def _(vector):
            for step in range(NT + 3):
                for behind, k in ((0, 0), (1, 1)):
                    t = step - behind
                    if not 0 <= t < NT:
                        continue
                    if k == 0:
                        vector.wait_ge(gathered[t % 4], 32 * (t // 4 + 1))
                    else:
                        vector.wait_ge(added[0], t + 1)
                    vector.scalar_tensor_tensor(out=G.X[:, t, :], in0=rt.took[k][:, t, :],
                                                scalar=rt.share[:, k, t:t + 1], in1=G.X[:, t, :],
                                                op0=ALU.mult, op1=ALU.add).then_inc(added[k], 1)
                moments_step(vector, G.X, G.stats, G.moments, step, added[1], stats_done)
            vector.wait_ge(stats_done, 2 * NT)
            vector.tensor_scalar(G.var_eps[:, :], G.moments[:, :, 1], LN_EPS, None, ALU.add)
        G.moments_made = True


def l0_ffn(nc, G, a):
    with ExitStack() as ctx:
        rt = Routing(nc, ctx, "f0_")
        router_block(nc, G, "f0r_", rt, a["w_route0"], a["b_route0"], joint=True, over_all=True, capacity=None)
        experts_block(nc, G, "f0e_", rt, 0, (a["W1_0"], a["W2_0"]), (a["b1_0"], a["b2_0"]))
        combine_block(nc, G, "f0c_", rt)


def l3_ffn(nc, G, a):
    with ExitStack() as ctx:
        rt = Routing(nc, ctx, "f3_")
        router_block(nc, G, "f3r_", rt, a["w_route3"], a["b_route3"], joint=True, over_all=False, capacity=CAPACITY)
        experts_block(nc, G, "f3e_", rt, 0, (a["W_3"], a["V_3"], a["Wout_3"]), None)
        combine_block(nc, G, "f3c_", rt)


def boost_block(nc, G, name, rt):
    with ExitStack() as ctx:
        sem = semaphores(nc, ctx, name)
        gathered = [sem(f"gathered{t}") for t in range(4)]
        boosted, scattered = sem("boosted"), sem("scattered")
        block = ctx.enter_context(nc.Block())

        @block.gpsimd
        def _(pool):
            def scatter(t):
                pool.wait_ge(boosted, t + 1)
                pool.indirect_dma_start(G.rows[:, :], bass.IndirectOffsetOnAxis(rt.slots[:, 1, t:t + 1], 0),
                                        rt.took[1][:, t, :], None).then_inc(scattered, 16)

            for t in range(NT):
                pool.indirect_dma_start(rt.took[0][:, t, :], None, G.rows[:, :],
                                        bass.IndirectOffsetOnAxis(rt.slots[:, 0, t:t + 1], 0)
                                        ).then_inc(gathered[t % 4], 16)
                if t >= 3:
                    pool.wait_ge(gathered[(t - 3) % 4], 16 * ((t - 3) // 4 + 1))
            for i in range(4):
                pool.wait_ge(gathered[i], 16 * (NT // 4))
            for t in range(NT):
                scatter(t)
            pool.wait_ge(scattered, 16 * NT)

        @block.vector
        def _(vector):
            for t in range(NT):
                vector.wait_ge(gathered[t % 4], 16 * (t // 4 + 1))
                vector.scalar_tensor_tensor(out=rt.took[1][:, t, :], in0=rt.took[0][:, t, :], scalar=0.5,
                                            in1=rt.xn[:, t, :], op0=ALU.mult, op1=ALU.add).then_inc(boosted, 1)


def fuse_block(nc, G, name, rt, affine):
    X = G.X
    with ExitStack() as ctx:
        sb = lambda m, shape, dt=F32: ctx.enter_context(nc.sbuf_tensor(name + m, shape, dt))
        sem = semaphores(nc, ctx, name)
        gamma_beta = sb("gamma_beta", [P, 2, D])
        stats, moments = sb("stats", [P, NT, 6]), sb("moments", [P, NT, 2])
        var_eps, rstd = sb("var_eps", [P, NT]), sb("rstd", [P, NT])
        gathered = [sem(f"gathered{t}") for t in range(4)]
        x_moved = sem("x_moved")
        landed, first_added, both_added = sem("landed"), sem("first_added"), sem("both_added")
        stats_done, var_ready, rstd_ready = sem("stats_done"), sem("var_ready"), sem("rstd_ready")
        normed, scaled = sem("normed"), sem("scaled")
        block = ctx.enter_context(nc.Block())

        @block.sync
        def _(sync):
            sync.dma_start(gamma_beta[:, :, :].rearrange("p i d -> p (i d)"), affine).then_inc(landed, 16)

        @block.gpsimd
        def _(pool):
            for t in range(NT):
                pool.indirect_dma_start(rt.took[1][:, t, :], None, G.rows[:, :],
                                        bass.IndirectOffsetOnAxis(rt.slots[:, 1, t:t + 1], 0)
                                        ).then_inc(gathered[t % 4], 16)
                if t >= 3:
                    pool.wait_ge(gathered[(t - 3) % 4], 16 * ((t - 3) // 4 + 1))
            layer_norm_root(pool, G, rstd, var_eps, var_ready, rstd_ready)
            pool.wait_ge(landed, 16)
            for t in range(NT):
                pool.wait_ge(normed, t + 1)
                pool.tensor_tensor(rt.took[0][:, t, :], rt.took[0][:, t, :], gamma_beta[:, 0, :], ALU.mult).then_inc(scaled, 1)

        @block.vector
        def _(vector):
            for t in range(NT):
                vector.scalar_tensor_tensor(out=rt.xn[:, t, :], in0=rt.took[0][:, t, :], scalar=rt.share[:, 0, t:t + 1],
                                            in1=rt.xn[:, t, :], op0=ALU.mult, op1=ALU.add).then_inc(first_added, 1)
            vector.wait_ge(landed, 16)
            vector.tensor_tensor(X[:, :, :], X[:, :, :], gamma_beta[:, 1, :].unsqueeze(1).to_broadcast([P, NT, D]),
                                 ALU.add).then_inc(x_moved, 1)
            for step in range(NT + 3):
                if step < NT:
                    t = step
                    vector.wait_ge(first_added, t + 1)
                    vector.wait_ge(gathered[t % 4], 16 * (t // 4 + 1))
                    vector.scalar_tensor_tensor(out=rt.xn[:, t, :], in0=rt.took[1][:, t, :], scalar=rt.share[:, 1, t:t + 1],
                                                in1=rt.xn[:, t, :], op0=ALU.mult, op1=ALU.add).then_inc(both_added, 1)
                moments_step(vector, rt.xn, stats, moments, step, both_added, stats_done)
            vector.wait_ge(stats_done, 2 * NT)
            vector.tensor_scalar(var_eps[:, :], moments[:, :, 1], LN_EPS, None, ALU.add).then_inc(var_ready, 1)
            vector.wait_ge(rstd_ready, 1)
            vector.wait_ge(x_moved, 1)
            for t in range(NT + 2):
                if t < NT:
                    vector.tensor_scalar(rt.took[0][:, t, :], rt.xn[:, t, :], moments[:, t, 0:1], rstd[:, t:t + 1],
                                         ALU.subtract, ALU.mult).then_inc(normed, 1)
                if t >= 2:
                    vector.wait_ge(scaled, t - 1)
                    vector.tensor_tensor(X[:, t - 2, :], X[:, t - 2, :], rt.took[0][:, t - 2, :], ALU.add)


def l1_ffn(nc, G, a):
    with ExitStack() as ctx:
        rt = Routing(nc, ctx, "f1_")
        w, b = (a["W1_1"], a["W2_1"]), (a["b1_1"], a["b2_1"])
        router_block(nc, G, "f1r_", rt, a["w_route1"], a["b_route1"], joint=False, over_all=True, capacity=None)
        experts_block(nc, G, "f1e0_", rt, 0, w, b)
        boost_block(nc, G, "f1b_", rt)
        experts_block(nc, G, "f1e1_", rt, 1, w, b)
        fuse_block(nc, G, "f1c_", rt, a["affine1"])


MASK_FILL = 2.3819763e38
NO_FLOOR = -3.4e38


def l0_attention(nc, G, a):
    HEADS, DH = 4, 64
    PAIRS = HEADS // 2
    GB = TPB * PAIRS
    PVN = 96
    RMS_EPS = 1e-6
    X, PS, name = G.X, G.PS, "a0_"
    with ExitStack() as ctx:
        sb = lambda n, shape, dt=F32: ctx.enter_context(nc.sbuf_tensor(name + n, shape, dt))
        sem = semaphores(nc, ctx, name)
        w, wk, wv, gain = (G.weights[n] for n in ("w_att0", "wk_att0", "wv_att0", "gain_att0"))
        context = G.context
        kept, floor = sb("kept", [P, B, S]), sb("floor", [P, B, S])
        stats, moments = sb("stats", [P, NT, 6]), sb("moments", [P, NT, 2])
        c_stats, c_moments = sb("c_stats", [P, NT, 6]), sb("c_moments", [P, NT, 2])
        var_eps, c_sq = sb("var_eps", [P, NT]), sb("c_sq", [P, NT])
        rstd, xf, cf = sb("rstd", [P, NT]), sb("xf", [P, NT]), sb("cf", [P, NT])
        xn, cn = sb("xn", [P, TPB, D]), sb("cn", [P, TPB, D])
        xnT, cnT = sb("xnT", [P, DC, S]), sb("cnT", [P, DC, S])
        turn = sb("turn", [P, 2, DC, S])
        qT, kT, kTm = sb("qT", [P, DC, S]), sb("kT", [P, S]), sb("kTm", [P, 2, S])
        vaug = sb("vaug", [P, 2, TPB, PVN])
        masked = sb("masked", [P, 2, 2, S])
        nmax = sb("nmax", [P, 2, 2])
        prob, probT = sb("prob", [P, 2, 2, S]), sb("probT", [P, 2, 4, P])
        rsum = sb("rsum", [P, TPB, HEADS])
        enc, encT = sb("enc", [P, TPB, D]), sb("encT", [P, DC, S])
        gain_ready, scaled, ones_ready = sem("gain_ready"), sem("scaled"), sem("ones_ready")
        stats_done, c_stats_done, var_ready, c_var_ready = sem("stats_done"), sem("c_stats_done"), sem("var_ready"), sem("c_var_ready")
        c_sq_ready, root_s, root_ready = sem("c_sq_ready"), sem("root_steps"), sem("root_ready")
        kept_ready, fill_ready = sem("kept_ready"), sem("fill_ready")
        xn_ready, xT_done, xnT_ready = sem("xn_ready"), sem("xT_done"), sem("xnT_ready")
        q_turn, k_turn, recip_s, masked_ready = sem("q_turn"), sem("k_turn"), sem("reciprocals"), sem("masked_ready")
        q_done, q_ready, k_done, k_ready = sem("q_done"), sem("q_ready"), sem("k_done"), sem("k_ready")
        v_done, v_ready = sem("v_done"), sem("v_ready")
        score_done, max_ready, prob_ready = sem("score_done"), sem("max_ready"), sem("prob_ready")
        probT_done, probT_ready, pv_done = sem("probT_done"), sem("probT_ready"), sem("pv_done")
        enc_ready, encT_done, encT_ready = sem("enc_ready"), sem("encT_done"), sem("encT_ready")
        out_done, added = sem("out_done"), sem("added")
        ps_x, ps_q, ps_f, ps_s, ps_t, ps_o = PS[0], PS[1], PS[2], PS[3], [PS[4], PS[5]], [PS[6], PS[7]]
        LAST = GB - 1
        block = ctx.enter_context(nc.Block())

        @block.gpsimd
        def _(pool):
            step = Chain(pool, root_s)
            half = G.mhalf(NT)
            pool.wait_ge(var_ready, 1)
            step(pool.tensor_tensor(rstd[:, :], var_eps[:, :], half, ALU.pow))
            step(pool.tensor_tensor(xf[:, :], rstd[:, :], rstd[:, :], ALU.mult))
            step(pool.tensor_tensor(xf[:, :], xf[:, :], moments[:, :, 1], ALU.mult))
            step(pool.tensor_scalar(xf[:, :], xf[:, :], RMS_EPS, None, ALU.add))
            step(pool.tensor_tensor(xf[:, :], xf[:, :], half, ALU.pow))
            pool.tensor_tensor(xf[:, :], xf[:, :], rstd[:, :], ALU.mult).then_inc(root_ready, 1)
            pool.wait_ge(c_sq_ready, 1)
            pool.tensor_tensor(cf[:, :], c_sq[:, :], half, ALU.pow).then_inc(root_ready, 1)

        @block.scalar
        def _(act):
            prime(act, xnT_ready, v_ready, prob_ready)

            def x_turned(b, q):
                act.wait_ge(xT_done, PRIMED + b + 1)
                act.wait_ge(v_done, PRIMED + b)
                act.copy(xnT[:, :, :].rearrange("p c s -> p (c s)"), ps_x[:, :])
                act.copy(cnT[:, :, :].rearrange("p c s -> p (c s)"), ps_q[:, :]).then_inc(xnT_ready, 1)

            def values(b, q):
                act.wait_ge(v_done, PRIMED + b + 1)
                if not isinstance(b, int) or b >= 2:
                    act.wait_ge(pv_done, PRIMED + GB * (b - 1))
                act.copy(vaug[:, q, :, 0:DH], ps_q[:, 0:TPB * DH].rearrange("p (k v) -> p k v", v=DH)).then_inc(v_ready, 1)

            def exponents(b, q, g, before):
                if isinstance(b, int) and b == B:
                    return
                act.wait_ge(max_ready, PRIMED + GB * b + g + 1)
                if before is not None or g >= 2:
                    act.wait_ge(probT_done, PRIMED + GB * b + g - 1)
                for i in range(2):
                    ins = act.activation(prob[:, g % 2, i, :], masked[:, g % 2, i, :], ACT.Exp,
                                         bias=nmax[:, g % 2, i:i + 1], scale=-1.0)
                ins.then_inc(prob_ready, 1)

            act.wait_ge(G.mask_landed, 16)
            act.copy(kept[:, :, :], G.mask[:, :, :]).then_inc(kept_ready, 1)
            act.wait_ge(ones_ready, 1)
            over_batches(act, {1: x_turned, 3: values}, exponents, GB, {})

        @block.vector
        def _(vector):
            prime(vector, q_turn, k_turn, recip_s, masked_ready, xn_ready, q_ready, k_ready, max_ready, probT_ready, enc_ready, encT_ready, added)
            vector.memset(vaug[:, :, :, :], 1.0).then_inc(ones_ready, 1)
            layer_norm_stats(vector, X, stats, moments, var_eps, stats_done, var_ready)
            vector.wait_ge(G.context_landed, 16)
            layer_norm_stats(vector, context, c_stats, c_moments, c_sq, c_stats_done, c_var_ready, RMS_EPS)
            vector.wait_ge(G.landed["att0"], 16 * 4)
            vector.tensor_scalar(gain[:, :], gain[:, :], 1.0, None, ALU.add).then_inc(gain_ready, 1)
            vector.wait_ge(gain_ready, 1)
            for c in range(DC):
                for part in (w[:, 0:2, c, :], wk[:, :, c, :], wv[:, c, :]):
                    ins = vector.tensor_scalar(part, part, gain[:, c:c + 1], None, ALU.mult)
            ins.then_inc(scaled, 1)
            vector.wait_ge(c_var_ready, 1)
            vector.tensor_tensor(cf[:, :], c_moments[:, :, 0], c_moments[:, :, 0], ALU.mult).then_inc(c_var_ready, 1)
            vector.wait_ge(c_var_ready, 2)
            vector.tensor_tensor(c_sq[:, :], c_sq[:, :], cf[:, :], ALU.add).then_inc(c_sq_ready, 1)
            vector.wait_ge(kept_ready, 1)
            vector.tensor_scalar(floor[:, :, :], kept[:, :, :], -MASK_FILL, MASK_FILL, ALU.mult, ALU.add).then_inc(fill_ready, 1)
            vector.wait_ge(fill_ready, 1)
            vector.scalar_tensor_tensor(out=floor[:, :, :], in0=kept[:, :, :], scalar=NO_FLOOR, in1=floor[:, :, :],
                                        op0=ALU.mult, op1=ALU.add).then_inc(fill_ready, 1)
            vector.wait_ge(root_ready, 2)
            vector.wait_ge(fill_ready, 2)

            def normalize(b, q):
                vector.wait_ge(xT_done, PRIMED + b)
                for k in range(TPB):
                    t = TPB * b + k
                    vector.tensor_scalar(xn[:, k, :], X[:, t, :], moments[:, t, 0:1], xf[:, bass.ds(t, 1)],
                                         ALU.subtract, ALU.mult)
                    ins = vector.tensor_scalar(cn[:, k, :], context[:, t, :], cf[:, bass.ds(t, 1)], None, ALU.mult)
                ins.then_inc(xn_ready, 1)

            def rotate_q(b, q):
                vector.wait_ge(q_done, PRIMED + b + 1)
                halves = lambda ps: ps[:, :].rearrange("p (c s) -> p c s", s=S)
                for i, ps, factor in ((0, ps_x, "cosq"), (1, ps_q, "sinq")):
                    vector.tensor_tensor(turn[:, i, :, :], halves(ps), G.const(factor).unsqueeze(1).to_broadcast([P, DC, S]),
                                         ALU.mult).then_inc(q_turn, 1)
                vector.wait_ge(score_done, PRIMED + GB * b)
                vector.wait_ge(q_turn, PRIMED + 2 * (b + 1))
                vector.tensor_tensor(qT[:, :, :], turn[:, 0, :, :], turn[:, 1, :, :], ALU.add).then_inc(q_ready, 1)

            def rotate_k(b, q):
                vector.wait_ge(k_done, PRIMED + b + 1)
                vector.wait_ge(q_ready, PRIMED + b + 1)
                for i, factor in enumerate(("cosk", "sink")):
                    vector.tensor_tensor(turn[:, i, 0, :], ps_x[:, i * S:(i + 1) * S], G.const(factor), ALU.mult).then_inc(k_turn, 1)
                vector.wait_ge(k_turn, PRIMED + 3 * b + 2)
                vector.tensor_tensor(kT[:, :], turn[:, 0, 0, :], turn[:, 1, 0, :], ALU.add).then_inc(k_turn, 1)
                vector.wait_ge(k_turn, PRIMED + 3 * b + 3)
                for i, rows in enumerate(("even", "odd")):
                    ins = vector.tensor_scalar(kTm[:, i, :], kT[:, :], G.const(rows), None, ALU.mult)
                ins.then_inc(k_ready, 1)

            def turn_probabilities(b, g):
                vector.wait_ge(probT_done, PRIMED + GB * b + g + 1)
                if not isinstance(b, int) or b > 0 or g >= 2:
                    vector.wait_ge(pv_done, PRIMED + GB * b + g - 1)
                vector.tensor_copy(probT[:, g % 2, :, :].rearrange("p a t -> p (a t)"),
                                   ps_t[g % 2][:, :]).then_inc(probT_ready, 1)

            def encode(b, k):
                vector.wait_ge(pv_done, PRIMED + GB * b + PAIRS * (k + 1))
                o = ps_o[k][:, 0:HEADS * PVN].rearrange("p (h v) -> p h v", v=PVN)
                vector.reciprocal(rsum[:, k, :], o[:, :, DH]).then_inc(recip_s, 1)
                vector.wait_ge(encT_done, PRIMED + b)
                vector.wait_ge(recip_s, PRIMED + TPB * b + k + 1)
                vector.tensor_tensor(enc[:, k, :].rearrange("p (h v) -> p h v", v=DH), o[:, :, 0:DH],
                                     bcast(rsum[:, k, :], DH), ALU.mult).then_inc(enc_ready, 1)

            def pair(b, q, g, before):
                if not isinstance(b, int) or b < B:
                    vector.wait_ge(score_done, PRIMED + GB * b + g + 1)
                    if before is not None or g >= 2:
                        vector.wait_ge(prob_ready, PRIMED + GB * b + g - 1)
                    m = masked[:, g % 2, :, :]
                    vector.tensor_tensor(m, ps_s[:, :].rearrange("p (h s) -> p h s", s=S),
                                         floor[:, bass.ds(b, 1), :].to_broadcast([P, 2, S]), ALU.max).then_inc(masked_ready, 1)
                    vector.wait_ge(masked_ready, PRIMED + GB * b + g + 1)
                    vector.tensor_reduce(nmax[:, g % 2, :], m, AX.X, ALU.min).then_inc(max_ready, 1)
                if g:
                    turn_probabilities(b, g - 1)
                elif before is not None:
                    turn_probabilities(before, LAST)
                if g == LAST:
                    encode(b, 0)

            def enc_turned(b, q):
                vector.wait_ge(encT_done, PRIMED + b + 1)
                vector.wait_ge(out_done, PRIMED + b)
                vector.tensor_copy(encT[:, :, :].rearrange("p c s -> p (c s)"), ps_f[:, :]).then_inc(encT_ready, 1)

            def add(b, q):
                vector.wait_ge(out_done, PRIMED + b + 1)
                x = X[:, bass.ds(TPB * b, TPB), :]
                vector.tensor_tensor(x, ps_f[:, :].rearrange("p (k d) -> p k d", d=D), x, ALU.add).then_inc(added, 1)

            over_batches(vector, {0: normalize, 2: rotate_q, 3: rotate_k}, pair, GB,
                         {1: lambda b, q: encode(b, 1), 2: enc_turned, 3: add})

        @block.tensor
        def _(pe):
            prime(pe, xT_done, q_done, k_done, v_done, score_done, probT_done, pv_done, encT_done, out_done)
            ident = G.const("ident")
            pe.wait_ge(scaled, 1)

            def turn_x(b, q):
                pe.wait_ge(xn_ready, PRIMED + b + 1)
                if not isinstance(b, int) or b >= 1:
                    pe.wait_ge(k_ready, PRIMED + b)
                    pe.wait_ge(v_ready, PRIMED + b)
                for source, to in ((xn, ps_x), (cn, ps_q)):
                    for c in range(DC):
                        for k in range(TPB):
                            ins = pe.transpose(to[:, c * S + k * P:c * S + (k + 1) * P],
                                               source[:, k, c * P:(c + 1) * P], ident)
                ins.then_inc(xT_done, 1)

            def project_q(b, q):
                pe.wait_ge(xnT_ready, PRIMED + b + 1)
                for i, to in ((0, ps_x), (1, ps_q)):
                    for m in range(DC):
                        for c in range(DC):
                            ins = pe.matmul(to[:, m * S:(m + 1) * S], w[:, i, c, m * P:(m + 1) * P], xnT[:, c, :],
                                            start=c == 0, stop=c == DC - 1)
                ins.then_inc(q_done, 1)

            def project_kv(b, q):
                pe.wait_ge(q_ready, PRIMED + b + 1)
                for i in range(2):
                    for c in range(DC):
                        ins = pe.matmul(ps_x[:, i * S:(i + 1) * S], wk[:, i, c, :], cnT[:, c, :],
                                        start=c == 0, stop=c == DC - 1)
                ins.then_inc(k_done, 1)
                for k in range(TPB):
                    for c in range(DC):
                        ins = pe.matmul(ps_q[:, k * DH:(k + 1) * DH], cnT[:, c, k * P:(k + 1) * P], wv[:, c, :],
                                        start=c == 0, stop=c == DC - 1)
                ins.then_inc(v_done, 1)

            def scores(b, q, g):
                k, j = divmod(g, PAIRS)
                if g == 0:
                    pe.wait_ge(k_ready, PRIMED + b + 1)
                if not isinstance(b, int) or b > 0 or g > 0:
                    pe.wait_ge(masked_ready, PRIMED + GB * b + g)
                pe.matmul(ps_s[:, :], qT[:, j, k * P:(k + 1) * P], kTm[:, :, :],
                          start=True, stop=True).then_inc(score_done, 1)

            def transposes(b, g):
                pe.wait_ge(prob_ready, PRIMED + GB * b + g + 1)
                if not isinstance(b, int) or b > 0 or g >= 2:
                    pe.wait_ge(probT_ready, PRIMED + GB * b + g - 1)
                for i in range(2):
                    for c in range(TPB):
                        ins = pe.transpose(ps_t[g % 2][:, (2 * i + c) * P:(2 * i + c + 1) * P],
                                           prob[:, g % 2, i, c * P:(c + 1) * P], ident)
                ins.then_inc(probT_done, 1)

            def values(b, q, g):
                k, j = divmod(g, PAIRS)
                pe.wait_ge(probT_ready, PRIMED + GB * b + g + 1)
                if j == 0 and (not isinstance(b, int) or b > 0):
                    pe.wait_ge(enc_ready, PRIMED + TPB * (b - 1) + k + 1)
                if g == 0:
                    pe.wait_ge(v_ready, PRIMED + b + 1)
                for i in range(2):
                    at = (2 * j + i) * PVN
                    for c in range(TPB):
                        ins = pe.matmul(ps_o[k][:, at:at + PVN], probT[:, g % 2, 2 * i + c, :],
                                        vaug[:, q, c, :], start=c == 0, stop=c == TPB - 1)
                ins.then_inc(pv_done, 1)

            def pair(b, q, g, before):
                if not isinstance(b, int) or b < B:
                    if before is None and g == 0:
                        scores(b, q, 0)
                    if g < LAST:
                        scores(b, q, g + 1)
                    transposes(b, g)
                    if g == LAST and not (isinstance(b, int) and b == B - 1):
                        scores(b + 1, 1 - q, 0)
                if g:
                    values(b, q, g - 1)
                elif before is not None:
                    values(before, 1 - q, LAST)

            def turn_enc(b, q):
                pe.wait_ge(enc_ready, PRIMED + TPB * (b + 1))
                if not isinstance(b, int) or b > 0:
                    pe.wait_ge(added, PRIMED + b)
                for c in range(DC):
                    for k in range(TPB):
                        ins = pe.transpose(ps_f[:, c * S + k * P:c * S + (k + 1) * P],
                                           enc[:, k, c * P:(c + 1) * P], ident)
                ins.then_inc(encT_done, 1)

            def project_out(b, q):
                pe.wait_ge(encT_ready, PRIMED + b + 1)
                for k in range(TPB):
                    for c in range(DC):
                        ins = pe.matmul(ps_f[:, k * D:(k + 1) * D], encT[:, c, k * P:(k + 1) * P], w[:, 2, c, :],
                                        start=c == 0, stop=c == DC - 1)
                ins.then_inc(out_done, 1)

            over_batches(pe, {0: turn_x, 1: project_q, 2: project_kv}, pair, GB, {1: turn_enc, 2: project_out})


FORGET, GATE_COLS = 32, 36


def l2_attention(nc, G, a):
    HEADS, DH = 4, 64
    VW = DH + 1
    PVN = 96
    VCOLS = (HEADS - 1) * VW + PVN
    LAST = HEADS - 1
    X, PS, name = G.X, G.PS, "a2_"
    BIG = 3.0e38
    with ExitStack() as ctx:
        sb = lambda n, shape, dt=F32: ctx.enter_context(nc.sbuf_tensor(name + n, shape, dt))
        sem = semaphores(nc, ctx, name)
        gates_w, gate_bias, out_gain = (G.weights[n] for n in ("gates_2", "gate_bias_2", "out_gain_2"))
        ctxT = sb("ctxT", [P, B, DC, S])
        stats, moments = sb("stats", [P, NT, 6]), sb("moments", [P, NT, 2])
        var_eps, rstd = sb("var_eps", [P, NT]), sb("rstd", [P, NT])
        xn, xnT = sb("xn", [P, TPB, D]), sb("xnT", [P, B, DC, S])
        ig, z, soft = (sb(n, [HEADS, B, S]) for n in ("ig", "z", "soft"))
        forget = sb("forget", [HEADS, B, S])
        go_on, apart = sb("go_on", [HEADS, B, S]), sb("apart", [HEADS, B, S])
        m_rows = sb("m_rows", [P, B, S])
        cols = sb("cols", [P, 2, NT, HEADS])
        vaug = sb("vaug", [P, NT, VCOLS])
        kTm = sb("kTm", [P, 2, 2, DC, S])
        expo, decay = sb("expo", [P, 2, S + P]), sb("decay", [P, 2, S + P])
        cT = sb("cT", [P, 2, S + P])
        norm = sb("norm", [P, TPB, HEADS])
        h, square = sb("h", [P, TPB, D]), sb("square", [P, TPB, D])
        mean, root = sb("mean", [P, TPB * HEADS]), sb("root", [P, TPB * HEADS])
        ctx_landed, zeros_ready, vaug_s = sem("ctx_landed"), sem("zeros_ready"), sem("vaug_ready")
        stats_done, var_ready, rstd_ready = sem("stats_done"), sem("var_ready"), sem("rstd_ready")
        gates_summed, xn_ready, xT_done, xnT_ready = sem("gates_summed"), sem("xn_ready"), sem("xT_done"), sem("xnT_ready")
        gates_done, gates_ready, abs_ready, soft_ready = sem("gates_done"), sem("gates_ready"), sem("abs_ready"), sem("soft_ready")
        row_s, act_s, rows_ready, cols_done, cols_ready = sem("row_steps"), sem("act_steps"), sem("rows_ready"), sem("cols_done"), sem("cols_ready")
        kTm_ready, spread_done, qk_done = sem("kTm_ready"), sem("spread_done"), sem("qk_done")
        expo_ready, decay_ready, cT_ready = sem("expo_ready"), sem("decay_ready"), sem("cT_ready")
        masked_ready, pv_done, h_ready = sem("masked_ready"), sem("pv_done"), sem("h_ready")
        chain_s, square_ready, var2_ready, root_ready = sem("chain"), sem("square_ready"), sem("h_var_ready"), sem("root_ready")
        scaled_ready, gained, added = sem("scaled_ready"), sem("gained"), sem("added")
        ps_x, ps_g, ps_c = PS[0], PS[1], PS[2]
        ps_qk, ps_m, ps_o = [PS[2], PS[3]], [PS[4], PS[5]], [[PS[6], PS[7]], [PS[0], PS[1]]]
        flat = lambda t: t.rearrange("p b s -> p (b s)")
        by_head = lambda t: t[:, :, :].rearrange("p k (h v) -> p (k h) v", v=DH)
        block = ctx.enter_context(nc.Block())

        @block.sync
        def _(sync):
            sync.dma_start(ctxT[:, :, :, :].rearrange("p b c s -> p (b c) s"),
                           a["ctxT"].rearrange("b (c p) s -> p (b c) s", p=P)).then_inc(ctx_landed, 16)

        @block.gpsimd
        def _(pool):
            prime(pool, kTm_ready, masked_ready, root_ready, gained, added)
            pool.memset(m_rows[:, :, :], 0.0).then_inc(zeros_ready, 1)
            pool.memset(vaug[:, :, :], 1.0).then_inc(vaug_s, 1)
            layer_norm_root(pool, G, rstd, var_eps, var_ready, rstd_ready)
            pool.wait_ge(vaug_s, 1)
            pool.wait_ge(G.context_landed, 16)
            for t in range(0, NT, 4):
                ins = pool.tensor_copy(vaug[:, t:t + 4, 0:HEADS * VW].rearrange("p t (h v) -> p t h v", v=VW)[:, :, :, 0:DH],
                                       G.context[:, t:t + 4, :].rearrange("p t (h v) -> p t h v", v=DH))
            ins.then_inc(vaug_s, 1)
            pool.wait_ge(ctx_landed, 16)

            def keys(b, q):
                if not isinstance(b, int) or b >= 2:
                    pool.wait_ge(qk_done, PRIMED + HEADS * (b - 1))
                for i, rows in enumerate(("even8", "odd8")):
                    ins = pool.tensor_tensor(kTm[:, q, i, :, :].rearrange("p c s -> p (c s)"),
                                             ctxT[:, bass.ds(b, 1), :, :].rearrange("p o c s -> p (o c s)"),
                                             G.const(rows).to_broadcast([P, DC * S]), ALU.mult)
                ins.then_inc(kTm_ready, 1)

            def mask(b, n):
                pool.wait_ge(cT_ready, PRIMED + HEADS * b + n + 1)
                for at in (0, S):
                    part = cT[:, n % 2, at:at + P]
                    ins = pool.tensor_tensor(part, part, G.const("upto"), ALU.mult)
                ins.then_inc(masked_ready, 1)

            def pair(b, q, n, before):
                if n:
                    mask(b, n - 1)
                elif before is not None:
                    mask(before, LAST)

            def root_of(b, q):
                pool.wait_ge(var2_ready, PRIMED + b + 1)
                pool.tensor_tensor(root[:, :], root[:, :], G.const("half")[:, 0:TPB * HEADS], ALU.pow).then_inc(root_ready, 1)

            def add(b, q):
                pool.wait_ge(scaled_ready, PRIMED + b + 1)
                pool.tensor_tensor(h[:, :, :], h[:, :, :], out_gain[:, :].unsqueeze(1).to_broadcast([P, TPB, D]),
                                   ALU.mult).then_inc(gained, 1)
                pool.wait_ge(gained, PRIMED + b + 1)
                x = X[:, bass.ds(TPB * b, TPB), :]
                pool.tensor_tensor(x, x, h[:, :, :], ALU.add).then_inc(added, 1)

            over_batches(pool, {1: keys}, pair, HEADS, {2: root_of, 3: add})

        @block.scalar
        def _(act):
            prime(act, decay_ready, square_ready)
            act.wait_ge(abs_ready, 1)
            act.activation(soft[:, :, :], soft[:, :, :], ACT.Exp, scale=-1.0).then_inc(act_s, 1)
            act.wait_ge(act_s, 1)
            act.activation(soft[:, :, :], soft[:, :, :], ACT.Ln, bias=1.0).then_inc(soft_ready, 1)
            act.wait_ge(cols_done, 1)
            rows_of = lambda i: ps_c[:, i * NT * HEADS:(i + 1) * NT * HEADS]
            act.activation(cols[:, 1, :, :].rearrange("p t n -> p (t n)"), rows_of(1), ACT.Exp, scale=-1.0)
            act.mul(cols[:, 0, :, :].rearrange("p t n -> p (t n)"), rows_of(0), -1.0).then_inc(cols_ready, 1)

            def exponents(b, q, n, before):
                if isinstance(b, int) and b == B:
                    return
                act.wait_ge(expo_ready, PRIMED + HEADS * b + n + 1)
                if before is not None or n >= 2:
                    act.wait_ge(cT_ready, PRIMED + HEADS * b + n - 1)
                act.activation(decay[:, n % 2, :], expo[:, n % 2, :], ACT.Exp).then_inc(decay_ready, 1)

            def squares(b, q):
                act.wait_ge(h_ready, PRIMED + b + 1)
                act.activation(square[:, :, :], h[:, :, :], ACT.Square).then_inc(square_ready, 1)

            over_batches(act, {}, exponents, HEADS, {1: squares})

        @block.vector
        def _(vector):
            prime(vector, xn_ready, xnT_ready, gates_ready, chain_s, expo_ready, cT_ready, h_ready, var2_ready, scaled_ready)
            layer_norm_stats(vector, X, stats, moments, var_eps, stats_done, var_ready)
            vector.wait_ge(G.landed["mlstm"], 16 * 3)
            vector.tensor_tensor(gates_w[:, 1, :, :], gates_w[:, 1, :, :], gates_w[:, 2, :, :], ALU.add).then_inc(gates_summed, 1)
            vector.wait_ge(rstd_ready, 1)

            def normalize(b):
                vector.wait_ge(xT_done, PRIMED + b)
                for k in range(TPB):
                    ins = vector.tensor_scalar(xn[:, k, :], X[:, TPB * b + k, :], moments[:, TPB * b + k, 0:1],
                                               rstd[:, bass.ds(TPB * b + k, 1)], ALU.subtract, ALU.mult)
                ins.then_inc(xn_ready, 1)

            def x_turned(b):
                vector.wait_ge(xT_done, PRIMED + b + 1)
                vector.tensor_copy(xnT[:, bass.ds(b, 1), :, :].rearrange("p o c s -> p (o c s)"), ps_x[:, :]).then_inc(xnT_ready, 1)

            def gates(b):
                vector.wait_ge(gates_done, PRIMED + b + 1)
                for to, at in ((ig, 0), (z, FORGET)):
                    ins = vector.tensor_scalar(to[:, bass.ds(b, 1), :].rearrange("p o s -> p (o s)"),
                                               ps_g[at:at + HEADS, 0:S], gate_bias[at:at + HEADS, 0:1], None, ALU.add)
                ins.then_inc(gates_ready, 1)

            normalize(0)
            row = Chain(vector, row_s)
            row(vector.memset(go_on[:, :, :], 1.0))
            row(vector.memset(go_on[:, :, 0:1], 0.0))
            row(vector.memset(apart[:, :, :], 0.0))
            row(vector.memset(apart[:, :, 0:1], BIG))
            x_turned(0)
            normalize(1)
            with vector.Fori(1, B - 1) as b:
                x_turned(b)
                normalize(b + 1)
                gates(b - 1)
            x_turned(B - 1)
            gates(B - 2)
            gates(B - 1)
            vector.wait_ge(gates_ready, PRIMED + B)
            vector.scalar_tensor_tensor(out=soft[:, :, :], in0=z[:, :, :], scalar=-1.0, in1=z[:, :, :], op0=ALU.mult,
                                        op1=ALU.max).then_inc(abs_ready, 1)
            vector.wait_ge(abs_ready, 1)
            vector.wait_ge(soft_ready, 1)
            row(vector.scalar_tensor_tensor(out=z[:, :, :], in0=z[:, :, :], scalar=0.0, in1=soft[:, :, :], op0=ALU.min,
                                            op1=ALU.subtract))
            row(vector.tensor_tensor_scan(flat(forget[:, :, :]), flat(go_on[:, :, :]), flat(z[:, :, :]), 0.0, ALU.mult, ALU.add))
            row(vector.tensor_tensor(ig[:, :, :], forget[:, :, :], ig[:, :, :], ALU.subtract))
            vector.wait_ge(zeros_ready, 1)
            row(vector.tensor_tensor_scan(flat(m_rows[0:HEADS, :, :]), flat(apart[:, :, :]), flat(ig[:, :, :]), 0.0, ALU.add, ALU.min))
            vector.tensor_tensor(z[:, :, :], forget[:, :, :], m_rows[0:HEADS, :, :], ALU.subtract).then_inc(rows_ready, 1)
            vector.wait_ge(cols_ready, 1)

            def expo_of(b, n):
                vector.wait_ge(spread_done, PRIMED + HEADS * b + n + 1)
                if not isinstance(b, int) or b > 0 or n >= 2:
                    vector.wait_ge(decay_ready, PRIMED + HEADS * b + n - 1)
                for k, to, lo in ((0, 0, 0), (1, S, P)):
                    ins = vector.tensor_scalar(expo[:, n % 2, to:to + S - lo], ps_m[n % 2][:, lo:S],
                                               cols[:, 0, bass.ds(TPB * b + k, 1), n], 0.0, ALU.add, ALU.min)
                ins.then_inc(expo_ready, 1)

            def cT_of(b, n):
                vector.wait_ge(qk_done, PRIMED + HEADS * b + n + 1)
                vector.wait_ge(decay_ready, PRIMED + HEADS * b + n + 1)
                if not isinstance(b, int) or b > 0 or n >= 2:
                    vector.wait_ge(pv_done, PRIMED + HEADS * b + n - 1)
                vector.tensor_tensor(cT[:, n % 2, :], ps_qk[n % 2][:, 0:S + P], decay[:, n % 2, :],
                                     ALU.mult).then_inc(cT_ready, 1)

            def pair(b, q, n, before):
                if not isinstance(b, int) or b < B:
                    expo_of(b, n)
                if n:
                    cT_of(b, n - 1)
                elif before is not None:
                    cT_of(before, LAST)

            CH = 11

            def outputs(b, q):
                chain = Chain(vector, chain_s, PRIMED + CH * b)
                heads = lambda k: ps_o[q][k][:, 0:HEADS * VW].rearrange("p (h v) -> p h v", v=VW)
                vector.wait_ge(pv_done, PRIMED + HEADS * (b + 1))
                for k in range(TPB):
                    chain(vector.tensor_copy(norm[:, k, :], heads(k)[:, :, DH]))
                chain(vector.scalar_tensor_tensor(out=norm[:, :, :], in0=norm[:, :, :], scalar=-1.0, in1=norm[:, :, :],
                                                  op0=ALU.mult, op1=ALU.max))
                chain(vector.tensor_tensor(norm[:, :, :], norm[:, :, :], cols[:, 1, bass.ds(TPB * b, TPB), :], ALU.max))
                chain(vector.tensor_scalar(norm[:, :, :], norm[:, :, :], 1e-6, None, ALU.add))
                chain(vector.reciprocal(norm[:, :, :], norm[:, :, :]))
                vector.wait_ge(added, PRIMED + b)
                for k in range(TPB):
                    ins = vector.tensor_tensor(h[:, k, :].rearrange("p (h v) -> p h v", v=DH),
                                               heads(k)[:, :, 0:DH], bcast(norm[:, k, :], DH), ALU.mult)
                chain(ins)
                chain(vector.tensor_reduce(mean[:, :], by_head(h), AX.X, ALU.add))
                chain(vector.tensor_scalar(mean[:, :], mean[:, :], 1.0 / DH, None, ALU.mult))
                vector.tensor_tensor(by_head(h), by_head(h), bcast(mean[:, :], DH), ALU.subtract).then_inc(h_ready, 1)

            def variance(b, q):
                chain = Chain(vector, chain_s, PRIMED + CH * b + 9)
                vector.wait_ge(square_ready, PRIMED + b + 1)
                chain(vector.tensor_reduce(root[:, :], by_head(square), AX.X, ALU.add))
                vector.tensor_scalar(root[:, :], root[:, :], 1.0 / DH, 1e-6, ALU.mult, ALU.add).then_inc(var2_ready, 1)
                vector.sem_inc(chain_s, 1)

            def scale(b, q):
                vector.wait_ge(root_ready, PRIMED + b + 1)
                vector.tensor_tensor(by_head(h), by_head(h), bcast(root[:, :], DH), ALU.mult).then_inc(scaled_ready, 1)

            over_batches(vector, {}, pair, HEADS, {1: outputs, 2: variance, 3: scale})

        @block.tensor
        def _(pe):
            prime(pe, xT_done, gates_done, spread_done, qk_done, pv_done)
            ident = G.const("ident")
            pe.wait_ge(gates_summed, 1)
            pe.wait_ge(ctx_landed, 16)

            def turn_x(b):
                pe.wait_ge(xn_ready, PRIMED + b + 1)
                pe.wait_ge(xnT_ready, PRIMED + b)
                for c in range(DC):
                    for k in range(TPB):
                        ins = pe.transpose(ps_x[:, c * S + k * P:c * S + (k + 1) * P],
                                           xn[:, k, c * P:(c + 1) * P], ident)
                ins.then_inc(xT_done, 1)

            def gates(b):
                pe.wait_ge(xnT_ready, PRIMED + b + 1)
                pe.wait_ge(gates_ready, PRIMED + b)
                for i, source in enumerate((xnT, ctxT)):
                    for c in range(DC):
                        ins = pe.matmul(ps_g[0:GATE_COLS, 0:S], gates_w[:, i, c, :],
                                        source[:, bass.ds(b, 1), c, :].rearrange("p o s -> p (o s)"),
                                        start=i == 0 and c == 0, stop=i == 1 and c == DC - 1)
                ins.then_inc(gates_done, 1)

            turn_x(0)
            with pe.Fori(1, B) as b:
                turn_x(b)
                gates(b - 1)
            gates(B - 1)
            pe.wait_ge(rows_ready, 1)
            for i, rows in enumerate((ig, z)):
                for t in range(NT):
                    at = (NT * i + t) * HEADS
                    ins = pe.transpose(ps_c[:, at:at + HEADS], flat(rows[:, :, :])[:, t * P:(t + 1) * P],
                                       G.const("ident")[0:HEADS, 0:HEADS])
            ins.then_inc(cols_done, 1)
            pe.wait_ge(cols_ready, 1)
            pe.wait_ge(vaug_s, 2)

            def spread(b, n):
                if not isinstance(b, int) or b > 0 or n >= 2:
                    pe.wait_ge(expo_ready, PRIMED + HEADS * b + n - 1)
                pe.matmul(ps_m[n % 2][:, 0:S], G.const("pick")[:, n * P:(n + 1) * P],
                          m_rows[:, bass.ds(b, 1), :].rearrange("p o s -> p (o s)"),
                          start=True, stop=True).then_inc(spread_done, 1)

            def qk(b, q, n):
                if n == 0:
                    pe.wait_ge(kTm_ready, PRIMED + b + 1)
                if not isinstance(b, int) or b > 0 or n >= 2:
                    pe.wait_ge(cT_ready, PRIMED + HEADS * b + n - 1)
                for k, to, lo in ((0, 0, 0), (1, S, P)):
                    ins = pe.matmul(ps_qk[n % 2][:, to:to + S - lo], kTm[:, q, n % 2, n // 2, k * P:(k + 1) * P],
                                    xnT[:, bass.ds(b, 1), n // 2, lo:S].rearrange("p o s -> p (o s)"), start=True, stop=True)
                ins.then_inc(qk_done, 1)

            def values(b, q, n):
                pe.wait_ge(masked_ready, PRIMED + HEADS * b + n + 1)
                if n == 0 and (not isinstance(b, int) or b >= 2):
                    pe.wait_ge(h_ready, PRIMED + b - 1)
                at = n * VW
                for k, c, lo in ((0, 0, 0), (1, 0, P), (1, 1, S)):
                    ins = pe.matmul(ps_o[q][k][:, at:at + PVN], cT[:, n % 2, lo:lo + P],
                                    vaug[:, bass.ds(TPB * b + c, 1), at:at + PVN].rearrange("p o v -> p (o v)"),
                                    start=c == 0, stop=c == k)
                ins.then_inc(pv_done, 1)

            def pair(b, q, n, before):
                if not isinstance(b, int) or b < B:
                    if before is None and n == 0:
                        spread(b, 0)
                        qk(b, q, 0)
                    if n < LAST:
                        spread(b, n + 1)
                        qk(b, q, n + 1)
                    elif not (isinstance(b, int) and b == B - 1):
                        spread(b + 1, 0)
                        qk(b + 1, 1 - q, 0)
                if n:
                    values(b, q, n - 1)
                elif before is not None:
                    values(before, 1 - q, LAST)

            over_batches(pe, {}, pair, HEADS, {})


def one_ahead(eng, body):
    body(0, 0, True)
    with eng.Fori(0, B // 2 - 1) as two:
        for q in (1, 0):
            body(2 * two + 2 - q, q, True)
    body(B - 1, 1, False)


def l2_ffn(nc, G, a):
    X, PS, name = G.X, G.PS, "f2_"
    with ExitStack() as ctx:
        sb = lambda n, shape, dt=F32: ctx.enter_context(nc.sbuf_tensor(name + n, shape, dt))
        sem = semaphores(nc, ctx, name)
        w, mu = sb("w", [P, 3, DC, D]), sb("mu", [P, 2, DC])
        stats, moments = sb("stats", [P, NT, 6]), sb("moments", [P, NT, 2])
        var_eps, rstd = sb("var_eps", [P, NT]), sb("rstd", [P, NT])
        xn = sb("xn", [P, 2, TPB, D])
        xnT = sb("xnT", [P, 2, DC, S + 1])
        step_x = sb("step_x", [P, DC, S])
        mixed = sb("mixed", [P, 2, 2, DC, S])
        act_k = sb("act_k", [P, 2, DC, S])
        recep = sb("recep", [P, 2, TPB, D])
        out = sb("out", [P, TPB, D])
        landed, zero_ready = sem("landed"), sem("zero_ready")
        stats_done, var_ready, rstd_ready = sem("stats_done"), sem("var_ready"), sem("rstd_ready")
        step_s, out_s, added = sem("steps"), sem("out"), sem("added")
        xn_ready, xT_done, xnT_ready = sem("xn_ready"), sem("xT_done"), sem("xnT_ready")
        mixed_ready, k_done, relu_s, act_ready = sem("mixed_ready"), sem("k_done"), sem("relu"), sem("act_ready")
        r_done, recep_ready, v_done = sem("r_done"), sem("recep_ready"), sem("v_done")
        block = ctx.enter_context(nc.Block())

        @block.sync
        def _(sync):
            for i in range(3):
                sync.dma_start(w[:, i, :, :], a["w_mix"][i].rearrange("(c p) n -> p c n", p=P)).then_inc(landed, 16)
            sync.dma_start(mu[:, :, :].rearrange("p i c -> p (i c)"), a["mu_mix"]).then_inc(landed, 16)

        @block.gpsimd
        def _(pool):
            layer_norm_root(pool, G, rstd, var_eps, var_ready, rstd_ready)

        @block.scalar
        def _(act):
            prime(act, xnT_ready, relu_s, act_ready, recep_ready)
            act.wait_ge(zero_ready, 1)

            def x_turned(b, q):
                act.wait_ge(xT_done, PRIMED + b + 1)
                act.wait_ge(mixed_ready, PRIMED + 2 * b)
                act.copy(xnT[:, q, :, 1:S + 1], PS[q][:, :].rearrange("p (c s) -> p c s", s=S)).then_inc(xnT_ready, 1)

            def body(b, q, more):
                act.wait_ge(k_done, PRIMED + b + 1)
                act.wait_ge(v_done, PRIMED + b)
                k = act_k[:, q, :, :].rearrange("p c s -> p (c s)")
                act.activation(k, PS[2 + q][:, :], ACT.Relu).then_inc(relu_s, 1)
                act.wait_ge(relu_s, PRIMED + b + 1)
                act.activation(k, k, ACT.Square).then_inc(act_ready, 1)
                if more:
                    x_turned(b + 1, 1 - q)
                act.wait_ge(r_done, PRIMED + b + 1)
                act.activation(recep[:, q, :, :].rearrange("p k d -> p (k d)"), PS[4 + q][:, :],
                               ACT.Sigmoid).then_inc(recep_ready, 1)

            x_turned(0, 0)
            one_ahead(act, body)

        @block.vector
        def _(vector):
            prime(vector, step_s, out_s, added, xn_ready, mixed_ready)
            vector.memset(xnT[:, :, :, 0:1], 0.0).then_inc(zero_ready, 1)
            layer_norm_stats(vector, X, stats, moments, var_eps, stats_done, var_ready)
            vector.wait_ge(landed, 16 * 4)
            vector.wait_ge(rstd_ready, 1)

            def mix(b, q):
                vector.wait_ge(xT_done, PRIMED + b)
                for k in range(TPB):
                    ins = vector.tensor_scalar(xn[:, q, k, :], X[:, TPB * b + k, :], moments[:, TPB * b + k, 0:1],
                                               rstd[:, bass.ds(TPB * b + k, 1)], ALU.subtract, ALU.mult)
                ins.then_inc(xn_ready, 1)
                vector.wait_ge(xnT_ready, PRIMED + b + 1)
                before, now = xnT[:, q, :, 0:S], xnT[:, q, :, 1:S + 1]
                vector.tensor_tensor(step_x[:, :, :], now, before, ALU.subtract).then_inc(step_s, 1)
                vector.wait_ge(step_s, PRIMED + b + 1)
                if not isinstance(b, int) or b >= 2:
                    vector.wait_ge(r_done, PRIMED + b - 1)
                for i in (1, 0):
                    for c in range(DC):
                        ins = vector.scalar_tensor_tensor(out=mixed[:, q, i, c, :], in0=step_x[:, c, :],
                                                          scalar=mu[:, i, c:c + 1], in1=before[:, c, :],
                                                          op0=ALU.mult, op1=ALU.add)
                    ins.then_inc(mixed_ready, 1)

            def body(b, q, more):
                if more:
                    mix(b + 1, 1 - q)
                vector.wait_ge(recep_ready, PRIMED + b + 1)
                vector.wait_ge(v_done, PRIMED + b + 1)
                vector.wait_ge(added, PRIMED + b)
                vector.tensor_tensor(out[:, :, :], PS[6 + q][:, :].rearrange("p (k d) -> p k d", d=D),
                                     recep[:, q, :, :], ALU.mult).then_inc(out_s, 1)
                vector.wait_ge(out_s, PRIMED + b + 1)
                x = X[:, bass.ds(TPB * b, TPB), :]
                vector.tensor_tensor(x, x, out[:, :, :], ALU.add).then_inc(added, 1)

            mix(0, 0)
            one_ahead(vector, body)

        @block.tensor
        def _(pe):
            prime(pe, xT_done, k_done, r_done, v_done)
            ident = G.const("ident")
            pe.wait_ge(landed, 16 * 4)

            def turn(b, q):
                pe.wait_ge(xn_ready, PRIMED + b + 1)
                pe.wait_ge(xnT_ready, PRIMED + b)
                for c in range(DC):
                    for k in range(TPB):
                        ins = pe.transpose(PS[q][:, c * S + k * P:c * S + (k + 1) * P],
                                           xn[:, q, k, c * P:(c + 1) * P], ident)
                ins.then_inc(xT_done, 1)

            def body(b, q, more):
                pe.wait_ge(mixed_ready, PRIMED + 2 * b + 1)
                pe.wait_ge(act_ready, PRIMED + b)
                for m in range(DC):
                    for c in range(DC):
                        ins = pe.matmul(PS[2 + q][:, m * S:(m + 1) * S], w[:, 1, c, m * P:(m + 1) * P],
                                        mixed[:, q, 1, c, :], start=c == 0, stop=c == DC - 1)
                ins.then_inc(k_done, 1)
                if more:
                    turn(b + 1, 1 - q)
                pe.wait_ge(mixed_ready, PRIMED + 2 * b + 2)
                pe.wait_ge(recep_ready, PRIMED + b)
                for k in range(TPB):
                    for c in range(DC):
                        ins = pe.matmul(PS[4 + q][:, k * D:(k + 1) * D], mixed[:, q, 0, c, k * P:(k + 1) * P],
                                        w[:, 0, c, :], start=c == 0, stop=c == DC - 1)
                ins.then_inc(r_done, 1)
                pe.wait_ge(act_ready, PRIMED + b + 1)
                if not isinstance(b, int) or b >= 2:
                    pe.wait_ge(out_s, PRIMED + b - 1)
                for k in range(TPB):
                    for c in range(DC):
                        ins = pe.matmul(PS[6 + q][:, k * D:(k + 1) * D], act_k[:, q, c, k * P:(k + 1) * P],
                                        w[:, 2, c, :], start=c == 0, stop=c == DC - 1)
                ins.then_inc(v_done, 1)

            turn(0, 0)
            one_ahead(pe, body)


class Shared:

    def __init__(self, X, consts, PS):
        self.X, self.consts, self.PS = X, consts, PS

    def const(self, name):
        lo, hi = CONST[name]
        return self.consts[:, lo:hi]

    def mhalf(self, n):
        return self.const("half")[:, 0:n]


KEPT = {"att0": (("w_att0", [3, DC, D]), ("wk_att0", [2, DC, P]), ("wv_att0", [DC, 64]), ("gain_att0", [DC])),
        "mha1": (("w_mha1", [4, DC, D]), ("v_mha1", [2 * DC + 2 * D])),
        "mlstm": (("gates_2", [3, DC, GATE_COLS]), ("gate_bias_2", [1]), ("out_gain_2", [D])),
        "mha3": (("w_mha3", [4, DC, D]), ("v_mha3", [2 * DC + 2 * D]))}


def build(nc, a, out):
    x_rows = a["x"].rearrange("b (k p) d -> p (b k) d", p=P)
    out_rows = out.rearrange("b (k p) d -> p (b k) d", p=P)
    with ExitStack() as ctx:
        X = ctx.enter_context(nc.sbuf_tensor("X", [P, NT, D], F32))
        consts = ctx.enter_context(nc.sbuf_tensor("consts", [P, CONSTS], F32))
        PS = [ctx.enter_context(nc.psum_tensor(f"bank{i}", [P, 512], F32)) for i in range(8)]
        x_landed = ctx.enter_context(nc.semaphore("x_landed"))
        stored = ctx.enter_context(nc.semaphore("stored"))
        G = Shared(X, consts, PS)
        G.moments_made = False
        G.stats = ctx.enter_context(nc.sbuf_tensor("x_stats", [P, NT, 6], F32))
        G.moments = ctx.enter_context(nc.sbuf_tensor("x_moments", [P, NT, 2], F32))
        G.var_eps = ctx.enter_context(nc.sbuf_tensor("x_var_eps", [P, NT], F32))
        G.mask = ctx.enter_context(nc.sbuf_tensor("mask", [P, B, S], U8))
        G.mask_landed = ctx.enter_context(nc.semaphore("mask_landed"))
        G.context = ctx.enter_context(nc.sbuf_tensor("context", [P, NT, D], F32))
        G.context_landed = ctx.enter_context(nc.semaphore("context_landed"))
        G.weights, G.landed = {}, {}
        for layer, parts in KEPT.items():
            G.landed[layer] = ctx.enter_context(nc.semaphore(f"weights_{layer}_landed"))
            for n, shape in parts:
                G.weights[n] = ctx.enter_context(nc.sbuf_tensor("kept_" + n, [P] + shape, F32))
        G.rows = nc.dram_tensor("rows", ((TILES + 1) * R, D), F32, kind="Internal").ap()
        zeroed = ctx.enter_context(nc.semaphore("zeroed"))
        G.rows_filled = ctx.enter_context(nc.semaphore("rows_filled"))
        zeros = ctx.enter_context(nc.sbuf_tensor("zeros", [P, D], F32))
        with nc.Block() as block:
            @block.vector
            def _(vector):
                vector.memset(zeros[:, :], 0.0).then_inc(zeroed, 1)

            def keep(eng, layer):
                for n, shape in KEPT[layer]:
                    to, source = G.weights[n], a[n]
                    if len(shape) == 3:
                        to, source = to[:, :, :, :].rearrange("p i c n -> p (i c) n"), source.rearrange("i (c p) n -> p (i c) n", p=P)
                    elif len(shape) == 2:
                        to, source = to[:, :, :], source.rearrange("(c p) n -> p c n", p=P)
                    else:
                        to = to[:, :]
                    eng.dma_start(to, source).then_inc(G.landed[layer], 16)

            @block.scalar
            def _(act):
                act.dma_start(G.context[:, :, :], a["ctx"].rearrange("b (k p) d -> p (b k) d", p=P)).then_inc(G.context_landed, 16)
                act.dma_start(G.mask[:, :, :].rearrange("p b s -> p (b s)"), a["kept"].to_broadcast([P, B * S])).then_inc(G.mask_landed, 16)

            @block.sync
            def _(sync):
                sync.dma_start(X[:, :, :], x_rows).then_inc(x_landed, 16)
                sync.dma_start(consts[:, :], a["consts"]).then_inc(x_landed, 16)
                keep(sync, "att0")
                sync.wait_ge(zeroed, 1)
                sync.dma_start(G.rows.rearrange("(n p) d -> p n d", p=P),
                               zeros[:, :].unsqueeze(1).to_broadcast([P, TILES + 1, D])).then_inc(G.rows_filled, 16)
                keep(sync, "mha1")
                keep(sync, "mlstm")
                keep(sync, "mha3")
                sync.wait_ge(x_landed, 32)

        for layer in LAYERS:
            layer(nc, G, a)

        with nc.Block() as block:
            @block.sync
            def _(sync):
                sync.dma_start(out_rows, X[:, :, :]).then_inc(stored, 16)
                sync.wait_ge(stored, 16)
                sync.wait_ge(G.rows_filled, 16)
                sync.wait_ge(G.context_landed, 16)
                sync.wait_ge(G.mask_landed, 16)
                for layer, parts in KEPT.items():
                    sync.wait_ge(G.landed[layer], 16 * len(parts))


LAYERS = (
    l0_attention,
    l0_ffn,
    lambda nc, G, a: mha_block(nc, G, "mha1", a["ctxT"]),
    l1_ffn,
    l2_attention,
    l2_ffn,
    lambda nc, G, a: mha_block(nc, G, "mha3", a["ctxT"]),
    l3_ffn,
)


def constants():
    c = np.zeros((P, CONSTS), np.float32)

    def put(name, value):
        lo, hi = CONST[name]
        c[:, lo:hi] = value

    p, j = np.arange(P)[:, None], np.arange(P)[None, :]
    put("ident", p == j)
    put("before", p < j)
    put("upto", p <= j)
    put("ones", 1.0)
    put("restart", np.broadcast_to(j % NT != 0, (P, P)))
    put("head", p // 16 == np.arange(8)[None, :])
    put("iota", np.broadcast_to(np.arange(8)[None, :], (P, 8)))
    put("half", -0.5)
    put("even", p < P // 2)
    put("odd", p >= P // 2)
    put("even8", (p < P // 2) / 8)
    put("odd8", (p >= P // 2) / 8)
    put("pick", (p == np.arange(4 * P)[None, :] // P))
    HEAD = 64
    scale = np.float32(10000.0) ** (np.float32(2.0 / HEAD) * np.arange(HEAD // 2, dtype=np.float32))
    row = np.arange(P) % HEAD
    sign = np.where(row < HEAD // 2, np.float32(-1), np.float32(1))[:, None]
    for q, at in (("q", S), ("k", 0)):
        angle = np.arange(at, at + S, dtype=np.float32)[None, :] / scale[row % (HEAD // 2)][:, None]
        by = np.float32(-(HEAD ** -0.5) if q == "q" else 1.0)
        put("cos" + q, np.cos(angle) * by)
        put("sin" + q, np.sin(angle) * sign * by)
    return c


def kernel(**inputs):
    import concourse.bacc as bacc
    from concourse.bass_utils import run_bass_kernel_spmd

    i = {k: np.asarray(v) for k, v in inputs.items()}
    T = lambda a: np.ascontiguousarray(a.T)
    rows = lambda a: np.broadcast_to(a.reshape(1, -1), (P, a.size))
    chunks = lambda a: T(a.reshape(-1, P))
    cat = lambda *a: np.ascontiguousarray(np.concatenate(a, axis=1))
    laid = {"x": i["x"], "consts": constants(), "ctx": i["ctx_1024"],
            "ctxT": np.ascontiguousarray(i["ctx_1024"].transpose(0, 2, 1))}
    by_feature = lambda a: a.reshape(16, D // 16, *a.shape[1:]).swapaxes(0, 1).reshape(a.shape)
    for n in "13":
        part = lambda m: by_feature(i[f"L{n}_xattn_{m}"]) if m[1] in "qk" else i[f"L{n}_xattn_{m}"]
        laid["w_mha" + n] = np.stack([T(part("W" + m)) for m in "qkvo"])
        laid["v_mha" + n] = cat(chunks(part("bq")), chunks(part("bk")), rows(part("bv")), rows(part("bo")))
    hidden_chunks = lambda a: np.ascontiguousarray(a.reshape(E * HC, P).T)
    laid["w_route0"], laid["b_route0"] = i["L0_ffn_Wg"], np.zeros((P, E), np.float32)
    laid["w_route1"], laid["b_route1"] = i["L1_ffn_gate_W"], rows(i["L1_ffn_gate_b"])
    laid["w_route3"], laid["b_route3"] = T(i["L3_ffn_router_w"]), rows(i["L3_ffn_router_b"])
    for n in "01":
        laid["W1_" + n], laid["W2_" + n] = i[f"L{n}_ffn_W1"], i[f"L{n}_ffn_W2"]
        laid["b1_" + n], laid["b2_" + n] = hidden_chunks(i[f"L{n}_ffn_b1"]), rows(i[f"L{n}_ffn_b2"])
    laid["W_3"], laid["V_3"], laid["Wout_3"] = i["L3_ffn_W"], i["L3_ffn_V"], i["L3_ffn_W_out"]
    laid["affine1"] = cat(rows(i["L1_ffn_ln_gamma"]), rows(i["L1_ffn_ln_beta"]))
    wq = i["L0_xattn_q_w"].transpose(1, 0, 2)
    wk, wv = i["L0_xattn_kv_w"][0, 0], i["L0_xattn_kv_w"][1, 0]
    swap = lambda w: np.concatenate([w[..., 32:], w[..., :32]], axis=-1)
    laid["w_att0"] = np.stack([wq.reshape(D, D), swap(wq).reshape(D, D), i["L0_xattn_out_w"].reshape(D, D)])
    laid["wk_att0"] = np.stack([cat(wk, wk), cat(swap(wk), swap(wk))])
    laid["wv_att0"] = wv
    laid["gain_att0"] = chunks(i["L0_xattn_rms_scale"])
    laid["kept"] = i["mask_BxS2_bk0"].reshape(1, -1)
    gates = np.zeros((3, D, GATE_COLS), np.float32)
    gates[:, :, 0:4] = i["L2_xattn_ig_kernel"].reshape(3, D, 4)
    gates[:, :, FORGET:FORGET + 4] = i["L2_xattn_fg_kernel"].reshape(3, D, 4)
    laid["gates_2"], laid["gate_bias_2"] = gates, np.zeros((P, 1), np.float32)
    laid["gate_bias_2"][0:4, 0], laid["gate_bias_2"][FORGET:FORGET + 4, 0] = i["L2_xattn_ig_bias"], i["L2_xattn_fg_bias"]
    laid["out_gain_2"] = rows(i["L2_xattn_outnorm_weight"])
    laid["w_mix"] = np.stack([T(i["L2_ffn_W_" + m]) for m in "rkv"])
    laid["mu_mix"] = cat(chunks(i["L2_ffn_mu_r"]), chunks(i["L2_ffn_mu_k"]))
    nc = bacc.Bacc("TRN2", target_bir_lowering=False, num_devices=1)
    aps = {}
    for name, value in laid.items():
        laid[name] = np.ascontiguousarray(value)
        aps[name] = nc.dram_tensor("in_" + name, value.shape, mybir.dt.from_np(value.dtype), kind="ExternalInput").ap()
    out = nc.dram_tensor("out", (B, S, D), F32, kind="ExternalOutput").ap()
    build(nc, aps, out)
    r = run_bass_kernel_spmd(nc, [{"in_" + name: value for name, value in laid.items()}], core_ids=[0])
    return r.results[0]["out"]
```
